# Optimizing a Trainium2 kernel written in Bass

```python
import numpy as np
import jax
import jax.numpy as jnp

def _softmax(x, axis=-1):
    return jax.nn.softmax(x, axis=axis)

def _gelu(x):
    return jax.nn.gelu(x, approximate=True)

def _silu(x):
    return jax.nn.silu(x)

def _sigmoid(x):
    return jax.nn.sigmoid(x)

def _layernorm(x, axis=-1, eps=1e-05):
    m = jnp.mean(x, axis=axis, keepdims=True)
    v = jnp.var(x, axis=axis, keepdims=True)
    return (x - m) / jnp.sqrt(v + eps)

def _scatter_add(tgt, idx, src, axis=0):
    return tgt.at[idx].add(src)

def _segment_sum(src, seg, n):
    return jax.ops.segment_sum(src, seg, n)
kernel_name = 'mk_gnn_preln_d4_gnn_r32_41ba97'

def setup_inputs(seed: int=0):
    np.random.seed(seed)
    _w = jnp.asarray

    def _rec_inputs():
        import jax
        import jax.numpy as jnp
        _gk = jax.random.key(seed)
        x = -0.000202 + 1 * jax.random.normal(jax.random.fold_in(_gk, 1), (3125, 128), jnp.float32)
        _s = jax.random.randint(jax.random.fold_in(_gk, 2), (50000,), 0, 3125, jnp.int32)
        _d = jax.random.randint(jax.random.fold_in(_gk, 3), (50000,), 0, 3125, jnp.int32)
        _loop = jnp.arange(3125, dtype=jnp.int32)
        src = jnp.concatenate([_s, _d, _loop])
        dst = jnp.concatenate([_d, _s, _loop])
        _o = jnp.argsort(dst, stable=True)
        src = src[_o]
        dst = dst[_o]
        edge_attr_64 = 0.000189758 + 1.00013 * jax.random.normal(jax.random.fold_in(_gk, 12), (103125, 64), jnp.float32)
        edge_type_100 = jax.random.randint(jax.random.fold_in(_gk, 14), (103125,), 0, 100, jnp.int32)
        return (x, src, dst, edge_attr_64, edge_type_100)
    x, src, dst, edge_attr_64, edge_type_100 = _rec_inputs()

    def _L0_gnn_setup():
        import jax, jax.numpy as jnp
        import numpy as np
        N = 50000
        E = 25000
        NODE_DIM = 128
        EDGE_DIM = 64

        def leaky_relu(x, slope=0.2):
            return jnp.where(x >= 0, x, slope * x)
        key = jax.random.key(seed)
        ks = jax.random.split(key, 12)
        node_feats = jax.random.normal(ks[0], (N, NODE_DIM), dtype=jnp.float32)
        edge_index = jax.random.randint(ks[1], (2, E), 0, N, dtype=jnp.int64)
        edge_feats = jax.random.normal(ks[2], (E, EDGE_DIM), dtype=jnp.float32)
        s1 = 1.0 / np.sqrt(NODE_DIM + EDGE_DIM)
        s2 = 1.0 / np.sqrt(NODE_DIM)
        s3 = 1.0 / np.sqrt(2 * NODE_DIM)
        msg_w1 = jax.random.uniform(ks[3], (NODE_DIM + EDGE_DIM, NODE_DIM), jnp.float32, -s1, s1)
        msg_b1 = jax.random.uniform(ks[4], (NODE_DIM,), jnp.float32, -s1, s1)
        msg_w2 = jax.random.uniform(ks[5], (NODE_DIM, NODE_DIM), jnp.float32, -s2, s2)
        msg_b2 = jax.random.uniform(ks[6], (NODE_DIM,), jnp.float32, -s2, s2)
        upd_w1 = jax.random.uniform(ks[7], (2 * NODE_DIM, NODE_DIM), jnp.float32, -s3, s3)
        upd_b1 = jax.random.uniform(ks[8], (NODE_DIM,), jnp.float32, -s3, s3)
        upd_w2 = jax.random.uniform(ks[9], (NODE_DIM, NODE_DIM), jnp.float32, -s2, s2)
        upd_b2 = jax.random.uniform(ks[10], (NODE_DIM,), jnp.float32, -s2, s2)
        return {'node_feats': node_feats, 'edge_feats': edge_feats, 'msg_w1': msg_w1, 'msg_b1': msg_b1, 'msg_w2': msg_w2, 'msg_b2': msg_b2, 'upd_w1': upd_w1, 'upd_b1': upd_b1, 'upd_w2': upd_w2, 'upd_b2': upd_b2, 'edge_index': edge_index}
    _L0_gnn_all = _L0_gnn_setup()
    _L0_gnn_in = {k: v for k, v in _L0_gnn_all.items() if k in ('msg_w1', 'msg_b1', 'msg_w2', 'msg_b2', 'upd_w1', 'upd_b1', 'upd_w2', 'upd_b2')}
    del _L0_gnn_all

    def _L1_gnn_setup():
        import jax, jax.numpy as jnp
        import numpy as np
        N_NODES = 50000
        N_EDGES = 25000
        D_IN = 128
        D_OUT = 128
        NUM_RELS = 100
        key = jax.random.key(seed)
        k1, k2, k3, k4, k5, k6, k7 = jax.random.split(key, 7)
        h = jax.random.normal(k1, (N_NODES, D_IN), dtype=jnp.float32)
        W = jax.random.normal(k2, (D_IN, D_OUT), dtype=jnp.float32) * 0.05
        attn = jax.random.normal(k3, (2 * D_OUT,), dtype=jnp.float32) * 0.05
        rel_emb = jax.random.normal(k4, (NUM_RELS, 1), dtype=jnp.float32)
        src = jax.random.randint(k5, (N_EDGES,), 0, N_NODES, dtype=jnp.int32)
        dst = jax.random.randint(k6, (N_EDGES,), 0, N_NODES, dtype=jnp.int32)
        etype = jax.random.randint(k7, (N_EDGES,), 0, NUM_RELS, dtype=jnp.int32)
        return {'h': h, 'W': W, 'attn': attn, 'rel_emb': rel_emb, 'src': src, 'dst': dst, 'etype': etype}
    _L1_gnn_all = _L1_gnn_setup()
    _L1_gnn_in = {k: v for k, v in _L1_gnn_all.items() if k in ('W', 'attn', 'rel_emb')}
    del _L1_gnn_all

    def _L2_gnn_setup():
        import jax, jax.numpy as jnp
        import numpy as np
        N_NODES = 3125
        IN_CH = 128
        HID_CH = 128
        N_EDGES = 50000

        def gcn_conv(x, edge_index, W, b):
            n = x.shape[0]
            loops = jnp.arange(n, dtype=edge_index.dtype)
            row = jnp.concatenate([edge_index[0], loops])
            col = jnp.concatenate([edge_index[1], loops])
            deg = jax.ops.segment_sum(jnp.ones_like(col, dtype=x.dtype), col, num_segments=n)
            dinv = jnp.where(deg > 0, jax.lax.rsqrt(deg), 0.0)
            norm = dinv[row] * dinv[col]
            h = x @ W
            msg = h[row] * norm[:, None]
            out = jax.ops.segment_sum(msg, col, num_segments=n)
            return out + b

        def mish(x):
            return x * jnp.tanh(jax.nn.softplus(x))
        key = jax.random.key(seed)
        k1, k2, k3, k4 = jax.random.split(key, 4)
        x = jax.random.normal(k1, (N_NODES, IN_CH), dtype=jnp.float32)
        edge_index = jax.random.randint(k2, (2, N_EDGES), 0, N_NODES, dtype=jnp.int64)
        limit = float(np.sqrt(6.0 / (IN_CH + HID_CH)))
        W = jax.random.uniform(k3, (IN_CH, HID_CH), minval=-limit, maxval=limit, dtype=jnp.float32)
        b = jnp.zeros((HID_CH,), dtype=jnp.float32)
        return {'x': x, 'edge_index': edge_index, 'W': W, 'b': b}
    _L2_gnn_all = _L2_gnn_setup()
    _L2_gnn_in = {k: v for k, v in _L2_gnn_all.items() if k in ('W', 'b')}
    del _L2_gnn_all

    def _L3_gnn_setup():
        import jax, jax.numpy as jnp
        import numpy as np
        N, E, D = (3125, 50000, 128)
        key = jax.random.key(seed)
        k_x, k_e, k_ws, k_bs, k_wn, k_bn = jax.random.split(key, 6)
        x = jax.random.normal(k_x, (N, D), dtype=jnp.float32)
        edge_index = jax.random.randint(k_e, (2, E), 0, N, dtype=jnp.int64)
        scale = 1.0 / np.sqrt(D)
        W_self = jax.random.normal(k_ws, (D, D), dtype=jnp.float32) * scale
        b_self = jax.random.normal(k_bs, (D,), dtype=jnp.float32) * scale
        W_neigh = jax.random.normal(k_wn, (D, D), dtype=jnp.float32) * scale
        b_neigh = jax.random.normal(k_bn, (D,), dtype=jnp.float32) * scale
        return {'x': x, 'edge_index': edge_index, 'W_self': W_self, 'b_self': b_self, 'W_neigh': W_neigh, 'b_neigh': b_neigh}
    _L3_gnn_all = _L3_gnn_setup()
    _L3_gnn_in = {k: v for k, v in _L3_gnn_all.items() if k in ('W_self', 'b_self', 'W_neigh', 'b_neigh')}
    del _L3_gnn_all
    return {'x': x, 'src': src, 'dst': dst, 'edge_attr_64': edge_attr_64, 'edge_type_100': edge_type_100, 'L0_gnn_msg_w1': _L0_gnn_in['msg_w1'], 'L0_gnn_msg_b1': _L0_gnn_in['msg_b1'], 'L0_gnn_msg_w2': _L0_gnn_in['msg_w2'], 'L0_gnn_msg_b2': _L0_gnn_in['msg_b2'], 'L0_gnn_upd_w1': _L0_gnn_in['upd_w1'], 'L0_gnn_upd_b1': _L0_gnn_in['upd_b1'], 'L0_gnn_upd_w2': _L0_gnn_in['upd_w2'], 'L0_gnn_upd_b2': _L0_gnn_in['upd_b2'], 'L1_gnn_W': _L1_gnn_in['W'], 'L1_gnn_attn': _L1_gnn_in['attn'], 'L1_gnn_rel_emb': _L1_gnn_in['rel_emb'], 'L2_gnn_W': _L2_gnn_in['W'], 'L2_gnn_b': _L2_gnn_in['b'], 'L3_gnn_W_self': _L3_gnn_in['W_self'], 'L3_gnn_b_self': _L3_gnn_in['b_self'], 'L3_gnn_W_neigh': _L3_gnn_in['W_neigh'], 'L3_gnn_b_neigh': _L3_gnn_in['b_neigh']}

def reference(x, src, dst, edge_attr_64, edge_type_100, L0_gnn_msg_w1, L0_gnn_msg_b1, L0_gnn_msg_w2, L0_gnn_msg_b2, L0_gnn_upd_w1, L0_gnn_upd_b1, L0_gnn_upd_w2, L0_gnn_upd_b2, L1_gnn_W, L1_gnn_attn, L1_gnn_rel_emb, L2_gnn_W, L2_gnn_b, L3_gnn_W_self, L3_gnn_b_self, L3_gnn_W_neigh, L3_gnn_b_neigh):
    import jax
    import jax.numpy as jnp

    def _L0_gnn_ref(node_feats, edge_feats, msg_w1, msg_b1, msg_w2, msg_b2, upd_w1, upd_b1, upd_w2, upd_b2, edge_index):
        import jax, jax.numpy as jnp
        import numpy as np
        N = 50000
        E = 25000
        NODE_DIM = 128
        EDGE_DIM = 64

        def leaky_relu(x, slope=0.2):
            return jnp.where(x >= 0, x, slope * x)
        src = edge_index[0]
        dst = edge_index[1]
        msg_input = jnp.concatenate([node_feats[dst], edge_feats], axis=1)
        h = leaky_relu(msg_input @ msg_w1 + msg_b1)
        messages = h @ msg_w2 + msg_b2
        aggregated = jax.ops.segment_sum(messages, src, num_segments=node_feats.shape[0])
        update_input = jnp.concatenate([node_feats, aggregated], axis=1)
        h2 = leaky_relu(update_input @ upd_w1 + upd_b1)
        return h2 @ upd_w2 + upd_b2

    def _L1_gnn_ref(h, W, attn, rel_emb, src, dst, etype):
        import jax, jax.numpy as jnp
        import numpy as np
        N_NODES = 50000
        N_EDGES = 25000
        D_IN = 128
        D_OUT = 128
        NUM_RELS = 100
        N = h.shape[0]
        d = W.shape[1]
        rel_table = rel_emb.at[0].set(0.0)
        z = h @ W
        s_src = z @ attn[:d]
        s_dst = z @ attn[d:]
        e = jax.nn.leaky_relu(s_src[src] + s_dst[dst])
        m = jax.ops.segment_max(e, dst, num_segments=N)
        ex = jnp.exp(e - m[dst])
        denom = jax.ops.segment_sum(ex, dst, num_segments=N)
        alpha = ex / denom[dst]
        coef = rel_table[etype, 0] * alpha
        out = jax.ops.segment_sum(coef[:, None] * z[src], dst, num_segments=N)
        return out

    def _L2_gnn_ref(x, edge_index, W, b):
        import jax, jax.numpy as jnp
        import numpy as np
        N_NODES = 3125
        IN_CH = 128
        HID_CH = 128
        N_EDGES = 50000

        def gcn_conv(x, edge_index, W, b):
            n = x.shape[0]
            loops = jnp.arange(n, dtype=edge_index.dtype)
            row = jnp.concatenate([edge_index[0], loops])
            col = jnp.concatenate([edge_index[1], loops])
            deg = jax.ops.segment_sum(jnp.ones_like(col, dtype=x.dtype), col, num_segments=n)
            dinv = jnp.where(deg > 0, jax.lax.rsqrt(deg), 0.0)
            norm = dinv[row] * dinv[col]
            h = x @ W
            msg = h[row] * norm[:, None]
            out = jax.ops.segment_sum(msg, col, num_segments=n)
            return out + b

        def mish(x):
            return x * jnp.tanh(jax.nn.softplus(x))
        return mish(gcn_conv(x, edge_index, W, b))

    def _L3_gnn_ref(x, edge_index, W_self, b_self, W_neigh, b_neigh):
        import jax, jax.numpy as jnp
        import numpy as np
        N, E, D = (3125, 50000, 128)
        src, dst = (edge_index[0], edge_index[1])
        n = x.shape[0]
        agg = jax.ops.segment_sum(x[src], dst, num_segments=n)
        deg = jax.ops.segment_sum(jnp.ones((src.shape[0],), x.dtype), dst, num_segments=n)
        agg = agg / jnp.maximum(deg, 1.0)[:, None]
        h = x @ W_self.T + b_self + agg @ W_neigh.T + b_neigh
        return jax.nn.relu(h)
    edge_index = jnp.stack([src, dst])
    h = jnp.maximum(_layernorm(x, axis=-1), 0.0)
    x = x + _L0_gnn_ref(h, edge_attr_64, L0_gnn_msg_w1, L0_gnn_msg_b1, L0_gnn_msg_w2, L0_gnn_msg_b2, L0_gnn_upd_w1, L0_gnn_upd_b1, L0_gnn_upd_w2, L0_gnn_upd_b2, edge_index)
    h = jnp.maximum(_layernorm(x, axis=-1), 0.0)
    x = x + _L1_gnn_ref(h, L1_gnn_W, L1_gnn_attn, L1_gnn_rel_emb, src, dst, edge_type_100)
    h = jnp.maximum(_layernorm(x, axis=-1), 0.0)
    x = x + _L2_gnn_ref(h, edge_index, L2_gnn_W, L2_gnn_b)
    h = jnp.maximum(_layernorm(x, axis=-1), 0.0)
    x = x + _L3_gnn_ref(h, edge_index, L3_gnn_W_self, L3_gnn_b_self, L3_gnn_W_neigh, L3_gnn_b_neigh)
    return x

_drawn_inputs = setup_inputs


def setup_inputs(seed=0):
    import zlib

    import numpy as np

    out = dict(_drawn_inputs(seed))
    spreads = {'L2_gnn_b': (0.0, 0.1)}
    factors = {'L0_gnn_upd_b1': 3.946, 'L1_gnn_attn': 6.52}
    for name, (base, spread) in spreads.items():
        noise = np.random.default_rng([zlib.crc32(name.encode()), seed]).standard_normal(out[name].shape)
        drawn = base * np.exp(spread * noise) if base else spread * noise
        out[name] = jnp.asarray(drawn.astype(out[name].dtype))
    for name, factor in factors.items():
        out[name] = (out[name] * factor).astype(out[name].dtype)
    return out
```

```python
from contextlib import ExitStack

import concourse.bass as bass
from concourse import mybir

F32 = mybir.dt.float32
F16 = mybir.dt.float16
I32 = mybir.dt.int32
ALU = mybir.AluOpType
ACT = mybir.ActivationFunctionType
AX = mybir.AxisListType
ds = bass.ds

P = 128
D = 128
N = 3125
NT = -(-N // P)
NP = NT * P
NR = N - (NT - 1) * P
ED = 64
E = 103125
EC = -(-E // P)
ER = E - (P - 1) * EC
NREL = 100
BINS = NT * NT
ROW = 68
CH = 13
NCH = EC // CH
assert EC % (2 * CH) == 0
G = 4
STEPS = -(-(EC + BINS) // G)
TT = STEPS * G
TCOL = -(-TT // P)
DUMMY = NT * P * NT
EPS = 1e-5
BANK = 512
CUTS = [(a, min(a + BANK, NP)) for a in range(0, NP, BANK)]
INTERNAL = "Internal"


class Chain:

    def __init__(self, eng, sem):
        self.eng, self.sem, self.count, self.i, self.per = eng, sem, 0, None, 0

    def __call__(self, ins):
        ins.then_inc(self.sem, 1)
        self.count += 1
        self.eng.wait_ge(self.sem, self.count if self.i is None else self.i * self.per + self.count)

    def loop(self, i, first, per):
        self.i, self.per, self.base = i, per, self.count
        self.count -= first * per

    def end(self, total):
        done = self.count
        self.i = None
        self.count = self.base + total * self.per
        return done


def build(nc, x, src, dst, ea, et, w1, b1, w2, b2, u1, c1, u2, c2,
          W1, attn, rel, W2, bb2, Ws, bs, Wn, bn, out):
    sortd = nc.dram_tensor("sorted_rows", [TT * P, ROW], F32, kind=INTERNAL).ap()
    ar = nc.dram_tensor("count_matrices", [(NT + 1) * P * NT, 2 * P], F32, kind=INTERNAL).ap()
    rows1 = nc.dram_tensor("row_a", [2, BINS], F32, kind=INTERNAL).ap()
    rowinc = nc.dram_tensor("row_inc", [BINS], F32, kind=INTERNAL).ap()
    nodes_row = nc.dram_tensor("node_rows", [2, NP], F32, kind=INTERNAL).ap()

    with ExitStack() as top:
        def tsb(name, shape, dt=F32):
            return top.enter_context(nc.sbuf_tensor(name, shape, dt))

        def sem(name):
            return top.enter_context(nc.semaphore(name))

        X = tsb("X", [P, NT, D])
        H = tsb("H", [P, NT, D])
        HT = tsb("HT", [P, NP])
        ident = tsb("ident", [P, P])
        iota128 = tsb("iota128", [P, P])
        stats = tsb("stats", [P, NT, 6])
        mv = tsb("mv", [P, NT, 2])
        rstd = tsb("rstd", [P, NT])
        nbias = tsb("nbias", [P, NT])
        eps = tsb("eps", [P, 1])
        ones = tsb("ones", [P, P])
        DEG = tsb("DEG", [P, NT])
        wl = {}
        for name in ("w1a", "w2", "u1a", "u1b", "u2", "W1", "W2", "WsT", "WnT"):
            wl[name] = tsb("sb_" + name, [P, P])
        w1b = tsb("sb_w1b", [ED, D])
        brow = {}
        for name in ("b1", "b2", "c2", "bs", "bn", "bb2"):
            brow[name] = tsb("row_" + name, [1, D])
        c1col = tsb("c1col", [P, 1])

        mid = ExitStack()

        def msb(name, shape, dt=F32):
            return mid.enter_context(nc.sbuf_tensor(name, shape, dt))

        table = msb("table", [P, 4, TCOL])
        tilei = msb("tilei", [1, 3, TT], I32)
        keep = msb("keep", [P, TT])
        S = msb("S", [P, NT + 1, D + 1])

        def layernorm(tag, weights=None):
            with ExitStack() as ctx:
                tp = ctx.enter_context(nc.psum_tensor("ln_tp" + tag, [P, 2, BANK], F32))
                s_st = sem("ln_stats" + tag)
                s_var = sem("ln_var" + tag)
                s_h = sem("ln_h" + tag)
                s_t = sem("ln_t" + tag)
                s_c = sem("ln_c" + tag)
                s_ch = sem("ln_chain" + tag)
                block = ctx.enter_context(nc.Block())

                @block.vector
                def _(dve):
                    link = Chain(dve, s_ch)
                    for t in range(NT):
                        last = nc.vector.bn_stats(stats[:, t, :], X[:, t, :])
                    link(last)
                    for t in range(NT):
                        last = nc.vector.bn_aggr(mv[:, t, :], stats[:, t, :])
                    last.then_inc(s_st, 1)
                    dve.wait_ge(s_var, 1)
                    link(nc.vector.reciprocal(rstd[:], rstd[:]))
                    nc.vector.scalar_tensor_tensor(nbias[:], mv[:, :, 0], -1.0, rstd[:],
                                                   ALU.mult, ALU.mult).then_inc(s_st, 1)
                    for g in range(0, NT, 4):
                        k = min(4, NT - g)
                        dve.wait_ge(s_t, g // 4 + 1)
                        nc.vector.tensor_copy(HT[:, g * P:(g + k) * P], tp[:, g // 4 % 2, 0:k * P]).then_inc(s_c, 1)

                @block.scalar
                def _(act):
                    act.wait_ge(s_st, 1)
                    nc.scalar.activation(rstd[:], mv[:, :, 1], ACT.Sqrt, bias=eps[:, 0:1]).then_inc(s_var, 1)
                    act.wait_ge(s_st, 2)
                    for t in range(NT):
                        nc.scalar.activation(H[:, t, :], X[:, t, :], ACT.Relu, bias=nbias[:, t:t + 1],
                                             scale=rstd[:, t:t + 1]).then_inc(s_h, 1)

                @block.tensor
                def _(pe):
                    for t in range(NT):
                        pe.wait_ge(s_h, t + 1)
                        if t % 4 == 0 and t >= 8:
                            pe.wait_ge(s_c, t // 4 - 1)
                        last = nc.tensor.transpose(tp[:, t // 4 % 2, (t % 4) * P:(t % 4 + 1) * P], H[:, t, :], ident[:])
                        if t % 4 == 3 or t == NT - 1:
                            last.then_inc(s_t, 1)

        def evacuate(tag, num, AGT):
            with nc.Block() as block:
                @block.vector
                def _(dve):
                    for c, (a, b) in enumerate(CUTS[0::2]):
                        nc.vector.tensor_copy(AGT[:, a:b], num[:, 2 * c, 0:b - a])

                @block.scalar
                def _(act):
                    for c, (a, b) in enumerate(CUTS[1::2]):
                        nc.scalar.activation(AGT[:, a:b], num[:, 2 * c + 1, 0:b - a], ACT.Copy)

        with ExitStack() as ctx:
            wraw = [ctx.enter_context(nc.sbuf_tensor("wraw%d" % k, [P, P], F32)) for k in range(2)]
            tp = ctx.enter_context(nc.psum_tensor("ld_tp", [P, 2, BANK], F32))
            s_ld = sem("loads")
            s_ms = sem("memsets")
            s_x = sem("x_padding")
            s_id = sem("identity")
            s_t = sem("w_transposed")
            block = ctx.enter_context(nc.Block())

            @block.sync
            def _(sp):
                sp.wait_ge(s_x, 1)
                sp.dma_start(X[:, 0:NT - 1, :], x[0:(NT - 1) * P, :].rearrange("(t p) d -> p t d", p=P)).then_inc(s_ld, 16)
                sp.dma_start(X[0:NR, NT - 1, :], x[(NT - 1) * P:N, :]).then_inc(s_ld, 16)
                for to, fr in ((wl["w1a"], w1[0:P, :]), (wl["w2"], w2), (wl["u1a"], u1[0:P, :]),
                               (wl["u1b"], u1[P:2 * P, :]), (wl["u2"], u2), (wl["W1"], W1), (wl["W2"], W2),
                               (wraw[0], Ws), (wraw[1], Wn), (w1b, w1[P:P + ED, :])):
                    sp.dma_start(to[:], fr).then_inc(s_ld, 16)
                for name, fr in (("b1", b1), ("b2", b2), ("c2", c2), ("bs", bs), ("bn", bn), ("bb2", bb2)):
                    sp.dma_start(brow[name][:], fr.rearrange("(a d) -> a d", a=1)).then_inc(s_ld, 16)
                sp.dma_start(c1col[:], c1.rearrange("(d a) -> d a", a=1)).then_inc(s_ld, 16)
                sp.wait_ge(s_ld, 16 * 19)

            @block.gpsimd
            def _(pool):
                nc.gpsimd.iota(iota128[:], pattern=[[1, P]], base=0, channel_multiplier=0,
                               allow_small_or_imprecise_dtypes=True)
                nc.gpsimd.memset(ident[:], 0.0).then_inc(s_ms, 1)
                pool.wait_ge(s_ms, 1)
                nc.gpsimd.affine_select(out=ident[:], in_=ident[:], compare_op=ALU.not_equal, fill=1.0, base=0,
                                        pattern=[[-1, P]], channel_multiplier=1).then_inc(s_id, 1)

            @block.vector
            def _(dve):
                nc.vector.memset(X[:], 0.0).then_inc(s_x, 1)
                nc.vector.memset(eps[:], EPS)
                nc.vector.memset(ones[:], 1.0)
                nc.vector.memset(S[:], 0.0)
                for k, name in enumerate(("WsT", "WnT")):
                    dve.wait_ge(s_t, k + 1)
                    nc.vector.tensor_copy(wl[name][:], tp[:, k, 0:P])

            @block.tensor
            def _(pe):
                pe.wait_ge(s_id, 1)
                pe.wait_ge(s_ld, 16 * 19)
                for k in range(2):
                    nc.tensor.transpose(tp[:, k, 0:P], wraw[k][:], ident[:]).then_inc(s_t, 1)

        layernorm("0")

        with ExitStack() as srt:
            def sb(name, shape, dt=F32):
                return srt.enter_context(nc.sbuf_tensor(name, shape, dt))

            raw = sb("raw", [P, 3, EC], I32)
            hi = sb("hi", [P, 2, EC], I32)
            lo = sb("lo", [P, 3, EC])
            tile = sb("tile", [P, 2, EC])
            binf = sb("binf", [P, EC])
            iota25 = sb("iota25", [P, NT])
            iota625 = sb("iota625", [P, BINS], F16)
            tri = sb("tri", [P, P], F16)
            ntri = sb("ntri", [P, P], F16)
            relt = sb("relt", [P, NREL])
            iotar = sb("iotar", [P, NREL])
            starts = sb("starts", [1, 2, BINS])
            incb = sb("incb", [P, BINS])

            with ExitStack() as ctx:
                SUB = 62
                ohd = ctx.enter_context(nc.sbuf_tensor("ohd", [P, 2, SUB, NT], F16))
                ohs = ctx.enter_context(nc.sbuf_tensor("ohs", [P, 2, SUB, NT], F16))
                hist = ctx.enter_context(nc.psum_tensor("hist", [NT, 2, BANK], F32))
                zrow = ctx.enter_context(nc.sbuf_tensor("zrow", [P, G * 2, ROW], F32))
                triF = ctx.enter_context(nc.sbuf_tensor("triF", [P, P], F32))
                cnt = ctx.enter_context(nc.sbuf_tensor("cnt", [NT, 8, NT], F32))
                cnti = ctx.enter_context(nc.sbuf_tensor("cnti", [NT, 2, NT], I32))
                pre = ctx.enter_context(nc.psum_tensor("pre", [NT, BANK], F32))
                dcol = ctx.enter_context(nc.sbuf_tensor("dcol", [P, 1], I32))
                dcolf = ctx.enter_context(nc.sbuf_tensor("dcolf", [P, 1], F32))
                kidx = ctx.enter_context(nc.sbuf_tensor("kidx", [P, 3, TCOL], F32))
                junk = ctx.enter_context(nc.sbuf_tensor("junk", [P, BINS], F32))
                edges = ctx.enter_context(nc.sbuf_tensor("edges", [P, NT], F32))
                s_ms = sem("h_memset")
                s_ld = sem("h_load")
                s_ch = sem("h_chain")
                s_oh = sem("h_onehot")
                s_mm = sem("h_counted")
                s_con = sem("h_const")
                s_z = sem("h_zero_row")
                s_zd = sem("h_rows_cleared")
                s_pc = sem("h_pool_chain")
                s_rt = sem("h_row_totals")
                s_pre = sem("h_prefix")
                s_st = sem("h_starts")
                s_bo = sem("h_bounce")
                s_tb = sem("h_tables")
                block = ctx.enter_context(nc.Block())

                @block.sync
                def _(sp):
                    sp.wait_ge(s_ms, 1)
                    for k, a in enumerate((dst, src, et)):
                        sp.dma_start(raw[0:P - 1, k, :], a[0:(P - 1) * EC].rearrange("(p c) -> p c", c=EC)).then_inc(s_ld, 16)
                        sp.dma_start(raw[P - 1:P, k, 0:ER], a[(P - 1) * EC:E].rearrange("(p c) -> p c", p=1)).then_inc(s_ld, 16)
                    sp.dma_start(relt[:], rel.rearrange("r a -> a r").partition_broadcast(P).rearrange("p a r -> p (a r)")).then_inc(s_ld, 16)
                    sp.wait_ge(s_st, 1)
                    sp.dma_start(rows1[0].rearrange("(a b) -> a b", a=NT), cnt[:, 4, :]).then_inc(s_bo, 16)
                    sp.dma_start(rows1[1].rearrange("(a b) -> a b", a=NT), cnt[:, 5, :]).then_inc(s_bo, 16)
                    sp.dma_start(rowinc.rearrange("(a b) -> a b", a=NT), cnt[:, 6, :]).then_inc(s_bo, 16)
                    sp.wait_ge(s_bo, 48)
                    sp.dma_start(starts[0:1, :, :].rearrange("a b c -> a (b c)"), rows1.rearrange("a b -> (a b)").unsqueeze(0)).then_inc(s_bo, 16)
                    sp.dma_start(incb[:], rowinc.partition_broadcast(P)).then_inc(s_bo, 16)
                    sp.wait_ge(s_bo, 80)

                @block.scalar
                def _(act):
                    act.wait_ge(s_z, 2)
                    z = G * 2
                    sv = sortd.rearrange("(n p k) w -> n p (k w)", p=P, k=z)
                    with act.Fori(0, TT // z) as n:
                        act.dma_start(sv[ds(n, 1)].squeeze(0), zrow[:].rearrange("p k w -> p (k w)")).then_inc(s_zd, 16)
                    act.wait_ge(s_zd, 16 * (TT // z))

                @block.gpsimd
                def _(pool):
                    nc.gpsimd.memset(zrow[:], 0.0).then_inc(s_z, 1)
                    pool.wait_ge(s_z, 1)
                    nc.gpsimd.memset(zrow[:, :, ED:ED + 2], -1.0).then_inc(s_z, 1)
                    nc.gpsimd.iota(iota25[:], pattern=[[1, NT]], base=0, channel_multiplier=0,
                                   allow_small_or_imprecise_dtypes=True).then_inc(s_con, 1)
                    nc.gpsimd.iota(iota625[:], pattern=[[1, BINS]], base=0, channel_multiplier=0,
                                   allow_small_or_imprecise_dtypes=True).then_inc(s_con, 1)
                    nc.gpsimd.iota(iotar[:], pattern=[[1, NREL]], base=0, channel_multiplier=0,
                                   allow_small_or_imprecise_dtypes=True).then_inc(s_con, 1)
                    nc.gpsimd.iota(edges[:], pattern=[[NT, NT]], base=NT, channel_multiplier=0,
                                   allow_small_or_imprecise_dtypes=True).then_inc(s_con, 1)
                    for k in range(3):
                        nc.gpsimd.iota(kidx[:, k, :], pattern=[[P, TCOL]], base=k - 1, channel_multiplier=1,
                                       allow_small_or_imprecise_dtypes=True).then_inc(s_con, 1)
                    nc.gpsimd.iota(dcol[:], pattern=[[0, 1]], base=0, channel_multiplier=1).then_inc(s_con, 1)
                    nc.gpsimd.memset(triF[:], 1.0).then_inc(s_pc, 1)
                    pool.wait_ge(s_pc, 1)
                    nc.gpsimd.affine_select(out=triF[:], in_=triF[:], compare_op=ALU.is_gt, fill=0.0, base=0,
                                            pattern=[[1, P]], channel_multiplier=-1).then_inc(s_pc, 1)
                    pool.wait_ge(s_pc, 2)
                    nc.gpsimd.tensor_copy(tri[:], triF[:]).then_inc(s_con, 1)
                    nc.gpsimd.tensor_scalar(ntri[:], triF[:], -1.0, 1.0, ALU.mult, ALU.add).then_inc(s_con, 1)

                @block.vector
                def _(dve):
                    link = Chain(dve, s_ch)
                    link(nc.vector.memset(raw[:, 2, :], 0))
                    nc.vector.memset(raw[:, 0:2, :], NP - 1).then_inc(s_ms, 1)
                    dve.wait_ge(s_ld, 16 * 7)
                    nc.vector.tensor_single_scalar(hi[:], raw[:, 0:2, :], 7, ALU.logical_shift_right)
                    nc.vector.memset(relt[:, 0:1], 0.0)
                    link(nc.vector.tensor_copy(lo[:, 2, :], raw[:, 2, :]))
                    link(nc.vector.tensor_single_scalar(raw[:, 0:2, :], raw[:, 0:2, :], P - 1, ALU.bitwise_and))
                    nc.vector.tensor_copy(lo[:, 0:2, :], raw[:, 0:2, :])
                    link(nc.vector.tensor_copy(tile[:], hi[:]))
                    link(nc.vector.scalar_tensor_tensor(binf[:], tile[:, 1, :], float(NT), tile[:, 0, :], ALU.mult, ALU.add))
                    dve.wait_ge(s_con, 10)
                    for n in range(EC // SUB):
                        if n >= 2:
                            dve.wait_ge(s_mm, n - 1)
                        c = slice(n * SUB, (n + 1) * SUB)
                        for k, oh in ((0, ohd), (1, ohs)):
                            ins = nc.vector.tensor_tensor(
                                oh[:, n % 2, :, :], iota25[:].unsqueeze(1).to_broadcast([P, SUB, NT]),
                                tile[:, k, c].unsqueeze(2).to_broadcast([P, SUB, NT]), ALU.is_equal)
                        ins.then_inc(s_oh, 1)
                    dve.wait_ge(s_mm, EC // SUB)
                    link(nc.vector.tensor_copy(cnt[:, 0:2, :], hist[:, :, 0:NT]))
                    link(nc.vector.tensor_tensor(cnt[:, 2, :], cnt[:, 0, :], cnt[:, 1, :], ALU.add))
                    link(nc.vector.tensor_scalar(cnt[:, 2, :], cnt[:, 2, :], float(P - 1), float(P), ALU.add, ALU.max))
                    link(nc.vector.tensor_copy(cnti[:, 0, :], cnt[:, 2, :]))
                    link(nc.vector.tensor_single_scalar(cnti[:, 1, :], cnti[:, 0, :], 7, ALU.logical_shift_right))
                    link(nc.vector.tensor_copy(cnt[:, 2, :], cnti[:, 1, :]))
                    link(nc.vector.tensor_tensor_scan(cnt[:, 3, :], ones[0:NT, 0:NT], cnt[:, 2, :], 0.0, ALU.mult, ALU.add))
                    nc.vector.tensor_copy(cnt[:, 7, 0:1], cnt[:, 3, NT - 1:NT]).then_inc(s_rt, 1)
                    dve.wait_ge(s_pre, 1)
                    link(nc.vector.tensor_copy(cnt[:, 7, 1:2], pre[:, 0:1]))
                    link(nc.vector.tensor_scalar(cnt[:, 6, :], cnt[:, 3, :], cnt[:, 7, 1:2], None, ALU.add))
                    link(nc.vector.tensor_tensor(cnt[:, 3, :], cnt[:, 6, :], cnt[:, 2, :], ALU.subtract))
                    link(nc.vector.tensor_scalar(cnt[:, 4, :], cnt[:, 3, :], float(P), None, ALU.mult))
                    nc.vector.tensor_tensor(cnt[:, 5, :], cnt[:, 4, :], cnt[:, 0, :], ALU.add).then_inc(s_st, 1)
                    dve.wait_ge(s_bo, 80)
                    for k in range(3):
                        for j in range(TCOL):
                            link(nc.vector.tensor_scalar(junk[:], incb[:], kidx[:, k, j:j + 1], None, ALU.is_le,
                                                         ALU.add, accum_out=table[:, k, j:j + 1]))
                    link(nc.vector.tensor_tensor(table[:, 0, :], table[:, 0, :], table[:, 1, :], ALU.is_equal))
                    link(nc.vector.tensor_tensor(table[:, 2, :], table[:, 2, :], table[:, 1, :], ALU.is_equal))
                    for j in range(TCOL):
                        link(nc.vector.tensor_scalar(junk[:, 0:NT], edges[:], table[:, 1, j:j + 1], None, ALU.is_le,
                                                     ALU.add, accum_out=table[:, 3, j:j + 1]))
                    link(nc.vector.scalar_tensor_tensor(table[:, 1, :], table[:, 3, :], -float(NT), table[:, 1, :],
                                                        ALU.mult, ALU.add))
                    link(nc.vector.scalar_tensor_tensor(junk[:, 0:TCOL], table[:, 3, :], float(P * NT), table[:, 1, :],
                                                        ALU.mult, ALU.add))
                    link(nc.vector.tensor_single_scalar(dcol[:, 0:1], dcol[:, 0:1], 3, ALU.bitwise_and))
                    link(nc.vector.tensor_scalar(dcolf[:], dcol[:], float(DUMMY), None, ALU.add))
                    link(nc.vector.tensor_scalar(junk[:, TCOL:2 * TCOL], junk[:, 0:TCOL], dcolf[:, 0:1], -1.0,
                                                 ALU.subtract, ALU.mult))
                    link(nc.vector.tensor_tensor(junk[:, TCOL:2 * TCOL], junk[:, TCOL:2 * TCOL], table[:, 2, :], ALU.mult))
                    nc.vector.tensor_tensor(table[:, 2, :], junk[:, 0:TCOL], junk[:, TCOL:2 * TCOL], ALU.add).then_inc(s_tb, 1)

                @block.tensor
                def _(pe):
                    for n in range(EC // SUB):
                        pe.wait_ge(s_oh, n + 1)
                        for c in range(SUB):
                            a = n * SUB + c
                            last = nc.tensor.matmul(hist[:, a % 2, 0:NT], ohs[:, n % 2, c, :], ohd[:, n % 2, c, :],
                                                    start=(a < 2), stop=(a >= EC - 2))
                        last.then_inc(s_mm, 1)
                    pe.wait_ge(s_rt, 1)
                    nc.tensor.matmul(pre[:, 0:1], triF[0:NT, 0:NT], cnt[:, 7, 0:1], start=True, stop=True).then_inc(s_pre, 1)

            with ExitStack() as ctx:
                trow = nc.dram_tensor("tile_rows", [4, TCOL * P], F32, kind=INTERNAL).ap()
                tf = ctx.enter_context(nc.sbuf_tensor("tf", [1, 3, TT], F32))
                tT = ctx.enter_context(nc.sbuf_tensor("tT", [TCOL, 4, P], F32))
                tp = ctx.enter_context(nc.psum_tensor("tb_tp", [TCOL, 4, P], F32))
                s_t = sem("tb_transposed")
                s_c = sem("tb_copied")
                s_b = sem("tb_bounce")
                block = ctx.enter_context(nc.Block())

                @block.tensor
                def _(pe):
                    for k in range(4):
                        last = nc.tensor.transpose(tp[:, k, :], table[:, k, :], ident[:])
                    last.then_inc(s_t, 1)

                @block.vector
                def _(dve):
                    dve.wait_ge(s_t, 1)
                    nc.vector.tensor_copy(tT[:], tp[:]).then_inc(s_c, 1)
                    dve.wait_ge(s_b, 80)
                    nc.vector.tensor_copy(tilei[:], tf[:])

                @block.sync
                def _(sp):
                    sp.wait_ge(s_c, 1)
                    sp.dma_start(trow.rearrange("k (j p) -> j k p", p=P), tT[:]).then_inc(s_b, 16)
                    sp.wait_ge(s_b, 16)
                    sp.dma_start(keep[:], trow[0, 0:TT].partition_broadcast(P)).then_inc(s_b, 16)
                    for k, r in ((0, 1), (1, 3), (2, 2)):
                        sp.dma_start(tf[:, k, :], trow[r:r + 1, 0:TT]).then_inc(s_b, 16)
                    sp.wait_ge(s_b, 80)

            with ExitStack() as ctx:
                rows = ctx.enter_context(nc.sbuf_tensor("rows", [P, 2, CH, ROW], F32))
                binc = ctx.enter_context(nc.sbuf_tensor("binc", [P, 2, CH], F32))
                oh = ctx.enter_context(nc.sbuf_tensor("oh", [P, CH, BINS], F16))
                posf = ctx.enter_context(nc.sbuf_tensor("posf", [P, 2, CH], F32))
                posi = ctx.enter_context(nc.sbuf_tensor("posi", [P, 2, CH], I32))
                junk = ctx.enter_context(nc.sbuf_tensor("junk2", [P, 2, BINS], F32))
                junkr = ctx.enter_context(nc.sbuf_tensor("junkr", [P, CH, NREL], F32))
                run = ctx.enter_context(nc.psum_tensor("run", [P, 2, 2 * BANK], F32))
                s_row = [sem("s_row_a"), sem("s_row_b")]
                s_idx = sem("s_row_indices")
                s_rel = sem("s_row_weight")
                s_bin = sem("s_bins_copied")
                s_oh = sem("s_onehot")
                s_run = sem("s_running")
                s_pos = sem("s_position")
                s_upd = sem("s_run_updated")
                s_int = sem("s_position_int")
                s_sc = [sem("s_scattered_a"), sem("s_scattered_b")]
                s_pad = sem("s_rows_padded")
                s_go = sem("s_pool_passed")
                s_ago = sem("s_act_passed")
                block = ctx.enter_context(nc.Block())

                @block.sync
                def _(sp):
                    sp.wait_ge(s_pad, 1)

                    def load(i, h, first):
                        if not first:
                            sp.wait_ge(s_sc[h], i * (16 * CH))
                        c0 = (i * 2 + h) * CH
                        sp.dma_start(rows[0:P - 1, h, :, 0:ED],
                                     ea[0:(P - 1) * EC, :].rearrange("(p c) d -> p c d", c=EC)[:, ds(c0, CH), :]).then_inc(s_row[h], 16)

                    def load_last(i, h, n):
                        c0 = (P - 1) * EC + (i * 2 + h) * CH
                        sp.dma_start(rows[P - 1:P, h, 0:n, 0:ED],
                                     ea[ds(c0, n), :].unsqueeze(0)).then_inc(s_row[h], 16)

                    full = ER // CH
                    whole = full // 2
                    for h in range(2):
                        load(0, h, True)
                        load_last(0, h, CH)
                    with sp.Fori(1, whole) as i:
                        for h in range(2):
                            load(i, h, False)
                            load_last(i, h, CH)
                    for i in range(whole, NCH // 2):
                        for h in range(2):
                            load(i, h, False)
                            n = min(CH, ER - (i * 2 + h) * CH)
                            if n > 0:
                                load_last(i, h, n)
                            else:
                                load_last(0, h, 1)

                @block.scalar
                def _(act):
                    act.wait_ge(s_pad, 1)

                    def step(i, first):
                        for h in range(2):
                            if not first:
                                act.wait_ge(s_sc[h], i * (16 * CH))
                            c0 = (i * 2 + h) * CH
                            act.sem_inc(s_ago, 1)
                            nc.scalar.activation(rows[:, h, :, ED:ED + 2].rearrange("p c k -> p k c"),
                                                 lo[:, 0:2, ds(c0, CH)], ACT.Copy).then_inc(s_idx, 1)
                            for c in range(CH):
                                act.wait_ge(s_pos, i * (2 * CH) + h * CH + c + 1)
                                nc.scalar.activation(posi[:, h, c:c + 1], posf[:, h, c:c + 1], ACT.Copy).then_inc(s_int, 1)
                    step(0, True)
                    with act.Fori(1, NCH // 2) as i:
                        step(i, False)

                @block.vector
                def _(dve):
                    nc.vector.memset(rows[:], 0.0).then_inc(s_pad, 1)
                    dve.wait_ge(s_pad, 1)

                    def step(i, first):
                        for h in range(2):
                            c0 = (i * 2 + h) * CH
                            if not first:
                                dve.wait_ge(s_sc[h], i * (16 * CH))
                            nc.vector.tensor_copy(binc[:, h, :], binf[:, ds(c0, CH)]).then_inc(s_bin, 1)
                            nc.vector.tensor_copy(posf[:, h, :], lo[:, 2, ds(c0, CH)]).then_inc(s_bin, 1)
                            dve.wait_ge(s_bin, i * 4 + 2 * h + 2)
                            for c in range(CH):
                                last = nc.vector.scalar_tensor_tensor(
                                    junkr[:, c, :], iotar[:], posf[:, h, c:c + 1], relt[:], ALU.is_equal, ALU.mult,
                                    accum_out=rows[:, h, c, ED + 2:ED + 3])
                            last.then_inc(s_rel, 1)
                            dve.wait_ge(s_rel, i * 2 + h + 1)

                            def onehot(c):
                                k = (h * CH + c)
                                n = i * (2 * CH) + k
                                if not (first and k < CH):
                                    dve.wait_ge(s_upd, n - CH + 1)
                                nc.vector.tensor_scalar(oh[:, c, :], iota625[:], binc[:, h, c:c + 1], None,
                                                        ALU.is_equal).then_inc(s_oh, 1)

                            onehot(0)
                            for c in range(CH):
                                k = h * CH + c
                                if c + 1 < CH:
                                    onehot(c + 1)
                                dve.wait_ge(s_run, i * (2 * CH) + k + 1)
                                nc.vector.tensor_tensor_reduce(
                                    junk[:, k % 2, :], run[:, k % 2, 0:BINS], oh[:, c, :], 1.0, 0.0, ALU.mult, ALU.add,
                                    posf[:, h, c:c + 1]).then_inc(s_pos, 1)
                    step(0, True)
                    with dve.Fori(1, NCH // 2) as i:
                        step(i, False)

                @block.tensor
                def _(pe):
                    parts = ((0, BANK), (BANK, BINS))
                    for k in range(2):
                        for a, b in parts:
                            nc.tensor.matmul(run[:, k, a:b], ones[0:1, :], starts[:, k, a:b], start=True, stop=False,
                                             skip_group_check=True)

                    def step(i):
                        def update(k):
                            pe.wait_ge(s_pos, i * (2 * CH) + k + 1)
                            for a, b in parts:
                                last = nc.tensor.matmul(run[:, k % 2, a:b], ntri[:], oh[:, k % CH, a:b], start=False,
                                                        stop=False, skip_group_check=True)
                            last.then_inc(s_upd, 1)

                        for k in range(2 * CH):
                            pe.wait_ge(s_oh, i * (2 * CH) + k + 1)
                            for a, b in parts:
                                last = nc.tensor.matmul(run[:, k % 2, a:b], tri[:], oh[:, k % CH, a:b], start=False,
                                                        stop=False, skip_group_check=True)
                            last.then_inc(s_run, 1)
                            if k >= 1:
                                update(k - 1)
                        update(2 * CH - 1)
                    step(0)
                    with pe.Fori(1, NCH // 2) as i:
                        step(i)

                @block.gpsimd
                def _(pool):
                    def step(i):
                        for h in range(2):
                            pool.wait_ge(s_row[h], i * 32 + 32)
                            pool.wait_ge(s_idx, i * 2 + h + 1)
                            pool.wait_ge(s_rel, i * 2 + h + 1)
                            for c in range(CH):
                                pool.wait_ge(s_int, i * (2 * CH) + h * CH + c + 1)
                                pool.sem_inc(s_go, 1)
                                pool.indirect_dma_start(
                                    sortd, bass.IndirectOffsetOnAxis(ap=posi[:, h, c:c + 1], axis=0),
                                    rows[:, h, c, :], None).then_inc(s_sc[h], 16)
                    step(0)
                    with pool.Fori(1, NCH // 2) as i:
                        step(i)
                    for h in range(2):
                        pool.wait_ge(s_sc[h], 16 * CH * (NCH // 2))

        with ExitStack() as ctx:
            def sb(name, shape, dt=F32):
                return ctx.enter_context(nc.sbuf_tensor(name, shape, dt))

            NB = 2
            PN = sb("PN", [P, NT + 1, D])
            rt = sb("rt", [P, NB, G, ROW])
            mov = sb("mov", [P, 4, 3 * P + 1])
            ohs = sb("ohs_e", [P, 4, P])
            eT = sb("eT", [ED, 4, P])
            dT = sb("dT", [P, 4, P])
            y02 = sb("y02", [P, 4, P])
            acc = sb("acc", [P, 4, 2 * P])
            pq = ctx.enter_context(nc.psum_tensor("pq", [P, 2, 4, P], F32))
            px = ctx.enter_context(nc.psum_tensor("px", [P, 2, BANK], F32))
            pm = ctx.enter_context(nc.psum_tensor("pm", [P, 2, BANK], F32))
            s_pn = sem("e_pn")
            s_pc = sem("e_pn_copied")
            s_rt = [sem("e_rows_a"), sem("e_rows_b")]
            s_oh = sem("e_onehots")
            s_tp = sem("e_transposed")
            s_tc = sem("e_transposes_copied")
            s_x = sem("e_hidden")
            s_y = sem("e_hidden_02")
            s_g = sem("e_leaky")
            s_m = sem("e_products")
            s_acc = sem("e_accumulated")
            s_w = [sem("e_written%d" % k) for k in range(4)]
            s_one = sem("e_ones")
            s_sa = sem("e_sums")
            block = ctx.enter_context(nc.Block())

            assert STEPS % NB == 0
            LOOPS = STEPS // NB
            K = NB * G
            sv = sortd.rearrange("(n j p) w -> n p j w", p=P, j=G)

            @block.sync
            def _(sp):
                def load(n, b):
                    sp.dma_start(rt[:, b, :, :], sv[ds(n, 1)].squeeze(0)).then_inc(s_rt[b], 16)

                def step(i, last):
                    for k in range(K):
                        n = i * K + k
                        row = nc.sync.value_load(tilei[0:1, 2, ds(n, 1)], min_val=0, max_val=DUMMY + 3)
                        sp.wait_ge(s_acc, n + 1)
                        sp.dma_start(ar[ds(row, P, NT), :], acc[:, k % 4, :]).then_inc(s_w[k % 4], 16)
                        if k % G == G - 1 and not last:
                            load(i * NB + NB + k // G, k // G)

                for b in range(NB):
                    load(b, b)
                with sp.Fori(0, LOOPS - 1) as i:
                    step(i, False)
                step(LOOPS - 1, True)
                for k in range(4):
                    sp.wait_ge(s_w[k], 16 * TT // 4)

            @block.scalar
            def _(act):
                def step(i, first):
                    for k in range(K):
                        n = i * K + k
                        act.wait_ge(s_tp, n + 1)
                        if not (first and k < 4):
                            act.wait_ge(s_x, n - 3)
                        nc.scalar.activation(dT[:, k % 4, :], pq[:, k % 2, 0, :], ACT.Copy)
                        nc.scalar.activation(eT[:, k % 4, :], pq[0:ED, k % 2, 1, :], ACT.Copy).then_inc(s_tc, 1)
                        if first and k == 0:
                            continue
                        half(i, k - 1)

                def half(i, k):
                    n = i * K + k
                    act.wait_ge(s_x, n + 1)
                    nc.scalar.activation(y02[:, k % 4, :], px[:, k % 2, 0:D], ACT.Copy, scale=0.2).then_inc(s_y, 1)

                step(0, True)
                with act.Fori(1, LOOPS) as i:
                    step(i, False)
                half(LOOPS - 1, K - 1)

            @block.tensor
            def _(pe):
                for t in range(NT):
                    if t >= 2:
                        pe.wait_ge(s_pc, t - 1)
                    nc.tensor.matmul(px[:, t % 2, 0:D], HT[:, t * P:(t + 1) * P], wl["w1a"][:], start=True, stop=False)
                    nc.tensor.matmul(px[:, t % 2, 0:D], ones[0:1, :], brow["b1"][:], start=False, stop=True).then_inc(s_pn, 1)
                pe.wait_ge(s_pc, NT + 1)

                def transposes(i, k, first):
                    n = i * K + k
                    pe.wait_ge(s_oh, n + 1)
                    if not (first and k < 2):
                        pe.wait_ge(s_tc, n - 1)
                    nc.tensor.transpose(pq[:, k % 2, 0, :], mov[:, k % 4, D + 1:2 * D + 1], ident[:])
                    nc.tensor.transpose(pq[0:ED, k % 2, 1, :], rt[:, k // G, k % G, 0:ED], ident[:]).then_inc(s_tp, 1)

                def hidden(i, k, dt, first):
                    n = i * K + k
                    pe.wait_ge(s_tc, n + 1)
                    if not (first and k < 2):
                        pe.wait_ge(s_g, n - 1)
                    nc.tensor.matmul(px[:, k % 2, 0:D], eT[:, k % 4, :], w1b[:], start=True, stop=False)
                    nc.tensor.matmul(px[:, k % 2, 0:D], dT[:, k % 4, :], PN[:, ds(dt, 1), :].rearrange("p a d -> p (a d)"),
                                     start=False, stop=True).then_inc(s_x, 1)

                def products(i, k, first):
                    n = i * K + k
                    pe.wait_ge(s_g, n + 1)
                    if not (first and k < 2):
                        pe.wait_ge(s_acc, n - 1)
                    nc.tensor.matmul(pm[:, k % 2, 0:3 * P + 1], ohs[:, k % 4, :], mov[:, k % 4, :], start=True,
                                     stop=True).then_inc(s_m, 1)

                def step(i, first):
                    for k in range(K):
                        transposes(i, k, first)
                        if not (first and k < 1):
                            kk = k - 1
                            dt = nc.tensor.value_load(tilei[0:1, 0, ds(i * K + kk, 1)], min_val=0, max_val=NT)
                            hidden(i, kk, dt, first)
                        if not (first and k < 2):
                            products(i, k - 2, first)

                step(0, True)
                with pe.Fori(1, LOOPS) as i:
                    step(i, False)
                dt = nc.tensor.value_load(tilei[0:1, 0, TT - 1:TT], min_val=0, max_val=NT)
                hidden(LOOPS - 1, K - 1, dt, False)
                products(LOOPS - 1, K - 2, False)
                products(LOOPS - 1, K - 1, False)

            @block.vector
            def _(dve):
                for t in range(NT):
                    dve.wait_ge(s_pn, t + 1)
                    nc.vector.tensor_copy(PN[:, t, :], px[:, t % 2, 0:D]).then_inc(s_pc, 1)
                nc.vector.memset(PN[:, NT, :], 0.0).then_inc(s_pc, 1)
                nc.vector.memset(acc[:], 0.0).then_inc(s_one, 1)
                nc.vector.memset(mov[:], 1.0).then_inc(s_one, 1)
                dve.wait_ge(s_one, 2)

                def onehots(i, k, first):
                    n = i * K + k
                    if k % G == 0:
                        dve.wait_ge(s_rt[k // G], i * 16 + 16)
                    if not (first and k < 4):
                        dve.wait_ge(s_m, n - 3)
                    r = rt[:, k // G, k % G, :]
                    nc.vector.tensor_scalar(ohs[:, k % 4, :], iota128[:], r[:, ED + 1:ED + 2], None, ALU.is_equal)
                    nc.vector.tensor_scalar(mov[:, k % 4, 2 * D + 1:3 * D + 1], iota128[:], r[:, ED:ED + 1],
                                            r[:, ED + 2:ED + 3], ALU.is_equal, ALU.mult)
                    nc.vector.tensor_scalar(mov[:, k % 4, D + 1:2 * D + 1], iota128[:], r[:, ED:ED + 1], None,
                                            ALU.is_equal).then_inc(s_oh, 1)

                def leaky(i, k):
                    n = i * K + k
                    dve.wait_ge(s_y, n + 1)
                    nc.vector.tensor_tensor(mov[:, k % 4, 0:D], px[:, k % 2, 0:D], y02[:, k % 4, :], ALU.max).then_inc(s_g, 1)

                def collect(i, k, st, first):
                    n = i * K + k
                    dve.wait_ge(s_m, n + 1)
                    Sv = S[:, ds(st, 1), :].rearrange("p a d -> p (a d)")
                    if not (first and k < 1):
                        dve.wait_ge(s_sa, n)
                    nc.vector.tensor_tensor(Sv, Sv, pm[:, k % 2, 0:D + 1], ALU.add).then_inc(s_sa, 1)
                    if not (first and k < 4):
                        dve.wait_ge(s_w[k % 4], i * 32 + (k // 4) * 16)
                    if not (first and k < 1):
                        dve.wait_ge(s_acc, n)
                    nc.vector.scalar_tensor_tensor(acc[:, k % 4, :], acc[:, (k - 1) % 4, :], keep_at(i, k),
                                                   pm[:, k % 2, D + 1:3 * D + 1], ALU.mult, ALU.add).then_inc(s_acc, 1)

                def keep_at(i, k):
                    n = i * K + k
                    return keep[:, n:n + 1] if isinstance(n, int) else keep[:, ds(n, 1)]

                def step(i, first):
                    for k in range(K):
                        onehots(i, k, first)
                        if not (first and k < 2):
                            leaky(i, k - 2)
                        if not (first and k < 3):
                            st = nc.vector.value_load(tilei[0:1, 1, ds(i * K + k - 3, 1)], min_val=0, max_val=NT)
                            collect(i, k - 3, st, first)

                step(0, True)
                with dve.Fori(1, LOOPS) as i:
                    step(i, False)
                for k in (K - 2, K - 1):
                    leaky(LOOPS - 1, k)
                for k in (K - 3, K - 2, K - 1):
                    st = nc.vector.value_load(tilei[0:1, 1, TT - K + k:TT - K + k + 1], min_val=0, max_val=NT)
                    collect(LOOPS - 1, k, st, False)


        with ExitStack() as ctx:
            ST = ctx.enter_context(nc.sbuf_tensor("ST", [P, NP], F32))
            OD = ctx.enter_context(nc.sbuf_tensor("OD", [1, NP], F32))
            AG = ctx.enter_context(nc.sbuf_tensor("AG", [P, NP], F32))
            Y2 = ctx.enter_context(nc.sbuf_tensor("Y2", [P, 2, BANK], F32))
            c02 = ctx.enter_context(nc.sbuf_tensor("c02", [P, 1], F32))
            tp = ctx.enter_context(nc.psum_tensor("u_tp", [P, 2, BANK], F32))
            tr = ctx.enter_context(nc.psum_tensor("u_tr", [1, 2, BANK], F32))
            mm = ctx.enter_context(nc.psum_tensor("u_mm", [P, 2, BANK], F32))
            po = ctx.enter_context(nc.psum_tensor("u_po", [P, 2, BANK], F32))
            s_t = sem("u_transposed")
            s_tc = sem("u_transposed_copied")
            s_a = sem("u_aggregate")
            s_ac = sem("u_aggregate_copied")
            s_h = sem("u_hidden")
            s_y = sem("u_hidden_02")
            s_hc = sem("u_hidden_done")
            s_o = sem("u_out")
            s_x = sem("u_x")
            s_c = sem("u_bias_02")
            block = ctx.enter_context(nc.Block())
            NC = len(CUTS)

            @block.tensor
            def _(pe):
                def turn(c):
                    a, b = CUTS[c]
                    if c >= 2:
                        pe.wait_ge(s_tc, c - 1)
                    for t in range(a // P, b // P):
                        o = t * P - a
                        nc.tensor.transpose(tp[:, c % 2, o:o + P], S[:, t, 0:D], ident[:])
                        last = nc.tensor.transpose(tr[:, c % 2, o:o + P], S[:, t, D:D + 1], ident[:])
                    last.then_inc(s_t, 1)

                def aggregate(c):
                    a, b = CUTS[c]
                    pe.wait_ge(s_tc, c + 1)
                    if c >= 1:
                        pe.wait_ge(s_hc, c)
                    nc.tensor.matmul(mm[:, 0, 0:b - a], wl["w2"][:], ST[:, a:b], start=True, stop=False)
                    nc.tensor.matmul(mm[:, 0, 0:b - a], brow["b2"][:], OD[:, a:b], start=False, stop=True).then_inc(s_a, 1)

                def hidden(c):
                    a, b = CUTS[c]
                    nc.tensor.matmul(mm[:, 1, 0:b - a], wl["u1a"][:], HT[:, a:b], start=True, stop=False)
                    pe.wait_ge(s_ac, c + 1)
                    nc.tensor.matmul(mm[:, 1, 0:b - a], wl["u1b"][:], AG[:, a:b], start=False, stop=True).then_inc(s_h, 1)

                def out_tiles(c):
                    a, b = CUTS[c]
                    pe.wait_ge(s_hc, c + 1)
                    for t in range(a // P, b // P):
                        if t >= 2:
                            pe.wait_ge(s_x, t - 1)
                        nc.tensor.matmul(po[:, t % 2, 0:D], ST[:, t * P:(t + 1) * P], wl["u2"][:], start=True, stop=False)
                        nc.tensor.matmul(po[:, t % 2, 0:D], ones[0:1, :], brow["c2"][:], start=False, stop=True).then_inc(s_o, 1)

                turn(0)
                for c in range(NC):
                    if c + 1 < NC:
                        turn(c + 1)
                    aggregate(c)
                    hidden(c)
                    out_tiles(c)

            @block.scalar
            def _(act):
                nc.scalar.activation(c02[:], c1col[:], ACT.Copy, scale=0.2).then_inc(s_c, 1)
                act.wait_ge(s_c, 1)
                for c, (a, b) in enumerate(CUTS):
                    act.wait_ge(s_a, c + 1)
                    nc.scalar.activation(AG[:, a:b], mm[:, 0, 0:b - a], ACT.Copy).then_inc(s_ac, 1)
                    act.wait_ge(s_h, c + 1)
                    nc.scalar.activation(Y2[:, c % 2, 0:b - a], mm[:, 1, 0:b - a], ACT.Identity, scale=0.2,
                                         bias=c02[:, 0:1]).then_inc(s_y, 1)

            @block.vector
            def _(dve):
                def copy(c):
                    a, b = CUTS[c]
                    dve.wait_ge(s_t, c + 1)
                    nc.vector.tensor_copy(ST[:, a:b], tp[:, c % 2, 0:b - a])
                    nc.vector.tensor_copy(OD[:, a:b], tr[:, c % 2, 0:b - a]).then_inc(s_tc, 1)

                copy(0)
                for c, (a, b) in enumerate(CUTS):
                    if c + 1 < NC:
                        copy(c + 1)
                    dve.wait_ge(s_y, c + 1)
                    nc.vector.scalar_tensor_tensor(ST[:, a:b], mm[:, 1, 0:b - a], c1col[:, 0:1], Y2[:, c % 2, 0:b - a],
                                                   ALU.add, ALU.max).then_inc(s_hc, 1)
                    for t in range(a // P, b // P):
                        dve.wait_ge(s_o, t + 1)
                        nc.vector.tensor_tensor(X[:, t, :], X[:, t, :], po[:, t % 2, 0:D], ALU.add).then_inc(s_x, 1)

        mid.close()
        layernorm("1")

        arv = ar.rearrange("(s p q) c -> s p q c", p=P, q=NT)
        HALF = [(0, 12), (12, NT)]

        with ExitStack() as lay:
            ss = lay.enter_context(nc.sbuf_tensor("ss", [P, 3, NT], F32))
            sd = lay.enter_context(nc.sbuf_tensor("sd", [P, NT], F32))
            mn = lay.enter_context(nc.sbuf_tensor("mn", [P, 2], F32))
            MX = lay.enter_context(nc.sbuf_tensor("MX", [P, NP], F32))
            DG = lay.enter_context(nc.sbuf_tensor("DG", [P, NP], F32))
            with ExitStack() as ctx:
                WT = ctx.enter_context(nc.sbuf_tensor("WT", [P, P], F32))
                at = ctx.enter_context(nc.sbuf_tensor("at", [P, 2], F32))
                wa = ctx.enter_context(nc.sbuf_tensor("wa", [P, 2], F32))
                m1 = ctx.enter_context(nc.sbuf_tensor("m1", [P, 1], F32))
                m2 = ctx.enter_context(nc.sbuf_tensor("m2", [1, 1], F32))
                tp = ctx.enter_context(nc.psum_tensor("s_tp", [P, BANK], F32))
                pw = ctx.enter_context(nc.psum_tensor("s_pw", [P, BANK], F32))
                pss = ctx.enter_context(nc.psum_tensor("s_pss", [P, BANK // 2, 2], F32))
                pt = ctx.enter_context(nc.psum_tensor("s_pt", [1, BANK], F32))
                pb = ctx.enter_context(nc.psum_tensor("s_pb", [P, BANK], F32))
                s_ld = sem("a_attn")
                s_pe = sem("a_pe")
                s_dv = sem("a_dve")
                s_ch = sem("a_chain")
                block = ctx.enter_context(nc.Block())

                @block.sync
                def _(sp):
                    with nc.allow_non_contiguous_dma(reason="the attention vector as two columns"):
                        sp.dma_start(at[:], attn.rearrange("(a d) -> d a", a=2)).then_inc(s_ld, 16)
                    sp.wait_ge(s_ld, 16)

                @block.tensor
                def _(pe):
                    nc.tensor.transpose(tp[:, 0:P], wl["W1"][:], ident[:]).then_inc(s_pe, 1)
                    pe.wait_ge(s_ld, 16)
                    pe.wait_ge(s_dv, 1)
                    nc.tensor.matmul(pw[:, 0:2], WT[:], at[:], start=True, stop=True).then_inc(s_pe, 1)
                    pe.wait_ge(s_dv, 2)
                    for t in range(NT):
                        last = nc.tensor.matmul(pss[:, t, :], HT[:, t * P:(t + 1) * P], wa[:], start=True, stop=True)
                    last.then_inc(s_pe, 1)
                    pe.wait_ge(s_dv, 3)
                    nc.tensor.transpose(pt[:, 0:P], m1[:], ident[:]).then_inc(s_pe, 1)
                    pe.wait_ge(s_dv, 4)
                    nc.tensor.matmul(pb[:, 0:1], ones[0:1, :], m2[:], start=True, stop=True).then_inc(s_pe, 1)

                @block.vector
                def _(dve):
                    link = Chain(dve, s_ch)
                    nc.vector.memset(MX[:], 0.0)
                    nc.vector.memset(DG[:], 0.0)
                    dve.wait_ge(s_pe, 1)
                    nc.vector.tensor_copy(WT[:], tp[:, 0:P]).then_inc(s_dv, 1)
                    dve.wait_ge(s_pe, 2)
                    nc.vector.tensor_copy(wa[:], pw[:, 0:2]).then_inc(s_dv, 1)
                    dve.wait_ge(s_pe, 3)
                    nc.vector.tensor_copy(sd[:], pss[:, 0:NT, 1])
                    link(nc.vector.tensor_copy(ss[:, 0, :], pss[:, 0:NT, 0]))
                    nc.vector.tensor_scalar(ss[:, 1, :], ss[:, 0, :], 0.01, None, ALU.mult)
                    nc.vector.tensor_reduce(m1[:], ss[:, 0, :], AX.X, ALU.min).then_inc(s_dv, 1)
                    dve.wait_ge(s_pe, 4)
                    nc.vector.tensor_reduce(m2[:], pt[:, 0:P], AX.X, ALU.min).then_inc(s_dv, 1)
                    dve.wait_ge(s_pe, 5)
                    link(nc.vector.tensor_scalar(mn[:, 0:1], pb[:, 0:1], -1.0, None, ALU.add))
                    nc.vector.tensor_scalar(ss[:, 2, :], ss[:, 0, :], mn[:, 0:1], None, ALU.subtract)

            with ExitStack() as ctx:
                ab = ctx.enter_context(nc.sbuf_tensor("ab", [P, NT, P], F32))
                tm = ctx.enter_context(nc.sbuf_tensor("tm", [P, NT, P], F32))
                MXv = MX[:].rearrange("p (q d) -> p q d", q=NT)
                DGv = DG[:].rearrange("p (q d) -> p q d", q=NT)
                s_ld = [sem("m_load_a"), sem("m_load_b")]
                s_mk = sem("m_masked")
                s_mx = sem("m_max")
                s_dg = sem("m_degree")
                block = ctx.enter_context(nc.Block())

                @block.sync
                def _(sp):
                    def load(s, h):
                        a, b = HALF[h]
                        sp.dma_start(ab[:, a:b, :], arv[ds(s, 1), :, a:b, 0:P].squeeze(0)).then_inc(s_ld[h], 16)
                    load(0, 0)
                    load(0, 1)
                    with sp.Fori(1, NT) as s:
                        for h in range(2):
                            sp.wait_ge(s_mk, s * 2 + h - 1)
                            sp.wait_ge(s_dg, s * 2 + h - 1)
                            load(s, h)

                @block.vector
                def _(dve):
                    def step(s, first):
                        for h, (a, b) in enumerate(HALF):
                            dve.wait_ge(s_ld[h], s * 16 + 16)
                            if not first:
                                dve.wait_ge(s_mx, s * 2 + h - 1)
                            nc.vector.tensor_scalar(tm[:, a:b, :], ab[:, a:b, :], 0.0, ss[:, 2, ds(s, 1)], ALU.is_gt,
                                                    ALU.mult).then_inc(s_mk, 1)
                            dve.wait_ge(s_mk, s * 2 + h + 1)
                            nc.vector.tensor_tensor(MXv[:, a:b, :], MXv[:, a:b, :], tm[:, a:b, :], ALU.max).then_inc(s_mx, 1)
                    step(0, True)
                    with dve.Fori(1, NT) as s:
                        step(s, False)

                @block.gpsimd
                def _(pool):
                    def step(s, first):
                        for h, (a, b) in enumerate(HALF):
                            pool.wait_ge(s_ld[h], s * 16 + 16)
                            if not first:
                                pool.wait_ge(s_dg, s * 2 + h - 1)
                            nc.gpsimd.tensor_tensor(DGv[:, a:b, :], DGv[:, a:b, :], ab[:, a:b, :], ALU.add).then_inc(s_dg, 1)
                    step(0, True)
                    with pool.Fori(1, NT) as s:
                        step(s, False)

            RB = lay.enter_context(nc.sbuf_tensor("RB", [P, 2, NP], F32))
            with ExitStack() as ctx:
                mc = ctx.enter_context(nc.sbuf_tensor("mc", [P, 3, NT], F32))
                dm = ctx.enter_context(nc.sbuf_tensor("dm", [P, 2 * NT], F32))
                dT = ctx.enter_context(nc.sbuf_tensor("dmT", [2 * NT, P], F32))
                tp = ctx.enter_context(nc.psum_tensor("x_tp", [P, 2, BANK], F32))
                pd = ctx.enter_context(nc.psum_tensor("x_pd", [P, BANK], F32))
                pr = ctx.enter_context(nc.psum_tensor("x_pr", [2 * NT, BANK], F32))
                s_t = sem("x_turned")
                s_r = sem("x_reduced")
                s_d = sem("x_degrees")
                s_m = sem("x_rows")
                s_mt = sem("x_rows_turned")
                s_mc = sem("x_rows_copied")
                s_b = sem("x_bounce")
                s_ch = sem("x_chain")
                block = ctx.enter_context(nc.Block())

                @block.tensor
                def _(pe):
                    for t in range(NT):
                        last = nc.tensor.matmul(pd[:, t:t + 1], DG[:, t * P:(t + 1) * P], ones[:, 0:1], start=True, stop=True)
                    last.then_inc(s_d, 1)
                    for c, (a, b) in enumerate(CUTS):
                        if c >= 2:
                            pe.wait_ge(s_r, c - 1)
                        for t in range(a // P, b // P):
                            last = nc.tensor.transpose(tp[:, c % 2, t * P - a:(t + 1) * P - a], MX[:, t * P:(t + 1) * P], ident[:])
                        last.then_inc(s_t, 1)
                    pe.wait_ge(s_m, 1)
                    nc.tensor.transpose(pr[:, 0:P], dm[:], ident[:]).then_inc(s_mt, 1)

                @block.vector
                def _(dve):
                    link = Chain(dve, s_ch)
                    dve.wait_ge(s_d, 1)
                    nc.vector.tensor_copy(DEG[:], pd[:, 0:NT])
                    for c, (a, b) in enumerate(CUTS):
                        dve.wait_ge(s_t, c + 1)
                        last = nc.vector.tensor_reduce(mc[:, 0, a // P:b // P],
                                                       tp[:, c % 2, 0:b - a].rearrange("p (t d) -> p t d", d=P), AX.X, ALU.max)
                        last.then_inc(s_r, 1)
                    dve.wait_ge(s_r, len(CUTS))
                    link(nc.vector.scalar_tensor_tensor(mc[:, 1, :], mc[:, 0, :], mn[:, 0:1], sd[:], ALU.add, ALU.add))
                    link(nc.vector.scalar_tensor_tensor(mc[:, 2, :], mc[:, 1, :], 0.01, mc[:, 1, :], ALU.mult, ALU.max))
                    nc.vector.tensor_tensor(dm[:, 0:NT], sd[:], mc[:, 2, :], ALU.subtract)
                    nc.vector.scalar_tensor_tensor(dm[:, NT:2 * NT], sd[:], 0.01, mc[:, 2, :], ALU.mult,
                                                   ALU.subtract).then_inc(s_m, 1)
                    dve.wait_ge(s_mt, 1)
                    nc.vector.tensor_copy(dT[:], pr[:, 0:P]).then_inc(s_mc, 1)

                @block.sync
                def _(sp):
                    sp.wait_ge(s_mc, 1)
                    sp.dma_start(nodes_row.rearrange("a (t p) -> (a t) p", p=P), dT[:]).then_inc(s_b, 16)
                    sp.wait_ge(s_b, 16)
                    sp.dma_start(RB[:].rearrange("p a n -> p (a n)"),
                                 nodes_row.rearrange("a n -> (a n)").partition_broadcast(P)).then_inc(s_b, 16)
                    sp.wait_ge(s_b, 32)

            with ExitStack() as ctx:
                arb = ctx.enter_context(nc.sbuf_tensor("arb", [P, NT, 2, P], F32))
                ex = ctx.enter_context(nc.sbuf_tensor("ex", [P, 2, 13, P], F32))
                rx = ctx.enter_context(nc.sbuf_tensor("rx", [P, NT, P], F32))
                hw = ctx.enter_context(nc.sbuf_tensor("hw", [P, D], F32))
                tmp2 = ctx.enter_context(nc.sbuf_tensor("tmp2", [P, NT, P], F32))
                num = ctx.enter_context(nc.psum_tensor("num", [P, len(CUTS), BANK], F32))
                RBv = RB[:].rearrange("p a (q d) -> p a q d", q=NT)
                MXv = MX[:].rearrange("p (q d) -> p q d", q=NT)
                s_ld = [sem("w_load_a"), sem("w_load_b")]
                s_e = sem("w_exp")
                s_mx = sem("w_exp_max")
                s_ax = sem("w_edge_weights")
                s_rx = sem("w_relation_weights")
                s_dn = sem("w_denominators")
                s_mm = sem("w_products")
                s_w = sem("w_stationary")
                s_z = sem("w_zero")
                s_ago = sem("w_act_passed")
                blk = ExitStack()
                block = blk.enter_context(nc.Block())
                PIECES = []
                for h, (a, b) in enumerate(HALF):
                    lo_, hi_ = a * P, b * P
                    while lo_ < hi_:
                        e_ = min(hi_, (lo_ // BANK + 1) * BANK)
                        PIECES.append((h, lo_, e_))
                        lo_ = e_

                @block.sync
                def _(sp):
                    def load(s, h):
                        a, b = HALF[h]
                        sp.dma_start(arb[:, a:b, :, :].rearrange("p q a d -> p (q a d)"),
                                     arv[ds(s, 1), :, a:b, :].squeeze(0).rearrange("p q c -> p (q c)")).then_inc(s_ld[h], 16)
                    load(0, 0)
                    load(0, 1)
                    with sp.Fori(1, NT) as s:
                        for h in range(2):
                            sp.wait_ge(s_rx, s * 2 + h - 1)
                            sp.wait_ge(s_dn, s * 2 + h - 1)
                            load(s, h)

                @block.scalar
                def _(act):
                    def step(s, first):
                        for h, (a, b) in enumerate(HALF):
                            if not first:
                                act.wait_ge(s_rx, s * 2 + h - 1)
                                act.wait_ge(s_dn, s * 2 + h - 1)
                            act.sem_inc(s_ago, 1)
                            nc.scalar.activation(ex[:, h, 0:b - a, :], RBv[:, 0, a:b, :], ACT.Exp,
                                                 bias=ss[:, 0, ds(s, 1)]).then_inc(s_e, 1)
                            nc.scalar.activation(tmp2[:, a:b, :], RBv[:, 1, a:b, :], ACT.Exp,
                                                 bias=ss[:, 1, ds(s, 1)]).then_inc(s_e, 1)
                        if not first:
                            act.wait_ge(s_mm, s)
                        act.sem_inc(s_ago, 1)
                        nc.scalar.activation(hw[:], H[:, ds(s, 1), :].squeeze(1), ACT.Copy).then_inc(s_w, 1)
                    step(0, True)
                    with act.Fori(1, NT) as s:
                        step(s, False)

                @block.vector
                def _(dve):
                    nc.vector.memset(MX[:], 0.0).then_inc(s_z, 1)
                    def step(s, first):
                        for h, (a, b) in enumerate(HALF):
                            e = ex[:, h, 0:b - a, :]
                            dve.wait_ge(s_e, s * 4 + 2 * h + 2)
                            nc.vector.tensor_tensor(e, e, tmp2[:, a:b, :], ALU.max).then_inc(s_mx, 1)
                            dve.wait_ge(s_mx, s * 2 + h + 1)
                            dve.wait_ge(s_ld[h], s * 16 + 16)
                            if not first:
                                dve.wait_ge(s_mm, s)
                            nc.vector.scalar_tensor_tensor(tmp2[:, a:b, :], e, 2.0, arb[:, a:b, 0, :], ALU.min,
                                                           ALU.mult).then_inc(s_ax, 1)
                            nc.vector.scalar_tensor_tensor(rx[:, a:b, :], e, 2.0, arb[:, a:b, 1, :], ALU.min,
                                                           ALU.mult).then_inc(s_rx, 1)
                    step(0, True)
                    with dve.Fori(1, NT) as s:
                        step(s, False)

                @block.gpsimd
                def _(pool):
                    pool.wait_ge(s_z, 1)

                    def step(s, first):
                        for h, (a, b) in enumerate(HALF):
                            pool.wait_ge(s_ax, s * 2 + h + 1)
                            if not first:
                                pool.wait_ge(s_dn, s * 2 + h - 1)
                            nc.gpsimd.tensor_tensor(MXv[:, a:b, :], MXv[:, a:b, :], tmp2[:, a:b, :], ALU.add).then_inc(s_dn, 1)
                    step(0, True)
                    with pool.Fori(1, NT) as s:
                        step(s, False)

                @block.tensor
                def _(pe):
                    def step(s, first, final):
                        pe.wait_ge(s_w, s + 1)
                        seen = -1
                        for h, a, b in PIECES:
                            if h != seen:
                                pe.wait_ge(s_rx, s * 2 + h + 1)
                                seen = h
                            c = a // BANK
                            last = nc.tensor.matmul(num[:, c, a - c * BANK:b - c * BANK], hw[:],
                                                    rx[:].rearrange("p q d -> p (q d)")[:, a:b],
                                                    start=first, stop=final, skip_group_check=True)
                        last.then_inc(s_mm, 1)
                    step(0, True, False)
                    with pe.Fori(1, NT - 1) as s:
                        step(s, False, False)
                    step(NT - 1, False, True)

                blk.close()
                evacuate("w", num, DG)

            with ExitStack() as ctx:
                pden = ctx.enter_context(nc.psum_tensor("q_den", [P, BANK], F32))
                po = ctx.enter_context(nc.psum_tensor("q_po", [P, 2, BANK], F32))
                rden = ctx.enter_context(nc.sbuf_tensor("rden", [P, NT], F32))
                s_d = sem("q_denominators")
                s_ch = sem("q_chain")
                s_o = sem("q_out")
                s_x = sem("q_x")
                block = ctx.enter_context(nc.Block())

                @block.tensor
                def _(pe):
                    for t in range(NT):
                        last = nc.tensor.matmul(pden[:, t:t + 1], MX[:, t * P:(t + 1) * P], ones[:, 0:1], start=True, stop=True)
                    last.then_inc(s_d, 1)
                    for t in range(NT):
                        if t >= 2:
                            pe.wait_ge(s_x, t - 1)
                        nc.tensor.matmul(po[:, t % 2, 0:D], DG[:, t * P:(t + 1) * P], wl["W1"][:], start=True, stop=True).then_inc(s_o, 1)

                @block.vector
                def _(dve):
                    link = Chain(dve, s_ch)
                    dve.wait_ge(s_d, 1)
                    link(nc.vector.tensor_scalar(rden[:], pden[:, 0:NT], 1e-30, None, ALU.max))
                    link(nc.vector.reciprocal(rden[:], rden[:]))
                    for t in range(NT):
                        dve.wait_ge(s_o, t + 1)
                        nc.vector.scalar_tensor_tensor(X[:, t, :], po[:, t % 2, 0:D], rden[:, t:t + 1], X[:, t, :],
                                                       ALU.mult, ALU.add).then_inc(s_x, 1)

        layernorm("2")

        def gather_product(tag, scale, AGT):
            with ExitStack() as ctx:
                R = 5
                ab = ctx.enter_context(nc.sbuf_tensor("ab" + tag, [P, R, NT, P], F32))
                hw = ctx.enter_context(nc.sbuf_tensor("hw" + tag, [P, R, D], F32))
                num = ctx.enter_context(nc.psum_tensor("num" + tag, [P, len(CUTS), BANK], F32))
                s_ld = [sem("g_load%d_" % r + tag) for r in range(R)]
                s_w = sem("g_stationary" + tag)
                s_mm = sem("g_products" + tag)
                s_on = sem("g_begun" + tag)
                assert NT % R == 0

                with nc.Block() as block:
                    @block.sync
                    def _(sp):
                        def load(s, r):
                            sp.dma_start(ab[:, r, :, :], arv[ds(s, 1), :, :, 0:P].squeeze(0)).then_inc(s_ld[r], 16)
                        for r in range(R):
                            load(r, r)
                        with sp.Fori(1, NT // R) as i:
                            for r in range(R):
                                sp.wait_ge(s_mm, (i - 1) * R + r + 1)
                                load(i * R + r, r)

                    @block.scalar
                    def _(act):
                        def step(i, first):
                            for r in range(R):
                                if not first:
                                    act.wait_ge(s_mm, (i - 1) * R + r + 1)
                                act.sem_inc(s_on, 1)
                                src = H[:, ds(i * R + r, 1), :].squeeze(1)
                                nc.scalar.activation(hw[:, r, :], src, ACT.Copy,
                                                     scale=1.0 if scale is None else scale[:, ds(i * R + r, 1)]).then_inc(s_w, 1)
                        step(0, True)
                        with act.Fori(1, NT // R) as i:
                            step(i, False)

                    @block.tensor
                    def _(pe):
                        def step(i, first, final):
                            for r in range(R):
                                pe.wait_ge(s_w, i * R + r + 1)
                                pe.wait_ge(s_ld[r], i * 16 + 16)
                                for c, (a, b) in enumerate(CUTS):
                                    last = nc.tensor.matmul(num[:, c, 0:b - a], hw[:, r, :],
                                                            ab[:, r, :, :].rearrange("p q d -> p (q d)")[:, a:b],
                                                            start=first and r == 0, stop=final and r == R - 1,
                                                            skip_group_check=True)
                                last.then_inc(s_mm, 1)
                        step(0, True, False)
                        with pe.Fori(1, NT // R - 1) as i:
                            step(i, False, False)
                        step(NT // R - 1, False, True)
                evacuate(tag, num, AGT)

        with ExitStack() as lay:
            AGT = lay.enter_context(nc.sbuf_tensor("AGT", [P, NP], F32))
            dinv = lay.enter_context(nc.sbuf_tensor("dinv", [P, 3, NT], F32))
            bbc = lay.enter_context(nc.sbuf_tensor("bbc", [P, D], F32))
            with ExitStack() as ctx:
                s_ch = sem("d_chain")
                s_a = sem("d_root")
                s_l = sem("d_bias")
                block = ctx.enter_context(nc.Block())

                @block.vector
                def _(dve):
                    link = Chain(dve, s_ch)
                    link(nc.vector.tensor_scalar(dinv[:, 2, :], DEG[:], 1.0, None, ALU.add))
                    link(nc.vector.reciprocal(dinv[:, 1, :], dinv[:, 2, :]))
                    dve.wait_ge(s_a, 1)
                    nc.vector.reciprocal(dinv[:, 0, :], dinv[:, 2, :])

                @block.scalar
                def _(act):
                    act.wait_ge(s_ch, 2)
                    nc.scalar.activation(dinv[:, 2, :], dinv[:, 2, :], ACT.Sqrt).then_inc(s_a, 1)

                @block.sync
                def _(sp):
                    sp.dma_start(bbc[:], bb2.partition_broadcast(P)).then_inc(s_l, 16)
                    sp.wait_ge(s_l, 16)

            gather_product("2", dinv[:, 0, :], AGT)
            with ExitStack() as ctx:
                Z = ctx.enter_context(nc.sbuf_tensor("Z", [P, NT, D], F32))
                Y = ctx.enter_context(nc.sbuf_tensor("Y", [P, 2, D], F32))
                Q = ctx.enter_context(nc.sbuf_tensor("Q", [P, NT, D], F32))
                pa = ctx.enter_context(nc.psum_tensor("pa2", [P, 2, BANK], F32))
                pb = ctx.enter_context(nc.psum_tensor("pb2", [P, 2, BANK], F32))
                s_p = sem("c_products")
                s_y = sem("c_self")
                s_z = sem("c_sum")
                s_e = sem("c_exp")
                s_zb = sem("c_bias")
                s_zm = sem("c_clamped")
                s_ch = sem("c_chain")
                block = ctx.enter_context(nc.Block())

                @block.tensor
                def _(pe):
                    for t in range(NT):
                        if t >= 2:
                            pe.wait_ge(s_z, t - 1)
                        nc.tensor.matmul(pb[:, t % 2, 0:D], HT[:, t * P:(t + 1) * P], wl["W2"][:], start=True, stop=True)
                        nc.tensor.matmul(pa[:, t % 2, 0:D], AGT[:, t * P:(t + 1) * P], wl["W2"][:], start=True,
                                         stop=True).then_inc(s_p, 1)

                @block.scalar
                def _(act):
                    for t in range(NT):
                        act.wait_ge(s_p, t + 1)
                        if t >= 2:
                            act.wait_ge(s_z, t - 1)
                        nc.scalar.activation(Y[:, t % 2, :], pb[:, t % 2, 0:D], ACT.Copy, scale=dinv[:, 1, t:t + 1]).then_inc(s_y, 1)
                    act.wait_ge(s_zm, 1)
                    nc.scalar.activation(Q[:], Q[:], ACT.Exp).then_inc(s_e, 1)

                @block.vector
                def _(dve):
                    link = Chain(dve, s_ch)
                    for t in range(NT):
                        dve.wait_ge(s_y, t + 1)
                        nc.vector.scalar_tensor_tensor(Z[:, t, :], pa[:, t % 2, 0:D], dinv[:, 0, t:t + 1], Y[:, t % 2, :],
                                                       ALU.mult, ALU.add).then_inc(s_z, 1)
                    dve.wait_ge(s_z, NT)
                    link(nc.vector.tensor_tensor(Z[:], Z[:], bbc[:].unsqueeze(1).to_broadcast([P, NT, D]), ALU.add))
                    nc.vector.tensor_scalar(Q[:], Z[:], 20.0, None, ALU.min).then_inc(s_zm, 1)
                    dve.wait_ge(s_e, 1)
                    link(nc.vector.scalar_tensor_tensor(Q[:], Q[:], 2.0, Q[:], ALU.add, ALU.mult))
                    link(nc.vector.tensor_tensor(Z[:], Z[:], Q[:], ALU.mult))
                    link(nc.vector.tensor_scalar(Q[:], Q[:], 2.0, None, ALU.add))
                    link(nc.vector.reciprocal(Q[:], Q[:]))
                    link(nc.vector.tensor_tensor(Z[:], Z[:], Q[:], ALU.mult))
                    nc.vector.tensor_tensor(X[:], X[:], Z[:], ALU.add)

            layernorm("3")
            gather_product("3", None, AGT)
            with ExitStack() as ctx:
                Y = ctx.enter_context(nc.sbuf_tensor("Y3", [P, 2, D], F32))
                Z = ctx.enter_context(nc.sbuf_tensor("Z3", [P, 2, D], F32))
                rdeg = ctx.enter_context(nc.sbuf_tensor("rdeg", [P, NT], F32))
                pa = ctx.enter_context(nc.psum_tensor("pa3", [P, 2, BANK], F32))
                pb = ctx.enter_context(nc.psum_tensor("pb3", [P, 2, BANK], F32))
                s_ch = sem("f_chain")
                s_r = sem("f_degree")
                s_p = sem("f_products")
                s_y = sem("f_neighbours")
                s_z = sem("f_sum")
                s_x = sem("f_x")
                s_out = sem("f_out")
                block = ctx.enter_context(nc.Block())

                @block.tensor
                def _(pe):
                    for t in range(NT):
                        if t >= 2:
                            pe.wait_ge(s_z, t - 1)
                        nc.tensor.matmul(pb[:, t % 2, 0:D], AGT[:, t * P:(t + 1) * P], wl["WnT"][:], start=True, stop=True)
                        nc.tensor.matmul(pa[:, t % 2, 0:D], HT[:, t * P:(t + 1) * P], wl["WsT"][:], start=True, stop=False)
                        nc.tensor.matmul(pa[:, t % 2, 0:D], ones[0:1, :], brow["bs"][:], start=False, stop=False)
                        nc.tensor.matmul(pa[:, t % 2, 0:D], ones[0:1, :], brow["bn"][:], start=False, stop=True).then_inc(s_p, 1)

                @block.scalar
                def _(act):
                    act.wait_ge(s_r, 1)
                    for t in range(NT):
                        act.wait_ge(s_p, t + 1)
                        if t >= 2:
                            act.wait_ge(s_z, t - 1)
                        nc.scalar.activation(Y[:, t % 2, :], pb[:, t % 2, 0:D], ACT.Copy, scale=rdeg[:, t:t + 1]).then_inc(s_y, 1)

                @block.vector
                def _(dve):
                    link = Chain(dve, s_ch)
                    link(nc.vector.tensor_scalar(rdeg[:], DEG[:], 1.0, None, ALU.max))
                    nc.vector.reciprocal(rdeg[:], rdeg[:]).then_inc(s_r, 1)
                    for t in range(NT):
                        dve.wait_ge(s_y, t + 1)
                        nc.vector.tensor_tensor(Z[:, t % 2, :], pa[:, t % 2, 0:D], Y[:, t % 2, :], ALU.add).then_inc(s_z, 1)
                        dve.wait_ge(s_z, t + 1)
                        nc.vector.scalar_tensor_tensor(X[:, t, :], Z[:, t % 2, :], 0.0, X[:, t, :], ALU.max,
                                                       ALU.add).then_inc(s_x, 1)

                @block.sync
                def _(sp):
                    for a in range(0, NT - 1, 6):
                        b = min(a + 6, NT - 1)
                        sp.wait_ge(s_x, b)
                        sp.dma_start(out[a * P:b * P, :].rearrange("(t p) d -> p t d", p=P), X[:, a:b, :]).then_inc(s_out, 16)
                    sp.wait_ge(s_x, NT)
                    sp.dma_start(out[(NT - 1) * P:N, :], X[0:NR, NT - 1, :]).then_inc(s_out, 16)
                    sp.wait_ge(s_out, 16 * 5)


_INS = ["x", "src", "dst", "edge_attr_64", "edge_type_100", "L0_gnn_msg_w1", "L0_gnn_msg_b1", "L0_gnn_msg_w2",
        "L0_gnn_msg_b2", "L0_gnn_upd_w1", "L0_gnn_upd_b1", "L0_gnn_upd_w2", "L0_gnn_upd_b2", "L1_gnn_W", "L1_gnn_attn",
        "L1_gnn_rel_emb", "L2_gnn_W", "L2_gnn_b", "L3_gnn_W_self", "L3_gnn_b_self", "L3_gnn_W_neigh", "L3_gnn_b_neigh"]


def kernel(**inputs):
    import numpy as _np
    import concourse.bacc as _bacc
    from concourse import mybir as _mybir
    from concourse.bass_utils import run_bass_kernel_spmd as _run

    nc = _bacc.Bacc("TRN2", target_bir_lowering=False, num_devices=1)
    arrays, args = {}, []
    for name in _INS:
        a = _np.ascontiguousarray(inputs[name])
        arrays[f"in_{name}_dram"] = a
        args.append(nc.dram_tensor(f"in_{name}_dram", a.shape, _mybir.dt.from_np(a.dtype), kind="ExternalInput").ap())
    args.append(nc.dram_tensor("out_0_dram", (N, D), _mybir.dt.float32, kind="ExternalOutput").ap())
    build(nc, *args)
    r = _run(nc, [arrays], core_ids=[0])
    return r.results[0]["out_0_dram"]
```

```python
from contextlib import ExitStack

import concourse.bass as bass
from concourse import mybir

F32 = mybir.dt.float32
F16 = mybir.dt.float16
BF16 = mybir.dt.bfloat16
I32 = mybir.dt.int32
ALU = mybir.AluOpType
ACT = mybir.ActivationFunctionType
AX = mybir.AxisListType
ds = bass.ds

P = 128
D = 128
N = 3125
NT = -(-N // P)
NP = NT * P
NR = N - (NT - 1) * P
ED = 64
E = 103125
EC = -(-E // P)
ER = E - (P - 1) * EC
NREL = 100
BINS = NT * NT
ROW = D + 4
CH = 13
NCH = EC // CH
assert EC % (2 * CH) == 0
G = 4
RING = 4
LOOPS = -(-(EC + BINS + NT * (G - 1)) // (G * RING))
TT = LOOPS * RING * G
TCOL = -(-TT // P)
DUMMY = NT * P * NT
EPS = 1e-5
BANK = 512
CUTS = [(a, min(a + BANK, NP)) for a in range(0, NP, BANK)]
INTERNAL = "Internal"


def back(i, k, n):
    return (i + (k - n) // RING if (k - n) // RING else i), (k - n) % RING


def loads(nc, engine, ap, top):
    return nc.values_load_multi_w_load_instructions(
        ap, engines=[engine], min_val=0, max_val=top,
        skip_runtime_bounds_check_because="the table counts bins: its values are in range by construction")[1]


class Chain:

    def __init__(self, eng, sem):
        self.eng, self.sem, self.count, self.i, self.per = eng, sem, 0, None, 0

    def __call__(self, ins):
        ins.then_inc(self.sem, 1)
        self.count += 1
        self.eng.wait_ge(self.sem, self.count if self.i is None else self.i * self.per + self.count)

    def loop(self, i, first, per):
        self.i, self.per, self.base = i, per, self.count
        self.count -= first * per

    def end(self, total):
        done = self.count
        self.i = None
        self.count = self.base + total * self.per
        return done


def build(nc, x, src, dst, ea, et, w1, b1, w2, b2, u1, c1, u2, c2,
          W1, attn, rel, W2, bb2, Ws, bs, Wn, bn, out):
    sortd = nc.dram_tensor("sorted_rows", [TT * P, ROW], F32, kind=INTERNAL).ap()
    ar = nc.dram_tensor("count_matrices", [(NT + 1) * P * NT, 2 * P], F32, kind=INTERNAL).ap()
    rows1 = nc.dram_tensor("row_a", [2, BINS], F32, kind=INTERNAL).ap()
    rowinc = nc.dram_tensor("row_inc", [BINS], F32, kind=INTERNAL).ap()
    nodes_row = nc.dram_tensor("node_rows", [2, NP], F32, kind=INTERNAL).ap()

    with ExitStack() as top:
        def tsb(name, shape, dt=F32):
            return top.enter_context(nc.sbuf_tensor(name, shape, dt))

        def sem(name):
            return top.enter_context(nc.semaphore(name))

        X = tsb("X", [P, NT, D])
        H = tsb("H", [P, NT, D])
        HT = tsb("HT", [P, NP])
        ident = tsb("ident", [P, P])
        iota128 = tsb("iota128", [P, P])
        stats = tsb("stats", [P, NT, 6])
        mv = tsb("mv", [P, NT, 2])
        rstd = tsb("rstd", [P, NT])
        nbias = tsb("nbias", [P, NT])
        eps = tsb("eps", [P, 1])
        ones = tsb("ones", [P, P])
        DEG = tsb("DEG", [P, NT])
        ZR = 8
        zrow = tsb("zrow", [P, ZR, ROW])
        s_zd = sem("rows_cleared")
        wl = {}
        for name in ("w1a", "w2", "u1a", "u1b", "u2", "W1", "W2", "WsT", "WnT"):
            wl[name] = tsb("sb_" + name, [P, P])
        w1b = tsb("sb_w1b", [ED, D])
        brow = {}
        for name in ("b1", "b2", "c2", "bs", "bn", "bb2"):
            brow[name] = tsb("row_" + name, [1, D])
        c1col = tsb("c1col", [P, 1])

        mid = ExitStack()

        def msb(name, shape, dt=F32):
            return mid.enter_context(nc.sbuf_tensor(name, shape, dt))

        table = msb("table", [P, 4, TCOL])
        tilei = msb("tilei", [1, 3, TT], I32)
        keep = msb("keep", [P, TT])
        S = msb("S", [P, NT + 1, D + 1])

        s_ln = {name: sem("ln_" + name) for name in ("stats", "root", "h", "turned", "copied", "chain")}
        NQ = -(-NT // 4)

        def layernorm(r):
            with ExitStack() as ctx:
                tp = ctx.enter_context(nc.psum_tensor("ln_tp%d" % r, [P, 2, BANK], F32))
                block = ctx.enter_context(nc.Block())

                @block.vector
                def _(dve):
                    link = Chain(dve, s_ln["chain"])
                    link.count = 2 * r
                    for t in range(NT):
                        last = nc.vector.bn_stats(stats[:, t, :], X[:, t, :])
                    link(last)
                    for t in range(NT):
                        last = nc.vector.bn_aggr(mv[:, t, :], stats[:, t, :])
                    last.then_inc(s_ln["stats"], 1)
                    dve.wait_ge(s_ln["root"], r + 1)
                    link(nc.vector.reciprocal(rstd[:], rstd[:]))
                    nc.vector.scalar_tensor_tensor(nbias[:], mv[:, :, 0], -1.0, rstd[:],
                                                   ALU.mult, ALU.mult).then_inc(s_ln["stats"], 1)
                    for g in range(NQ):
                        k = min(4, NT - 4 * g)
                        dve.wait_ge(s_ln["turned"], r * NQ + g + 1)
                        nc.vector.tensor_copy(HT[:, 4 * g * P:(4 * g + k) * P], tp[:, g % 2, 0:k * P]).then_inc(s_ln["copied"], 1)

                @block.scalar
                def _(act):
                    act.wait_ge(s_ln["stats"], 2 * r + 1)
                    nc.scalar.activation(rstd[:], mv[:, :, 1], ACT.Sqrt, bias=eps[:, 0:1]).then_inc(s_ln["root"], 1)
                    act.wait_ge(s_ln["stats"], 2 * r + 2)
                    for t in range(NT):
                        nc.scalar.activation(H[:, t, :], X[:, t, :], ACT.Relu, bias=nbias[:, t:t + 1],
                                             scale=rstd[:, t:t + 1]).then_inc(s_ln["h"], 1)

                @block.tensor
                def _(pe):
                    for t in range(NT):
                        pe.wait_ge(s_ln["h"], r * NT + t + 1)
                        if t % 4 == 0 and t >= 8:
                            pe.wait_ge(s_ln["copied"], r * NQ + t // 4 - 1)
                        last = nc.tensor.transpose(tp[:, t // 4 % 2, (t % 4) * P:(t % 4 + 1) * P], H[:, t, :], ident[:])
                        if t % 4 == 3 or t == NT - 1:
                            last.then_inc(s_ln["turned"], 1)

        def evacuate(tag, num, AGT):
            with nc.Block() as block:
                @block.vector
                def _(dve):
                    for c, (a, b) in enumerate(CUTS[0::2]):
                        nc.vector.tensor_copy(AGT[:, a:b], num[:, 2 * c, 0:b - a])

                @block.scalar
                def _(act):
                    for c, (a, b) in enumerate(CUTS[1::2]):
                        nc.scalar.activation(AGT[:, a:b], num[:, 2 * c + 1, 0:b - a], ACT.Copy)

        with ExitStack() as ctx:
            s_z = sem("zero_row")
            wraw = [ctx.enter_context(nc.sbuf_tensor("wraw%d" % k, [P, P], F32)) for k in range(2)]
            tp = ctx.enter_context(nc.psum_tensor("ld_tp", [P, 2, BANK], F32))
            s_ld = sem("loads")
            s_ms = sem("memsets")
            s_x = sem("x_padding")
            s_id = sem("identity")
            s_t = sem("w_transposed")
            block = ctx.enter_context(nc.Block())

            @block.sync
            def _(sp):
                sp.wait_ge(s_x, 1)
                sp.dma_start(X[:, 0:NT - 1, :], x[0:(NT - 1) * P, :].rearrange("(t p) d -> p t d", p=P)).then_inc(s_ld, 16)
                sp.dma_start(X[0:NR, NT - 1, :], x[(NT - 1) * P:N, :]).then_inc(s_ld, 16)
                for to, fr in ((wl["w1a"], w1[0:P, :]), (wl["w2"], w2), (wl["u1a"], u1[0:P, :]),
                               (wl["u1b"], u1[P:2 * P, :]), (wl["u2"], u2), (wl["W1"], W1), (wl["W2"], W2),
                               (wraw[0], Ws), (wraw[1], Wn), (w1b, w1[P:P + ED, :])):
                    sp.dma_start(to[:], fr).then_inc(s_ld, 16)
                for name, fr in (("b1", b1), ("b2", b2), ("c2", c2), ("bs", bs), ("bn", bn), ("bb2", bb2)):
                    sp.dma_start(brow[name][:], fr.rearrange("(a d) -> a d", a=1)).then_inc(s_ld, 16)
                sp.dma_start(c1col[:], c1.rearrange("(d a) -> d a", a=1)).then_inc(s_ld, 16)
                sp.wait_ge(s_ld, 16 * 19)

            @block.scalar
            def _(act):
                act.wait_ge(s_z, 2)
                sv = sortd.rearrange("(n p k) w -> n p (k w)", p=P, k=ZR)
                with act.Fori(0, TT // ZR) as n:
                    act.dma_start(sv[ds(n, 1)].squeeze(0), zrow[:].rearrange("p k w -> p (k w)")).then_inc(s_zd, 16)

            @block.gpsimd
            def _(pool):
                nc.gpsimd.memset(zrow[:], 0.0).then_inc(s_z, 1)
                pool.wait_ge(s_z, 1)
                nc.gpsimd.memset(zrow[:, :, D:D + 2], -1.0).then_inc(s_z, 1)
                nc.gpsimd.iota(iota128[:], pattern=[[1, P]], base=0, channel_multiplier=0,
                               allow_small_or_imprecise_dtypes=True)
                nc.gpsimd.memset(ident[:], 0.0).then_inc(s_ms, 1)
                pool.wait_ge(s_ms, 1)
                nc.gpsimd.affine_select(out=ident[:], in_=ident[:], compare_op=ALU.not_equal, fill=1.0, base=0,
                                        pattern=[[-1, P]], channel_multiplier=1).then_inc(s_id, 1)

            @block.vector
            def _(dve):
                nc.vector.memset(X[:], 0.0).then_inc(s_x, 1)
                nc.vector.memset(eps[:], EPS)
                nc.vector.memset(ones[:], 1.0)
                nc.vector.memset(S[:], 0.0)
                for k, name in enumerate(("WsT", "WnT")):
                    dve.wait_ge(s_t, k + 1)
                    nc.vector.tensor_copy(wl[name][:], tp[:, k, 0:P])

            @block.tensor
            def _(pe):
                pe.wait_ge(s_id, 1)
                pe.wait_ge(s_ld, 16 * 19)
                for k in range(2):
                    nc.tensor.transpose(tp[:, k, 0:P], wraw[k][:], ident[:]).then_inc(s_t, 1)

        layernorm(0)

        with ExitStack() as srt:
            def sb(name, shape, dt=F32):
                return srt.enter_context(nc.sbuf_tensor(name, shape, dt))

            raw = sb("raw", [P, 3, EC], I32)
            hi = sb("hi", [P, 2, EC], I32)
            lo = sb("lo", [P, 3, EC])
            tile = sb("tile", [P, 2, EC])
            binf = sb("binf", [P, EC])
            iota25 = sb("iota25", [P, NT])
            iota625 = sb("iota625", [P, BINS], F16)
            tri = sb("tri", [P, P], F16)
            ntri = sb("ntri", [P, P], F16)
            typ = sb("typ", [P, EC])
            relt = sb("relt", [P, NREL])
            iotar = sb("iotar", [P, NREL])
            starts = sb("starts", [1, 2, BINS])
            incb = sb("incb", [P, BINS])

            with ExitStack() as ctx:
                SUB = 62
                ohd = ctx.enter_context(nc.sbuf_tensor("ohd", [P, 2, SUB, NT], F16))
                ohs = ctx.enter_context(nc.sbuf_tensor("ohs", [P, 2, SUB, NT], F16))
                hist = ctx.enter_context(nc.psum_tensor("hist", [NT, 2, BANK], F32))
                triF = ctx.enter_context(nc.sbuf_tensor("triF", [P, P], F32))
                cnt = ctx.enter_context(nc.sbuf_tensor("cnt", [NT, 8, NT], F32))
                cnti = ctx.enter_context(nc.sbuf_tensor("cnti", [NT, 2, NT], I32))
                pre = ctx.enter_context(nc.psum_tensor("pre", [NT, BANK], F32))
                dcol = ctx.enter_context(nc.sbuf_tensor("dcol", [P, 1], I32))
                dcolf = ctx.enter_context(nc.sbuf_tensor("dcolf", [P, 1], F32))
                WC = 2 * CH
                jw = ctx.enter_context(nc.sbuf_tensor("jw", [P, WC, NREL], F32))
                tw = ctx.enter_context(nc.sbuf_tensor("tw", [P, 2, WC], F32))
                kidx = ctx.enter_context(nc.sbuf_tensor("kidx", [P, 3, TCOL], F32))
                junk = ctx.enter_context(nc.sbuf_tensor("junk", [P, BINS], F32))
                edges = ctx.enter_context(nc.sbuf_tensor("edges", [P, NT], F32))
                s_ms = sem("h_memset")
                s_ld = sem("h_load")
                s_ch = sem("h_chain")
                s_oh = sem("h_onehot")
                s_mm = sem("h_counted")
                s_con = sem("h_const")
                s_w = sem("h_weights")
                s_pc = sem("h_pool_chain")
                s_rt = sem("h_row_totals")
                s_pre = sem("h_prefix")
                s_st = sem("h_starts")
                s_bo = sem("h_bounce")
                s_tb = sem("h_tables")
                block = ctx.enter_context(nc.Block())

                @block.sync
                def _(sp):
                    sp.wait_ge(s_ms, 1)
                    for k, a in enumerate((dst, src, et)):
                        sp.dma_start(raw[0:P - 1, k, :], a[0:(P - 1) * EC].rearrange("(p c) -> p c", c=EC)).then_inc(s_ld, 16)
                        sp.dma_start(raw[P - 1:P, k, 0:ER], a[(P - 1) * EC:E].rearrange("(p c) -> p c", p=1)).then_inc(s_ld, 16)
                    sp.dma_start(relt[:], rel.rearrange("r a -> a r").partition_broadcast(P).rearrange("p a r -> p (a r)")).then_inc(s_ld, 16)
                    sp.wait_ge(s_st, 1)
                    sp.dma_start(rows1[0].rearrange("(a b) -> a b", a=NT), cnt[:, 4, :]).then_inc(s_bo, 16)
                    sp.dma_start(rows1[1].rearrange("(a b) -> a b", a=NT), cnt[:, 5, :]).then_inc(s_bo, 16)
                    sp.dma_start(rowinc.rearrange("(a b) -> a b", a=NT), cnt[:, 6, :]).then_inc(s_bo, 16)
                    sp.wait_ge(s_bo, 48)
                    sp.dma_start(starts[0:1, :, :].rearrange("a b c -> a (b c)"), rows1.rearrange("a b -> (a b)").unsqueeze(0)).then_inc(s_bo, 16)
                    sp.dma_start(incb[:], rowinc.partition_broadcast(P)).then_inc(s_bo, 16)
                    sp.wait_ge(s_bo, 80)

                @block.gpsimd
                def _(pool):
                    nc.gpsimd.iota(iota25[:], pattern=[[1, NT]], base=0, channel_multiplier=0,
                                   allow_small_or_imprecise_dtypes=True).then_inc(s_con, 1)
                    nc.gpsimd.iota(iota625[:], pattern=[[1, BINS]], base=0, channel_multiplier=0,
                                   allow_small_or_imprecise_dtypes=True).then_inc(s_con, 1)
                    nc.gpsimd.iota(iotar[:], pattern=[[1, NREL]], base=0, channel_multiplier=0,
                                   allow_small_or_imprecise_dtypes=True).then_inc(s_con, 1)
                    nc.gpsimd.iota(edges[:], pattern=[[NT, NT]], base=NT, channel_multiplier=0,
                                   allow_small_or_imprecise_dtypes=True).then_inc(s_con, 1)
                    for k in range(3):
                        nc.gpsimd.iota(kidx[:, k, :], pattern=[[P, TCOL]], base=k - 1, channel_multiplier=1,
                                       allow_small_or_imprecise_dtypes=True).then_inc(s_con, 1)
                    nc.gpsimd.iota(dcol[:], pattern=[[0, 1]], base=0, channel_multiplier=1).then_inc(s_con, 1)
                    nc.gpsimd.memset(triF[:], 1.0).then_inc(s_pc, 1)
                    pool.wait_ge(s_pc, 1)
                    nc.gpsimd.affine_select(out=triF[:], in_=triF[:], compare_op=ALU.is_gt, fill=0.0, base=0,
                                            pattern=[[1, P]], channel_multiplier=-1).then_inc(s_pc, 1)
                    pool.wait_ge(s_pc, 2)
                    nc.gpsimd.tensor_copy(tri[:], triF[:]).then_inc(s_con, 1)
                    nc.gpsimd.tensor_scalar(ntri[:], triF[:], -1.0, 1.0, ALU.mult, ALU.add).then_inc(s_con, 1)

                @block.vector
                def _(dve):
                    link = Chain(dve, s_ch)
                    link(nc.vector.memset(raw[:, 2, :], 0))
                    nc.vector.memset(raw[:, 0:2, :], NP - 1).then_inc(s_ms, 1)
                    dve.wait_ge(s_ld, 16 * 7)
                    nc.vector.tensor_single_scalar(hi[:], raw[:, 0:2, :], 7, ALU.logical_shift_right)
                    nc.vector.memset(relt[:, 0:1], 0.0)
                    link(nc.vector.tensor_copy(typ[:], raw[:, 2, :]))
                    link(nc.vector.tensor_single_scalar(raw[:, 0:2, :], raw[:, 0:2, :], P - 1, ALU.bitwise_and))
                    nc.vector.tensor_copy(lo[:, 0:2, :], raw[:, 0:2, :])
                    link(nc.vector.tensor_copy(tile[:], hi[:]))
                    link(nc.vector.scalar_tensor_tensor(binf[:], tile[:, 1, :], float(NT), tile[:, 0, :], ALU.mult, ALU.add))
                    dve.wait_ge(s_con, 10)
                    for n in range(EC // SUB):
                        if n >= 2:
                            dve.wait_ge(s_mm, n - 1)
                        c = slice(n * SUB, (n + 1) * SUB)
                        for k, oh in ((0, ohd), (1, ohs)):
                            ins = nc.vector.tensor_tensor(
                                oh[:, n % 2, :, :], iota25[:].unsqueeze(1).to_broadcast([P, SUB, NT]),
                                tile[:, k, c].unsqueeze(2).to_broadcast([P, SUB, NT]), ALU.is_equal)
                        ins.then_inc(s_oh, 1)
                    dve.wait_ge(s_mm, EC // SUB)
                    link(nc.vector.tensor_copy(cnt[:, 0:2, :], hist[:, :, 0:NT]))
                    link(nc.vector.tensor_tensor(cnt[:, 2, :], cnt[:, 0, :], cnt[:, 1, :], ALU.add))
                    link(nc.vector.tensor_scalar(cnt[:, 2, :], cnt[:, 2, :], float(P - 1), float(P), ALU.add, ALU.max))
                    link(nc.vector.tensor_copy(cnti[:, 0, :], cnt[:, 2, :]))
                    link(nc.vector.tensor_single_scalar(cnti[:, 1, :], cnti[:, 0, :], 7, ALU.logical_shift_right))
                    link(nc.vector.tensor_copy(cnt[:, 2, :], cnti[:, 1, :]))
                    link(nc.vector.tensor_tensor_scan(cnt[:, 3, :], ones[0:NT, 0:NT], cnt[:, 2, :], 0.0, ALU.mult, ALU.add))
                    link(nc.vector.tensor_scalar(cnt[:, 7, 2:3], cnt[:, 3, NT - 1:NT], float(G - 1), None, ALU.add))
                    link(nc.vector.tensor_copy(cnti[:, 0, 0:1], cnt[:, 7, 2:3]))
                    link(nc.vector.tensor_single_scalar(cnti[:, 1, 0:1], cnti[:, 0, 0:1], -G, ALU.bitwise_and))
                    nc.vector.tensor_copy(cnt[:, 7, 0:1], cnti[:, 1, 0:1]).then_inc(s_rt, 1)
                    dve.wait_ge(s_pre, 1)
                    link(nc.vector.tensor_copy(cnt[:, 7, 1:2], pre[:, 0:1]))
                    link(nc.vector.tensor_scalar(cnt[:, 6, :], cnt[:, 3, :], cnt[:, 7, 1:2], None, ALU.add))
                    link(nc.vector.tensor_tensor(cnt[:, 3, :], cnt[:, 6, :], cnt[:, 2, :], ALU.subtract))
                    link(nc.vector.tensor_scalar(cnt[:, 4, :], cnt[:, 3, :], float(P), None, ALU.mult))
                    link(nc.vector.tensor_tensor(cnt[:, 6, NT - 1:NT], cnt[:, 7, 0:1], cnt[:, 7, 1:2], ALU.add))
                    nc.vector.tensor_tensor(cnt[:, 5, :], cnt[:, 4, :], cnt[:, 0, :], ALU.add).then_inc(s_st, 1)
                    with dve.Fori(0, EC // WC) as i:
                        nc.vector.tensor_copy(tw[:, 0, :], typ[:, ds(i * WC, WC)]).then_inc(s_w, 1)
                        dve.wait_ge(s_w, i * 3 + 1)
                        for c in range(WC):
                            last = nc.vector.scalar_tensor_tensor(jw[:, c, :], iotar[:], tw[:, 0, c:c + 1], relt[:],
                                                                  ALU.is_equal, ALU.mult, accum_out=tw[:, 1, c:c + 1])
                        last.then_inc(s_w, 1)
                        dve.wait_ge(s_w, i * 3 + 2)
                        nc.vector.tensor_copy(lo[:, 2, ds(i * WC, WC)], tw[:, 1, :]).then_inc(s_w, 1)
                        dve.wait_ge(s_w, i * 3 + 3)
                    dve.wait_ge(s_bo, 80)
                    for k in range(3):
                        for j in range(TCOL):
                            link(nc.vector.tensor_scalar(junk[:], incb[:], kidx[:, k, j:j + 1], None, ALU.is_le,
                                                         ALU.add, accum_out=table[:, k, j:j + 1]))
                    link(nc.vector.tensor_tensor(table[:, 0, :], table[:, 0, :], table[:, 1, :], ALU.is_equal))
                    link(nc.vector.tensor_tensor(table[:, 2, :], table[:, 2, :], table[:, 1, :], ALU.is_equal))
                    for j in range(TCOL):
                        link(nc.vector.tensor_scalar(junk[:, 0:NT], edges[:], table[:, 1, j:j + 1], None, ALU.is_le,
                                                     ALU.add, accum_out=table[:, 3, j:j + 1]))
                    link(nc.vector.scalar_tensor_tensor(table[:, 1, :], table[:, 3, :], -float(NT), table[:, 1, :],
                                                        ALU.mult, ALU.add))
                    link(nc.vector.scalar_tensor_tensor(junk[:, 0:TCOL], table[:, 3, :], float(P * NT), table[:, 1, :],
                                                        ALU.mult, ALU.add))
                    link(nc.vector.tensor_single_scalar(dcol[:, 0:1], dcol[:, 0:1], 3, ALU.bitwise_and))
                    link(nc.vector.tensor_scalar(dcolf[:], dcol[:], float(DUMMY), None, ALU.add))
                    link(nc.vector.tensor_scalar(junk[:, TCOL:2 * TCOL], junk[:, 0:TCOL], dcolf[:, 0:1], -1.0,
                                                 ALU.subtract, ALU.mult))
                    link(nc.vector.tensor_tensor(junk[:, TCOL:2 * TCOL], junk[:, TCOL:2 * TCOL], table[:, 2, :], ALU.mult))
                    nc.vector.tensor_tensor(table[:, 2, :], junk[:, 0:TCOL], junk[:, TCOL:2 * TCOL], ALU.add).then_inc(s_tb, 1)

                @block.tensor
                def _(pe):
                    for n in range(EC // SUB):
                        pe.wait_ge(s_oh, n + 1)
                        for c in range(SUB):
                            a = n * SUB + c
                            last = nc.tensor.matmul(hist[:, a % 2, 0:NT], ohs[:, n % 2, c, :], ohd[:, n % 2, c, :],
                                                    start=(a < 2), stop=(a >= EC - 2))
                        last.then_inc(s_mm, 1)
                    pe.wait_ge(s_rt, 1)
                    nc.tensor.matmul(pre[:, 0:1], triF[0:NT, 0:NT], cnt[:, 7, 0:1], start=True, stop=True).then_inc(s_pre, 1)

            with ExitStack() as ctx:
                trow = nc.dram_tensor("tile_rows", [4, TCOL * P], F32, kind=INTERNAL).ap()
                tf = ctx.enter_context(nc.sbuf_tensor("tf", [1, 3, TT], F32))
                tT = ctx.enter_context(nc.sbuf_tensor("tT", [TCOL, 4, P], F32))
                tp = ctx.enter_context(nc.psum_tensor("tb_tp", [TCOL, 4, P], F32))
                s_t = sem("tb_transposed")
                s_c = sem("tb_copied")
                s_b = sem("tb_bounce")
                block = ctx.enter_context(nc.Block())

                @block.tensor
                def _(pe):
                    for k in range(4):
                        last = nc.tensor.transpose(tp[:, k, :], table[:, k, :], ident[:])
                    last.then_inc(s_t, 1)

                @block.vector
                def _(dve):
                    dve.wait_ge(s_t, 1)
                    nc.vector.tensor_copy(tT[:], tp[:]).then_inc(s_c, 1)
                    dve.wait_ge(s_b, 80)
                    nc.vector.tensor_copy(tilei[:], tf[:])

                @block.sync
                def _(sp):
                    sp.wait_ge(s_zd, 16 * (TT // ZR))
                    sp.wait_ge(s_c, 1)
                    sp.dma_start(trow.rearrange("k (j p) -> j k p", p=P), tT[:]).then_inc(s_b, 16)
                    sp.wait_ge(s_b, 16)
                    sp.dma_start(keep[:], trow[0, 0:TT].partition_broadcast(P)).then_inc(s_b, 16)
                    for k, r in ((0, 1), (1, 3), (2, 2)):
                        sp.dma_start(tf[:, k, :], trow[r:r + 1, 0:TT]).then_inc(s_b, 16)
                    sp.wait_ge(s_b, 80)

            with ExitStack() as ctx:
                def sb2(name, shape, dt=F32):
                    return ctx.enter_context(nc.sbuf_tensor(name, shape, dt))

                K = 2 * CH
                BODIES = NCH // 2
                ef = sb2("ef", [P, 2, CH, ED])
                eT = sb2("eT", [ED, 2, P])
                rows = sb2("rows", [P, 2, CH, ROW])
                binc = sb2("binc", [P, 2, CH])
                oh = sb2("oh", [P, CH, BINS], F16)
                posf = sb2("posf", [P, 2, CH])
                posi = sb2("posi", [P, 2, CH], I32)
                junk = sb2("junk2", [P, 2, BINS])
                run = ctx.enter_context(nc.psum_tensor("run", [P, 2, 2 * BANK], F32))
                pe_t = ctx.enter_context(nc.psum_tensor("s_pet", [P, 2, BANK], F32))
                pe_q = ctx.enter_context(nc.psum_tensor("s_peq", [P, 2, BANK], F32))
                s_row = [sem("s_row_a"), sem("s_row_b")]
                s_idx = sem("s_row_indices")
                s_bin = sem("s_bins_copied")
                s_oh = sem("s_onehot")
                s_run = sem("s_running")
                s_pos = sem("s_position")
                s_upd = sem("s_run_updated")
                s_int = sem("s_position_int")
                s_te = sem("s_features_turned")
                s_ce = sem("s_features_copied")
                s_q = sem("s_projected")
                s_cq = sem("s_projected_copied")
                s_sc = [sem("s_scattered_a"), sem("s_scattered_b")]
                s_pad = sem("s_rows_padded")
                s_go = sem("s_pool_passed")
                s_ago = sem("s_act_passed")
                block = ctx.enter_context(nc.Block())

                def half(k):
                    return k // CH, k % CH

                def prev(i, k):
                    return (i, k - 1) if k else (i - 1, K - 1)

                @block.sync
                def _(sp):
                    sp.wait_ge(s_pad, 2)

                    def load(i, h, first):
                        if not first:
                            sp.wait_ge(s_te, (i - 1) * K + (h + 1) * CH)
                        c0 = (i * 2 + h) * CH
                        sp.dma_start(ef[0:P - 1, h, :, :],
                                     ea[0:(P - 1) * EC, :].rearrange("(p c) d -> p c d", c=EC)[:, ds(c0, CH), :]).then_inc(s_row[h], 16)

                    def load_last(i, h, n):
                        c0 = (P - 1) * EC + (i * 2 + h) * CH
                        sp.dma_start(ef[P - 1:P, h, 0:n, :], ea[ds(c0, n), :].unsqueeze(0)).then_inc(s_row[h], 16)

                    whole = ER // CH // 2
                    for h in range(2):
                        load(0, h, True)
                        load_last(0, h, CH)
                    with sp.Fori(1, whole) as i:
                        for h in range(2):
                            load(i, h, False)
                            load_last(i, h, CH)
                    for i in range(whole, BODIES):
                        for h in range(2):
                            load(i, h, False)
                            n = min(CH, ER - (i * 2 + h) * CH)
                            if n > 0:
                                load_last(i, h, n)
                            else:
                                load_last(0, h, 1)

                @block.scalar
                def _(act):
                    act.wait_ge(s_pad, 2)

                    def projected(i, k):
                        h, c = half(k)
                        act.wait_ge(s_q, i * K + k + 1)
                        nc.scalar.activation(rows[:, h, c, 0:D], pe_q[:, k % 2, 0:D], ACT.Copy).then_inc(s_cq, 1)

                    def step(i, first):
                        for k in range(K):
                            h, c = half(k)
                            act.wait_ge(s_te, i * K + k + 1)
                            nc.scalar.activation(eT[:, k % 2, :], pe_t[0:ED, k % 2, 0:P], ACT.Copy).then_inc(s_ce, 1)
                            if not (first and k == 0):
                                projected(*prev(i, k))
                            if c == 0:
                                if not first:
                                    act.wait_ge(s_sc[h], i * (16 * CH))
                                act.sem_inc(s_ago, 1)
                                nc.scalar.activation(rows[:, h, :, D:D + 3].rearrange("p c k -> p k c"),
                                                     lo[:, :, ds((i * 2 + h) * CH, CH)], ACT.Copy).then_inc(s_idx, 1)
                            act.wait_ge(s_pos, i * K + k + 1)
                            nc.scalar.activation(posi[:, h, c:c + 1], posf[:, h, c:c + 1], ACT.Copy).then_inc(s_int, 1)
                    step(0, True)
                    with act.Fori(1, BODIES) as i:
                        step(i, False)
                    projected(BODIES - 1, K - 1)

                @block.vector
                def _(dve):
                    nc.vector.memset(rows[:], 0.0).then_inc(s_pad, 1)
                    nc.vector.memset(ef[:], 0.0).then_inc(s_pad, 1)

                    def step(i, first):
                        for h in range(2):
                            c0 = (i * 2 + h) * CH
                            if not first:
                                dve.wait_ge(s_int, (i - 1) * K + (h + 1) * CH)
                            nc.vector.tensor_copy(binc[:, h, :], binf[:, ds(c0, CH)]).then_inc(s_bin, 1)
                            dve.wait_ge(s_bin, i * 2 + h + 1)

                            def onehot(c):
                                if not (first and h == 0):
                                    dve.wait_ge(s_upd, i * K + h * CH + c - CH + 1)
                                nc.vector.tensor_scalar(oh[:, c, :], iota625[:], binc[:, h, c:c + 1], None,
                                                        ALU.is_equal).then_inc(s_oh, 1)

                            onehot(0)
                            for c in range(CH):
                                k = h * CH + c
                                if c + 1 < CH:
                                    onehot(c + 1)
                                dve.wait_ge(s_run, i * K + k + 1)
                                nc.vector.tensor_tensor_reduce(
                                    junk[:, k % 2, :], run[:, k % 2, 0:BINS], oh[:, c, :], 1.0, 0.0, ALU.mult, ALU.add,
                                    posf[:, h, c:c + 1]).then_inc(s_pos, 1)
                    step(0, True)
                    with dve.Fori(1, BODIES) as i:
                        step(i, False)

                @block.tensor
                def _(pe):
                    parts = ((0, BANK), (BANK, BINS))
                    for k in range(2):
                        for a, b in parts:
                            nc.tensor.matmul(run[:, k, a:b], ones[0:1, :], starts[:, k, a:b], start=True, stop=False,
                                             skip_group_check=True)

                    def update(i, k):
                        pe.wait_ge(s_pos, i * K + k + 1)
                        for a, b in parts:
                            last = nc.tensor.matmul(run[:, k % 2, a:b], ntri[:], oh[:, k % CH, a:b], start=False,
                                                    stop=False, skip_group_check=True)
                        last.then_inc(s_upd, 1)

                    def project(i, k, first):
                        n = i * K + k
                        pe.wait_ge(s_ce, n + 1)
                        if not (first and k < 2):
                            pe.wait_ge(s_cq, n - 1)
                        nc.tensor.matmul(pe_q[:, k % 2, 0:D], eT[:, k % 2, :], w1b[:], start=True, stop=True).then_inc(s_q, 1)

                    def step(i, first):
                        for k in range(K):
                            h, c = half(k)
                            if c == 0:
                                pe.wait_ge(s_row[h], i * 32 + 32)
                            pe.wait_ge(s_oh, i * K + k + 1)
                            for a, b in parts:
                                last = nc.tensor.matmul(run[:, k % 2, a:b], tri[:], oh[:, c, a:b], start=False,
                                                        stop=False, skip_group_check=True)
                            last.then_inc(s_run, 1)
                            nc.tensor.matmul(pe_t[0:ED, k % 2, 0:P], ef[:, h, c, :], ident[:], is_transpose=True,
                                             start=True, stop=True).then_inc(s_te, 1)
                            if not (first and k < 1):
                                project(*prev(i, k), first)
                                update(*prev(i, k))
                    step(0, True)
                    with pe.Fori(1, BODIES) as i:
                        step(i, False)
                    project(BODIES - 1, K - 1, False)

                @block.gpsimd
                def _(pool):
                    def step(i):
                        for k in range(K):
                            h, c = half(k)
                            if c == 0:
                                pool.wait_ge(s_idx, i * 2 + h + 1)
                            pool.wait_ge(s_cq, i * K + k + 1)
                            pool.wait_ge(s_int, i * K + k + 1)
                            pool.sem_inc(s_go, 1)
                            pool.indirect_dma_start(
                                sortd, bass.IndirectOffsetOnAxis(ap=posi[:, h, c:c + 1], axis=0),
                                rows[:, h, c, :], None).then_inc(s_sc[h], 16)
                    step(0)
                    with pool.Fori(1, BODIES) as i:
                        step(i)
                    for h in range(2):
                        pool.wait_ge(s_sc[h], 16 * CH * BODIES)

        with ExitStack() as ctx:
            def sb(name, shape, dt=F32):
                return ctx.enter_context(nc.sbuf_tensor(name, shape, dt))

            def pb(name, shape, dt=F32):
                return ctx.enter_context(nc.psum_tensor(name, shape, dt))

            PN = sb("PN", [P, NT + 1, 3, D], BF16)
            pr = sb("pr", [P, 2, 2, D])
            iota16 = sb("iota16", [P, P], BF16)
            ident16 = sb("ident16", [P, P], BF16)
            rt = sb("rt", [P, RING, G, ROW])
            ohd = sb("ohd_e", [P, RING, G, P], BF16)
            ohw = sb("ohw_e", [P, RING, G, P])
            ohs = sb("ohs_e", [P, RING, G, P])
            ohs16 = sb("ohs16_e", [P, RING, G, P], BF16)
            dT = sb("dT", [P, 2, G, P], BF16)
            pre = sb("pre_e", [P, 2, G, P])
            hid = sb("hid", [P, 2, G, D + 1])
            acc = sb("acc", [P, G, 2 * P])
            pdt = pb("pdt", [P, 2 * G, P], BF16)
            px = pb("px", [P, 2, G, P])
            pm = pb("pm", [P, 2, 2, 2 * P])
            ps = pb("ps", [P, 2, BANK])
            s_pn = sem("e_pn")
            s_pc = sem("e_pn_copied")
            s_pr = sem("e_pn_parts")
            s_k = sem("e_constants")
            s_rt = [sem("e_rows%d" % r) for r in range(RING)]
            s_od = sem("e_dst_onehots")
            s_os = sem("e_src_onehots")
            s_o16 = sem("e_src_onehots16")
            s_td = sem("e_dst_turned")
            s_cd = sem("e_dst_copied")
            s_x = sem("e_hidden")
            s_pre = sem("e_pre")
            s_g = sem("e_leaky")
            s_ow = sem("e_weighted_onehots")
            s_m = sem("e_pair_products")
            s_acc = sem("e_accumulated")
            s_sp = sem("e_group_sums")
            s_sa = sem("e_sums_added")
            s_w = [sem("e_written%d" % k) for k in range(G)]
            s_go = sem("e_pool_passed")
            block = ctx.enter_context(nc.Block())
            sv = sortd.rearrange("(n j p) w -> n p j w", p=P, j=G)
            GROUPS = LOOPS * RING


            @block.sync
            def _(sp):
                def load(n, r):
                    sp.dma_start(rt[:, r, :, :], sv[ds(n, 1)].squeeze(0)).then_inc(s_rt[r], 16)

                def step(i, k, more):
                    n = i * RING + k
                    rows = loads(nc, mybir.EngineType.SP, tilei[0:1, 2, ds(n * G, G)], DUMMY + 3)
                    for j in range(G):
                        sp.wait_ge(s_acc, n * G + j + 1)
                        sp.dma_start(ar[ds(rows[j], P, NT), :], acc[:, j, :]).then_inc(s_w[j], 16)
                    if more:
                        load(n + RING, k)

                for r in range(RING):
                    load(r, r)
                with sp.Fori(0, LOOPS - 1) as i:
                    for k in range(RING):
                        step(i, k, True)
                for k in range(RING):
                    step(LOOPS - 1, k, False)
                for k in range(G):
                    sp.wait_ge(s_w[k], 16 * TT // G)

            @block.gpsimd
            def _(pool):
                def step(i, k, first):
                    n = i * RING + k
                    pool.wait_ge(s_rt[k], i * 16 + 16)
                    if not first:
                        pool.wait_ge(s_sp, n - RING + 1)
                        pool.wait_ge(s_o16, n - RING + 1)
                    pool.sem_inc(s_go, 1)
                    for j in range(G):
                        last = nc.gpsimd.tensor_scalar(ohs[:, k, j, :], iota128[:], rt[:, k, j, D + 1:D + 2], None, ALU.is_equal)
                    last.then_inc(s_os, 1)

                for k in range(RING):
                    step(0, k, True)
                with pool.Fori(1, LOOPS) as i:
                    for k in range(RING):
                        step(i, k, False)

            @block.scalar
            def _(act):
                def step(i, k, first):
                    n = i * RING + k
                    if not (first and k < 2):
                        act.wait_ge(s_x, n - 1)
                    act.wait_ge(s_td, n + 1)
                    nc.scalar.activation(dT[:, k % 2, :, :], pdt[:, 0:G, :], ACT.Copy).then_inc(s_cd, 1)
                    if not first:
                        act.wait_ge(s_m, 2 * (n - RING) + 2)
                    act.wait_ge(s_os, n + 1)
                    nc.scalar.activation(ohs16[:, k, :, :], ohs[:, k, :, :], ACT.Copy).then_inc(s_o16, 1)
                    for j in range(G):
                        last = nc.scalar.activation(ohw[:, k, j, :], ohd[:, k, j, :], ACT.Copy, scale=rt[:, k, j, D + 2:D + 3])
                    last.then_inc(s_ow, 1)

                for k in range(RING):
                    step(0, k, True)
                with act.Fori(1, LOOPS) as i:
                    for k in range(RING):
                        step(i, k, False)

            @block.tensor
            def _(pe):
                for t in range(NT):
                    if t >= 2:
                        pe.wait_ge(s_pc, t - 1)
                    nc.tensor.matmul(px[:, t % 2, 0, :], HT[:, t * P:(t + 1) * P], wl["w1a"][:], start=True, stop=False)
                    nc.tensor.matmul(px[:, t % 2, 0, :], ones[0:1, :], brow["b1"][:], start=False, stop=True).then_inc(s_pn, 1)
                pe.wait_ge(s_k, 1)

                def turn(i, k, first):
                    n = i * RING + k
                    pe.wait_ge(s_od, n + 1)
                    if not (first and k < 1):
                        pe.wait_ge(s_cd, n)
                    for j in range(G):
                        last = nc.tensor.transpose(pdt[:, j, :], ohd[:, k, j, :], ident16[:])
                    last.then_inc(s_td, 1)

                def hidden(i, k, first):
                    n = i * RING + k
                    dt = loads(nc, mybir.EngineType.PE, tilei[0:1, 0, ds(n * G, G)], NT)
                    pe.wait_ge(s_cd, n + 1)
                    if not (first and k < 2):
                        pe.wait_ge(s_pre, n - 1)
                    for j in range(G):
                        for part in range(3):
                            last = nc.tensor.matmul(px[:, k % 2, j, :], dT[:, k % 2, j, :],
                                                    PN[:, ds(dt[j], 1), part, :].squeeze(1), start=(part == 0), stop=(part == 2))
                    last.then_inc(s_x, 1)

                def products(i, k, first):
                    n = i * RING + k
                    pe.wait_ge(s_g, n + 1)
                    pe.wait_ge(s_ow, n + 1)
                    if not (first and k < 2):
                        pe.wait_ge(s_sa, n - 1)
                    for j in range(G):
                        q = j // 2
                        if j % 2 == 0 and not (first and k < 1):
                            pe.wait_ge(s_acc, (n - 1) * G + 2 * q + 2)
                        nc.tensor.matmul(pm[:, q, j % 2, 0:P], ohs16[:, k, j, :], ohd[:, k, j, :], start=True, stop=True)
                        last = nc.tensor.matmul(pm[:, q, j % 2, P:2 * P], ohs[:, k, j, :], ohw[:, k, j, :], start=True, stop=True)
                        if j % 2:
                            last.then_inc(s_m, 1)
                    for j in range(G):
                        last = nc.tensor.matmul(ps[:, k % 2, 0:D + 1], ohs[:, k, j, :], hid[:, k % 2, j, :],
                                                start=(j == 0), stop=(j == G - 1))
                    last.then_inc(s_sp, 1)

                def step(i, k, first):
                    turn(i, k, first)
                    if not (first and k < 1):
                        hidden(*back(i, k, 1), first)
                    if not (first and k < 2):
                        products(*back(i, k, 2), first)

                for k in range(RING):
                    step(0, k, True)
                with pe.Fori(1, LOOPS) as i:
                    for k in range(RING):
                        step(i, k, False)
                hidden(LOOPS - 1, RING - 1, False)
                products(LOOPS - 1, RING - 2, False)
                products(LOOPS - 1, RING - 1, False)

            @block.vector
            def _(dve):
                nc.vector.tensor_copy(iota16[:], iota128[:])
                nc.vector.tensor_copy(ident16[:], ident[:])
                nc.vector.memset(acc[:], 0.0)
                nc.vector.memset(hid[:], 1.0)
                link = Chain(dve, s_pr)
                for t in range(NT):
                    dve.wait_ge(s_pn, t + 1)
                    v = px[:, t % 2, 0, :]
                    link(nc.vector.tensor_copy(PN[:, t, 0, :], v))
                    link(nc.vector.tensor_tensor(pr[:, t % 2, 0, :], v, PN[:, t, 0, :], ALU.subtract))
                    nc.vector.tensor_copy(PN[:, t, 1, :], pr[:, t % 2, 0, :]).then_inc(s_pc, 1)
                    dve.wait_ge(s_pc, t + 1)
                    nc.vector.tensor_tensor(PN[:, t, 2, :], pr[:, t % 2, 0, :], PN[:, t, 1, :], ALU.subtract)
                link(nc.vector.memset(PN[:, NT, :, :], 0.0))
                dve.drain().then_inc(s_k, 1)
                dve.wait_ge(s_k, 1)

                def onehots(i, k, first, js):
                    n = i * RING + k
                    if js[0] == 0:
                        dve.wait_ge(s_rt[k], i * 16 + 16)
                        if not first:
                            dve.wait_ge(s_m, 2 * (n - RING) + 2)
                    for j in js:
                        last = nc.vector.tensor_scalar(ohd[:, k, j, :], iota16[:], rt[:, k, j, D:D + 1], None, ALU.is_equal)
                    if js[-1] == G - 1:
                        last.then_inc(s_od, 1)

                def add(i, k, first):
                    n = i * RING + k
                    dve.wait_ge(s_x, n + 1)
                    nc.vector.tensor_tensor(pre[:, k % 2, :, :], px[:, k % 2, :, :], rt[:, k, :, 0:D], ALU.add).then_inc(s_pre, 1)

                def leaky(i, k, first):
                    n = i * RING + k
                    dve.wait_ge(s_pre, n + 1)
                    nc.vector.scalar_tensor_tensor(hid[:, k % 2, :, 0:D], pre[:, k % 2, :, :], 0.2, pre[:, k % 2, :, :],
                                                   ALU.mult, ALU.max).then_inc(s_g, 1)

                def collect(i, k, first, j):
                    n = i * RING + k
                    if j % 2 == 0:
                        dve.wait_ge(s_m, 2 * n + j // 2 + 1)
                    if not (first and k < 1):
                        dve.wait_ge(s_w[j], n * 16)
                    if not (first and k < 1 and j < 1):
                        dve.wait_ge(s_acc, n * G + j)
                    at = n * G + j
                    nc.vector.scalar_tensor_tensor(acc[:, j, :], acc[:, (j - 1) % G, :],
                                                   keep[:, at:at + 1] if isinstance(at, int) else keep[:, ds(at, 1)],
                                                   pm[:, j // 2, j % 2, :], ALU.mult, ALU.add).then_inc(s_acc, 1)

                def sums(i, k, first):
                    n = i * RING + k
                    st = loads(nc, mybir.EngineType.DVE, tilei[0:1, 1, ds(n * G, 1)], NT)[0]
                    dve.wait_ge(s_sp, n + 1)
                    if not (first and k < 1):
                        dve.wait_ge(s_sa, n)
                    Sv = S[:, ds(st, 1), :].squeeze(1)
                    nc.vector.tensor_tensor(Sv, Sv, ps[:, k % 2, 0:D + 1], ALU.add).then_inc(s_sa, 1)

                def step(i, k, first, last):
                    one, two = (not (first and k < 1)), (not (first and k < 2))
                    b1, b2, nx = back(i, k, 1), back(i, k, 2), back(i, k, -1)
                    if one:
                        add(*b1, first)
                    if two:
                        collect(*b2, first, 0)
                    if one:
                        leaky(*b1, first)
                    if two:
                        collect(*b2, first, 1)
                    if not last:
                        onehots(*nx, first and k + 1 < RING, (0, 1))
                    if two:
                        collect(*b2, first, 2)
                    if not last:
                        onehots(*nx, first and k + 1 < RING, (2, 3))
                    if two:
                        collect(*b2, first, 3)
                        sums(*b2, first)

                onehots(0, 0, True, (0, 1, 2, 3))
                for k in range(RING):
                    step(0, k, True, False)
                with dve.Fori(1, LOOPS - 1) as i:
                    for k in range(RING):
                        step(i, k, False, False)
                for k in range(RING):
                    step(LOOPS - 1, k, False, k == RING - 1)
                add(LOOPS - 1, RING - 1, False)
                leaky(LOOPS - 1, RING - 1, False)
                for k in (RING - 2, RING - 1):
                    for j in range(G):
                        collect(LOOPS - 1, k, False, j)
                    sums(LOOPS - 1, k, False)

        with ExitStack() as ctx:
            ST = ctx.enter_context(nc.sbuf_tensor("ST", [P, NP], F32))
            OD = ctx.enter_context(nc.sbuf_tensor("OD", [1, NP], F32))
            AG = ctx.enter_context(nc.sbuf_tensor("AG", [P, NP], F32))
            Y2 = ctx.enter_context(nc.sbuf_tensor("Y2", [P, 2, BANK], F32))
            c02 = ctx.enter_context(nc.sbuf_tensor("c02", [P, 1], F32))
            tp = ctx.enter_context(nc.psum_tensor("u_tp", [P, 2, BANK], F32))
            tr = ctx.enter_context(nc.psum_tensor("u_tr", [1, 2, BANK], F32))
            mm = ctx.enter_context(nc.psum_tensor("u_mm", [P, 2, BANK], F32))
            po = ctx.enter_context(nc.psum_tensor("u_po", [P, 2, BANK], F32))
            s_t = sem("u_transposed")
            s_tc = sem("u_transposed_copied")
            s_a = sem("u_aggregate")
            s_ac = sem("u_aggregate_copied")
            s_h = sem("u_hidden")
            s_y = sem("u_hidden_02")
            s_hc = sem("u_hidden_done")
            s_o = sem("u_out")
            s_x = sem("u_x")
            s_c = sem("u_bias_02")
            block = ctx.enter_context(nc.Block())
            NC = len(CUTS)

            @block.tensor
            def _(pe):
                def turn(c):
                    a, b = CUTS[c]
                    if c >= 2:
                        pe.wait_ge(s_tc, c - 1)
                    for t in range(a // P, b // P):
                        o = t * P - a
                        nc.tensor.transpose(tp[:, c % 2, o:o + P], S[:, t, 0:D], ident[:])
                        last = nc.tensor.transpose(tr[:, c % 2, o:o + P], S[:, t, D:D + 1], ident[:])
                    last.then_inc(s_t, 1)

                def aggregate(c):
                    a, b = CUTS[c]
                    pe.wait_ge(s_tc, c + 1)
                    if c >= 1:
                        pe.wait_ge(s_hc, c)
                    nc.tensor.matmul(mm[:, 0, 0:b - a], wl["w2"][:], ST[:, a:b], start=True, stop=False)
                    nc.tensor.matmul(mm[:, 0, 0:b - a], brow["b2"][:], OD[:, a:b], start=False, stop=True).then_inc(s_a, 1)

                def hidden(c):
                    a, b = CUTS[c]
                    nc.tensor.matmul(mm[:, 1, 0:b - a], wl["u1a"][:], HT[:, a:b], start=True, stop=False)
                    pe.wait_ge(s_ac, c + 1)
                    nc.tensor.matmul(mm[:, 1, 0:b - a], wl["u1b"][:], AG[:, a:b], start=False, stop=True).then_inc(s_h, 1)

                def out_tiles(c):
                    a, b = CUTS[c]
                    pe.wait_ge(s_hc, c + 1)
                    for t in range(a // P, b // P):
                        if t >= 2:
                            pe.wait_ge(s_x, t - 1)
                        nc.tensor.matmul(po[:, t % 2, 0:D], ST[:, t * P:(t + 1) * P], wl["u2"][:], start=True, stop=False)
                        nc.tensor.matmul(po[:, t % 2, 0:D], ones[0:1, :], brow["c2"][:], start=False, stop=True).then_inc(s_o, 1)

                turn(0)
                for c in range(NC):
                    if c + 1 < NC:
                        turn(c + 1)
                    aggregate(c)
                    hidden(c)
                    out_tiles(c)

            @block.scalar
            def _(act):
                nc.scalar.activation(c02[:], c1col[:], ACT.Copy, scale=0.2).then_inc(s_c, 1)
                act.wait_ge(s_c, 1)
                for c, (a, b) in enumerate(CUTS):
                    act.wait_ge(s_a, c + 1)
                    nc.scalar.activation(AG[:, a:b], mm[:, 0, 0:b - a], ACT.Copy).then_inc(s_ac, 1)
                    act.wait_ge(s_h, c + 1)
                    nc.scalar.activation(Y2[:, c % 2, 0:b - a], mm[:, 1, 0:b - a], ACT.Identity, scale=0.2,
                                         bias=c02[:, 0:1]).then_inc(s_y, 1)

            @block.vector
            def _(dve):
                def copy(c):
                    a, b = CUTS[c]
                    dve.wait_ge(s_t, c + 1)
                    nc.vector.tensor_copy(ST[:, a:b], tp[:, c % 2, 0:b - a])
                    nc.vector.tensor_copy(OD[:, a:b], tr[:, c % 2, 0:b - a]).then_inc(s_tc, 1)

                copy(0)
                for c, (a, b) in enumerate(CUTS):
                    if c + 1 < NC:
                        copy(c + 1)
                    dve.wait_ge(s_y, c + 1)
                    nc.vector.scalar_tensor_tensor(ST[:, a:b], mm[:, 1, 0:b - a], c1col[:, 0:1], Y2[:, c % 2, 0:b - a],
                                                   ALU.add, ALU.max).then_inc(s_hc, 1)
                    for t in range(a // P, b // P):
                        dve.wait_ge(s_o, t + 1)
                        nc.vector.tensor_tensor(X[:, t, :], X[:, t, :], po[:, t % 2, 0:D], ALU.add).then_inc(s_x, 1)

        mid.close()
        layernorm(1)

        arv = ar.rearrange("(s p q) c -> s p q c", p=P, q=NT)
        HALF = [(0, 12), (12, NT)]

        with ExitStack() as lay:
            ss = lay.enter_context(nc.sbuf_tensor("ss", [P, 3, NT], F32))
            sd = lay.enter_context(nc.sbuf_tensor("sd", [P, NT], F32))
            mn = lay.enter_context(nc.sbuf_tensor("mn", [P, 2], F32))
            MX = lay.enter_context(nc.sbuf_tensor("MX", [P, NP], F32))
            DG = lay.enter_context(nc.sbuf_tensor("DG", [P, NP], F32))
            with ExitStack() as ctx:
                WT = ctx.enter_context(nc.sbuf_tensor("WT", [P, P], F32))
                at = ctx.enter_context(nc.sbuf_tensor("at", [P, 2], F32))
                wa = ctx.enter_context(nc.sbuf_tensor("wa", [P, 2], F32))
                m1 = ctx.enter_context(nc.sbuf_tensor("m1", [P, 1], F32))
                m2 = ctx.enter_context(nc.sbuf_tensor("m2", [1, 1], F32))
                tp = ctx.enter_context(nc.psum_tensor("s_tp", [P, BANK], F32))
                pw = ctx.enter_context(nc.psum_tensor("s_pw", [P, BANK], F32))
                pss = ctx.enter_context(nc.psum_tensor("s_pss", [P, BANK // 2, 2], F32))
                pt = ctx.enter_context(nc.psum_tensor("s_pt", [1, BANK], F32))
                pb = ctx.enter_context(nc.psum_tensor("s_pb", [P, BANK], F32))
                s_ld = sem("a_attn")
                s_pe = sem("a_pe")
                s_dv = sem("a_dve")
                s_ch = sem("a_chain")
                block = ctx.enter_context(nc.Block())

                @block.sync
                def _(sp):
                    with nc.allow_non_contiguous_dma(reason="the attention vector as two columns"):
                        sp.dma_start(at[:], attn.rearrange("(a d) -> d a", a=2)).then_inc(s_ld, 16)
                    sp.wait_ge(s_ld, 16)

                @block.tensor
                def _(pe):
                    nc.tensor.transpose(tp[:, 0:P], wl["W1"][:], ident[:]).then_inc(s_pe, 1)
                    pe.wait_ge(s_ld, 16)
                    pe.wait_ge(s_dv, 1)
                    nc.tensor.matmul(pw[:, 0:2], WT[:], at[:], start=True, stop=True).then_inc(s_pe, 1)
                    pe.wait_ge(s_dv, 2)
                    for t in range(NT):
                        last = nc.tensor.matmul(pss[:, t, :], HT[:, t * P:(t + 1) * P], wa[:], start=True, stop=True)
                    last.then_inc(s_pe, 1)
                    pe.wait_ge(s_dv, 3)
                    nc.tensor.transpose(pt[:, 0:P], m1[:], ident[:]).then_inc(s_pe, 1)
                    pe.wait_ge(s_dv, 4)
                    nc.tensor.matmul(pb[:, 0:1], ones[0:1, :], m2[:], start=True, stop=True).then_inc(s_pe, 1)

                @block.vector
                def _(dve):
                    link = Chain(dve, s_ch)
                    nc.vector.memset(MX[:], 0.0)
                    nc.vector.memset(DG[:], 0.0)
                    dve.wait_ge(s_pe, 1)
                    nc.vector.tensor_copy(WT[:], tp[:, 0:P]).then_inc(s_dv, 1)
                    dve.wait_ge(s_pe, 2)
                    nc.vector.tensor_copy(wa[:], pw[:, 0:2]).then_inc(s_dv, 1)
                    dve.wait_ge(s_pe, 3)
                    nc.vector.tensor_copy(sd[:], pss[:, 0:NT, 1])
                    link(nc.vector.tensor_copy(ss[:, 0, :], pss[:, 0:NT, 0]))
                    nc.vector.tensor_scalar(ss[:, 1, :], ss[:, 0, :], 0.01, None, ALU.mult)
                    nc.vector.tensor_reduce(m1[:], ss[:, 0, :], AX.X, ALU.min).then_inc(s_dv, 1)
                    dve.wait_ge(s_pe, 4)
                    nc.vector.tensor_reduce(m2[:], pt[:, 0:P], AX.X, ALU.min).then_inc(s_dv, 1)
                    dve.wait_ge(s_pe, 5)
                    link(nc.vector.tensor_scalar(mn[:, 0:1], pb[:, 0:1], -1.0, None, ALU.add))
                    nc.vector.tensor_scalar(ss[:, 2, :], ss[:, 0, :], mn[:, 0:1], None, ALU.subtract)

            with ExitStack() as ctx:
                ab = ctx.enter_context(nc.sbuf_tensor("ab", [P, NT, P], F32))
                tm = ctx.enter_context(nc.sbuf_tensor("tm", [P, NT, P], F32))
                MXv = MX[:].rearrange("p (q d) -> p q d", q=NT)
                DGv = DG[:].rearrange("p (q d) -> p q d", q=NT)
                s_ld = [sem("m_load_a"), sem("m_load_b")]
                s_mk = sem("m_masked")
                s_mx = sem("m_max")
                s_dg = sem("m_degree")
                block = ctx.enter_context(nc.Block())

                @block.sync
                def _(sp):
                    def load(s, h):
                        a, b = HALF[h]
                        sp.dma_start(ab[:, a:b, :], arv[ds(s, 1), :, a:b, 0:P].squeeze(0)).then_inc(s_ld[h], 16)
                    load(0, 0)
                    load(0, 1)
                    with sp.Fori(1, NT) as s:
                        for h in range(2):
                            sp.wait_ge(s_mk, s * 2 + h - 1)
                            sp.wait_ge(s_dg, s * 2 + h - 1)
                            load(s, h)

                @block.vector
                def _(dve):
                    def step(s, first):
                        for h, (a, b) in enumerate(HALF):
                            dve.wait_ge(s_ld[h], s * 16 + 16)
                            if not first:
                                dve.wait_ge(s_mx, s * 2 + h - 1)
                            nc.vector.tensor_scalar(tm[:, a:b, :], ab[:, a:b, :], 0.0, ss[:, 2, ds(s, 1)], ALU.is_gt,
                                                    ALU.mult).then_inc(s_mk, 1)
                            dve.wait_ge(s_mk, s * 2 + h + 1)
                            nc.vector.tensor_tensor(MXv[:, a:b, :], MXv[:, a:b, :], tm[:, a:b, :], ALU.max).then_inc(s_mx, 1)
                    step(0, True)
                    with dve.Fori(1, NT) as s:
                        step(s, False)

                @block.gpsimd
                def _(pool):
                    def step(s, first):
                        for h, (a, b) in enumerate(HALF):
                            pool.wait_ge(s_ld[h], s * 16 + 16)
                            if not first:
                                pool.wait_ge(s_dg, s * 2 + h - 1)
                            nc.gpsimd.tensor_tensor(DGv[:, a:b, :], DGv[:, a:b, :], ab[:, a:b, :], ALU.add).then_inc(s_dg, 1)
                    step(0, True)
                    with pool.Fori(1, NT) as s:
                        step(s, False)

            RB = lay.enter_context(nc.sbuf_tensor("RB", [P, 2, NP], F32))
            with ExitStack() as ctx:
                mc = ctx.enter_context(nc.sbuf_tensor("mc", [P, 3, NT], F32))
                dm = ctx.enter_context(nc.sbuf_tensor("dm", [P, 2 * NT], F32))
                dT = ctx.enter_context(nc.sbuf_tensor("dmT", [2 * NT, P], F32))
                tp = ctx.enter_context(nc.psum_tensor("x_tp", [P, 2, BANK], F32))
                pd = ctx.enter_context(nc.psum_tensor("x_pd", [P, BANK], F32))
                pr = ctx.enter_context(nc.psum_tensor("x_pr", [2 * NT, BANK], F32))
                s_t = sem("x_turned")
                s_r = sem("x_reduced")
                s_d = sem("x_degrees")
                s_m = sem("x_rows")
                s_mt = sem("x_rows_turned")
                s_mc = sem("x_rows_copied")
                s_b = sem("x_bounce")
                s_ch = sem("x_chain")
                block = ctx.enter_context(nc.Block())

                @block.tensor
                def _(pe):
                    for t in range(NT):
                        last = nc.tensor.matmul(pd[:, t:t + 1], DG[:, t * P:(t + 1) * P], ones[:, 0:1], start=True, stop=True)
                    last.then_inc(s_d, 1)
                    for c, (a, b) in enumerate(CUTS):
                        if c >= 2:
                            pe.wait_ge(s_r, c - 1)
                        for t in range(a // P, b // P):
                            last = nc.tensor.transpose(tp[:, c % 2, t * P - a:(t + 1) * P - a], MX[:, t * P:(t + 1) * P], ident[:])
                        last.then_inc(s_t, 1)
                    pe.wait_ge(s_m, 1)
                    nc.tensor.transpose(pr[:, 0:P], dm[:], ident[:]).then_inc(s_mt, 1)

                @block.vector
                def _(dve):
                    link = Chain(dve, s_ch)
                    dve.wait_ge(s_d, 1)
                    nc.vector.tensor_copy(DEG[:], pd[:, 0:NT])
                    for c, (a, b) in enumerate(CUTS):
                        dve.wait_ge(s_t, c + 1)
                        last = nc.vector.tensor_reduce(mc[:, 0, a // P:b // P],
                                                       tp[:, c % 2, 0:b - a].rearrange("p (t d) -> p t d", d=P), AX.X, ALU.max)
                        last.then_inc(s_r, 1)
                    dve.wait_ge(s_r, len(CUTS))
                    link(nc.vector.scalar_tensor_tensor(mc[:, 1, :], mc[:, 0, :], mn[:, 0:1], sd[:], ALU.add, ALU.add))
                    link(nc.vector.scalar_tensor_tensor(mc[:, 2, :], mc[:, 1, :], 0.01, mc[:, 1, :], ALU.mult, ALU.max))
                    nc.vector.tensor_tensor(dm[:, 0:NT], sd[:], mc[:, 2, :], ALU.subtract)
                    nc.vector.scalar_tensor_tensor(dm[:, NT:2 * NT], sd[:], 0.01, mc[:, 2, :], ALU.mult,
                                                   ALU.subtract).then_inc(s_m, 1)
                    dve.wait_ge(s_mt, 1)
                    nc.vector.tensor_copy(dT[:], pr[:, 0:P]).then_inc(s_mc, 1)

                @block.sync
                def _(sp):
                    sp.wait_ge(s_mc, 1)
                    sp.dma_start(nodes_row.rearrange("a (t p) -> (a t) p", p=P), dT[:]).then_inc(s_b, 16)
                    sp.wait_ge(s_b, 16)
                    sp.dma_start(RB[:].rearrange("p a n -> p (a n)"),
                                 nodes_row.rearrange("a n -> (a n)").partition_broadcast(P)).then_inc(s_b, 16)
                    sp.wait_ge(s_b, 32)

            with ExitStack() as ctx:
                arb = ctx.enter_context(nc.sbuf_tensor("arb", [P, NT, 2, P], F32))
                ex = ctx.enter_context(nc.sbuf_tensor("ex", [P, 2, 13, P], F32))
                rx = ctx.enter_context(nc.sbuf_tensor("rx", [P, NT, P], F32))
                hw = ctx.enter_context(nc.sbuf_tensor("hw", [P, D], F32))
                tmp2 = ctx.enter_context(nc.sbuf_tensor("tmp2", [P, NT, P], F32))
                num = ctx.enter_context(nc.psum_tensor("num", [P, len(CUTS), BANK], F32))
                RBv = RB[:].rearrange("p a (q d) -> p a q d", q=NT)
                MXv = MX[:].rearrange("p (q d) -> p q d", q=NT)
                s_ld = [sem("w_load_a"), sem("w_load_b")]
                s_e = sem("w_exp")
                s_mx = sem("w_exp_max")
                s_ax = sem("w_edge_weights")
                s_rx = sem("w_relation_weights")
                s_dn = sem("w_denominators")
                s_mm = sem("w_products")
                s_w = sem("w_stationary")
                s_z = sem("w_zero")
                s_ago = sem("w_act_passed")
                blk = ExitStack()
                block = blk.enter_context(nc.Block())
                PIECES = []
                for h, (a, b) in enumerate(HALF):
                    lo_, hi_ = a * P, b * P
                    while lo_ < hi_:
                        e_ = min(hi_, (lo_ // BANK + 1) * BANK)
                        PIECES.append((h, lo_, e_))
                        lo_ = e_

                @block.sync
                def _(sp):
                    def load(s, h):
                        a, b = HALF[h]
                        sp.dma_start(arb[:, a:b, :, :].rearrange("p q a d -> p (q a d)"),
                                     arv[ds(s, 1), :, a:b, :].squeeze(0).rearrange("p q c -> p (q c)")).then_inc(s_ld[h], 16)
                    load(0, 0)
                    load(0, 1)
                    with sp.Fori(1, NT) as s:
                        for h in range(2):
                            sp.wait_ge(s_rx, s * 2 + h - 1)
                            sp.wait_ge(s_dn, s * 2 + h - 1)
                            load(s, h)

                @block.scalar
                def _(act):
                    def step(s, first):
                        for h, (a, b) in enumerate(HALF):
                            if not first:
                                act.wait_ge(s_rx, s * 2 + h - 1)
                                act.wait_ge(s_dn, s * 2 + h - 1)
                            act.sem_inc(s_ago, 1)
                            nc.scalar.activation(ex[:, h, 0:b - a, :], RBv[:, 0, a:b, :], ACT.Exp,
                                                 bias=ss[:, 0, ds(s, 1)]).then_inc(s_e, 1)
                            nc.scalar.activation(tmp2[:, a:b, :], RBv[:, 1, a:b, :], ACT.Exp,
                                                 bias=ss[:, 1, ds(s, 1)]).then_inc(s_e, 1)
                        if not first:
                            act.wait_ge(s_mm, s)
                        act.sem_inc(s_ago, 1)
                        nc.scalar.activation(hw[:], H[:, ds(s, 1), :].squeeze(1), ACT.Copy).then_inc(s_w, 1)
                    step(0, True)
                    with act.Fori(1, NT) as s:
                        step(s, False)

                @block.vector
                def _(dve):
                    nc.vector.memset(MX[:], 0.0).then_inc(s_z, 1)
                    def step(s, first):
                        for h, (a, b) in enumerate(HALF):
                            e = ex[:, h, 0:b - a, :]
                            dve.wait_ge(s_e, s * 4 + 2 * h + 2)
                            nc.vector.tensor_tensor(e, e, tmp2[:, a:b, :], ALU.max).then_inc(s_mx, 1)
                            dve.wait_ge(s_mx, s * 2 + h + 1)
                            dve.wait_ge(s_ld[h], s * 16 + 16)
                            if not first:
                                dve.wait_ge(s_mm, s)
                            nc.vector.scalar_tensor_tensor(tmp2[:, a:b, :], e, 2.0, arb[:, a:b, 0, :], ALU.min,
                                                           ALU.mult).then_inc(s_ax, 1)
                            nc.vector.scalar_tensor_tensor(rx[:, a:b, :], e, 2.0, arb[:, a:b, 1, :], ALU.min,
                                                           ALU.mult).then_inc(s_rx, 1)
                    step(0, True)
                    with dve.Fori(1, NT) as s:
                        step(s, False)

                @block.gpsimd
                def _(pool):
                    pool.wait_ge(s_z, 1)

                    def step(s, first):
                        for h, (a, b) in enumerate(HALF):
                            pool.wait_ge(s_ax, s * 2 + h + 1)
                            if not first:
                                pool.wait_ge(s_dn, s * 2 + h - 1)
                            nc.gpsimd.tensor_tensor(MXv[:, a:b, :], MXv[:, a:b, :], tmp2[:, a:b, :], ALU.add).then_inc(s_dn, 1)
                    step(0, True)
                    with pool.Fori(1, NT) as s:
                        step(s, False)

                @block.tensor
                def _(pe):
                    def step(s, first, final):
                        pe.wait_ge(s_w, s + 1)
                        seen = -1
                        for h, a, b in PIECES:
                            if h != seen:
                                pe.wait_ge(s_rx, s * 2 + h + 1)
                                seen = h
                            c = a // BANK
                            last = nc.tensor.matmul(num[:, c, a - c * BANK:b - c * BANK], hw[:],
                                                    rx[:].rearrange("p q d -> p (q d)")[:, a:b],
                                                    start=first, stop=final, skip_group_check=True)
                        last.then_inc(s_mm, 1)
                    step(0, True, False)
                    with pe.Fori(1, NT - 1) as s:
                        step(s, False, False)
                    step(NT - 1, False, True)

                blk.close()
                evacuate("w", num, DG)

            with ExitStack() as ctx:
                pden = ctx.enter_context(nc.psum_tensor("q_den", [P, BANK], F32))
                po = ctx.enter_context(nc.psum_tensor("q_po", [P, 2, BANK], F32))
                rden = ctx.enter_context(nc.sbuf_tensor("rden", [P, NT], F32))
                s_d = sem("q_denominators")
                s_ch = sem("q_chain")
                s_o = sem("q_out")
                s_x = sem("q_x")
                block = ctx.enter_context(nc.Block())

                @block.tensor
                def _(pe):
                    for t in range(NT):
                        last = nc.tensor.matmul(pden[:, t:t + 1], MX[:, t * P:(t + 1) * P], ones[:, 0:1], start=True, stop=True)
                    last.then_inc(s_d, 1)
                    for t in range(NT):
                        if t >= 2:
                            pe.wait_ge(s_x, t - 1)
                        nc.tensor.matmul(po[:, t % 2, 0:D], DG[:, t * P:(t + 1) * P], wl["W1"][:], start=True, stop=True).then_inc(s_o, 1)

                @block.vector
                def _(dve):
                    link = Chain(dve, s_ch)
                    dve.wait_ge(s_d, 1)
                    link(nc.vector.tensor_scalar(rden[:], pden[:, 0:NT], 1e-30, None, ALU.max))
                    link(nc.vector.reciprocal(rden[:], rden[:]))
                    for t in range(NT):
                        dve.wait_ge(s_o, t + 1)
                        nc.vector.scalar_tensor_tensor(X[:, t, :], po[:, t % 2, 0:D], rden[:, t:t + 1], X[:, t, :],
                                                       ALU.mult, ALU.add).then_inc(s_x, 1)

        layernorm(2)

        def gather_product(tag, scale, AGT):
            with ExitStack() as ctx:
                R = 5
                ab = ctx.enter_context(nc.sbuf_tensor("ab" + tag, [P, R, NT, P], F32))
                hw = ctx.enter_context(nc.sbuf_tensor("hw" + tag, [P, R, D], F32))
                num = ctx.enter_context(nc.psum_tensor("num" + tag, [P, len(CUTS), BANK], F32))
                s_ld = [sem("g_load%d_" % r + tag) for r in range(R)]
                s_w = sem("g_stationary" + tag)
                s_mm = sem("g_products" + tag)
                s_on = sem("g_begun" + tag)
                assert NT % R == 0

                with nc.Block() as block:
                    @block.sync
                    def _(sp):
                        def load(s, r):
                            sp.dma_start(ab[:, r, :, :], arv[ds(s, 1), :, :, 0:P].squeeze(0)).then_inc(s_ld[r], 16)
                        for r in range(R):
                            load(r, r)
                        with sp.Fori(1, NT // R) as i:
                            for r in range(R):
                                sp.wait_ge(s_mm, (i - 1) * R + r + 1)
                                load(i * R + r, r)

                    @block.scalar
                    def _(act):
                        def step(i, first):
                            for r in range(R):
                                if not first:
                                    act.wait_ge(s_mm, (i - 1) * R + r + 1)
                                act.sem_inc(s_on, 1)
                                src = H[:, ds(i * R + r, 1), :].squeeze(1)
                                nc.scalar.activation(hw[:, r, :], src, ACT.Copy,
                                                     scale=1.0 if scale is None else scale[:, ds(i * R + r, 1)]).then_inc(s_w, 1)
                        step(0, True)
                        with act.Fori(1, NT // R) as i:
                            step(i, False)

                    @block.tensor
                    def _(pe):
                        def step(i, first, final):
                            for r in range(R):
                                pe.wait_ge(s_w, i * R + r + 1)
                                pe.wait_ge(s_ld[r], i * 16 + 16)
                                for c, (a, b) in enumerate(CUTS):
                                    last = nc.tensor.matmul(num[:, c, 0:b - a], hw[:, r, :],
                                                            ab[:, r, :, :].rearrange("p q d -> p (q d)")[:, a:b],
                                                            start=first and r == 0, stop=final and r == R - 1,
                                                            skip_group_check=True)
                                last.then_inc(s_mm, 1)
                        step(0, True, False)
                        with pe.Fori(1, NT // R - 1) as i:
                            step(i, False, False)
                        step(NT // R - 1, False, True)
                evacuate(tag, num, AGT)

        with ExitStack() as lay:
            AGT = lay.enter_context(nc.sbuf_tensor("AGT", [P, NP], F32))
            dinv = lay.enter_context(nc.sbuf_tensor("dinv", [P, 3, NT], F32))
            bbc = lay.enter_context(nc.sbuf_tensor("bbc", [P, D], F32))
            with ExitStack() as ctx:
                s_ch = sem("d_chain")
                s_a = sem("d_root")
                s_l = sem("d_bias")
                block = ctx.enter_context(nc.Block())

                @block.vector
                def _(dve):
                    link = Chain(dve, s_ch)
                    link(nc.vector.tensor_scalar(dinv[:, 2, :], DEG[:], 1.0, None, ALU.add))
                    link(nc.vector.reciprocal(dinv[:, 1, :], dinv[:, 2, :]))
                    dve.wait_ge(s_a, 1)
                    nc.vector.reciprocal(dinv[:, 0, :], dinv[:, 2, :])

                @block.scalar
                def _(act):
                    act.wait_ge(s_ch, 2)
                    nc.scalar.activation(dinv[:, 2, :], dinv[:, 2, :], ACT.Sqrt).then_inc(s_a, 1)

                @block.sync
                def _(sp):
                    sp.dma_start(bbc[:], bb2.partition_broadcast(P)).then_inc(s_l, 16)
                    sp.wait_ge(s_l, 16)

            gather_product("2", dinv[:, 0, :], AGT)
            with ExitStack() as ctx:
                Z = ctx.enter_context(nc.sbuf_tensor("Z", [P, NT, D], F32))
                Y = ctx.enter_context(nc.sbuf_tensor("Y", [P, 2, D], F32))
                Q = ctx.enter_context(nc.sbuf_tensor("Q", [P, NT, D], F32))
                pa = ctx.enter_context(nc.psum_tensor("pa2", [P, 2, BANK], F32))
                pb = ctx.enter_context(nc.psum_tensor("pb2", [P, 2, BANK], F32))
                s_p = sem("c_products")
                s_y = sem("c_self")
                s_z = sem("c_sum")
                s_e = sem("c_exp")
                s_zb = sem("c_bias")
                s_zm = sem("c_clamped")
                s_ch = sem("c_chain")
                block = ctx.enter_context(nc.Block())

                @block.tensor
                def _(pe):
                    for t in range(NT):
                        if t >= 2:
                            pe.wait_ge(s_z, t - 1)
                        nc.tensor.matmul(pb[:, t % 2, 0:D], HT[:, t * P:(t + 1) * P], wl["W2"][:], start=True, stop=True)
                        nc.tensor.matmul(pa[:, t % 2, 0:D], AGT[:, t * P:(t + 1) * P], wl["W2"][:], start=True,
                                         stop=True).then_inc(s_p, 1)

                @block.scalar
                def _(act):
                    for t in range(NT):
                        act.wait_ge(s_p, t + 1)
                        if t >= 2:
                            act.wait_ge(s_z, t - 1)
                        nc.scalar.activation(Y[:, t % 2, :], pb[:, t % 2, 0:D], ACT.Copy, scale=dinv[:, 1, t:t + 1]).then_inc(s_y, 1)
                    act.wait_ge(s_zm, 1)
                    nc.scalar.activation(Q[:], Q[:], ACT.Exp).then_inc(s_e, 1)

                @block.vector
                def _(dve):
                    link = Chain(dve, s_ch)
                    for t in range(NT):
                        dve.wait_ge(s_y, t + 1)
                        nc.vector.scalar_tensor_tensor(Z[:, t, :], pa[:, t % 2, 0:D], dinv[:, 0, t:t + 1], Y[:, t % 2, :],
                                                       ALU.mult, ALU.add).then_inc(s_z, 1)
                    dve.wait_ge(s_z, NT)
                    link(nc.vector.tensor_tensor(Z[:], Z[:], bbc[:].unsqueeze(1).to_broadcast([P, NT, D]), ALU.add))
                    nc.vector.tensor_scalar(Q[:], Z[:], 20.0, None, ALU.min).then_inc(s_zm, 1)
                    dve.wait_ge(s_e, 1)
                    link(nc.vector.scalar_tensor_tensor(Q[:], Q[:], 2.0, Q[:], ALU.add, ALU.mult))
                    link(nc.vector.tensor_tensor(Z[:], Z[:], Q[:], ALU.mult))
                    link(nc.vector.tensor_scalar(Q[:], Q[:], 2.0, None, ALU.add))
                    link(nc.vector.reciprocal(Q[:], Q[:]))
                    link(nc.vector.tensor_tensor(Z[:], Z[:], Q[:], ALU.mult))
                    nc.vector.tensor_tensor(X[:], X[:], Z[:], ALU.add)

            layernorm(3)
            gather_product("3", None, AGT)
            with ExitStack() as ctx:
                Y = ctx.enter_context(nc.sbuf_tensor("Y3", [P, 2, D], F32))
                Z = ctx.enter_context(nc.sbuf_tensor("Z3", [P, 2, D], F32))
                rdeg = ctx.enter_context(nc.sbuf_tensor("rdeg", [P, NT], F32))
                pa = ctx.enter_context(nc.psum_tensor("pa3", [P, 2, BANK], F32))
                pb = ctx.enter_context(nc.psum_tensor("pb3", [P, 2, BANK], F32))
                s_ch = sem("f_chain")
                s_r = sem("f_degree")
                s_p = sem("f_products")
                s_y = sem("f_neighbours")
                s_z = sem("f_sum")
                s_x = sem("f_x")
                s_out = sem("f_out")
                block = ctx.enter_context(nc.Block())

                @block.tensor
                def _(pe):
                    for t in range(NT):
                        if t >= 2:
                            pe.wait_ge(s_z, t - 1)
                        nc.tensor.matmul(pb[:, t % 2, 0:D], AGT[:, t * P:(t + 1) * P], wl["WnT"][:], start=True, stop=True)
                        nc.tensor.matmul(pa[:, t % 2, 0:D], HT[:, t * P:(t + 1) * P], wl["WsT"][:], start=True, stop=False)
                        nc.tensor.matmul(pa[:, t % 2, 0:D], ones[0:1, :], brow["bs"][:], start=False, stop=False)
                        nc.tensor.matmul(pa[:, t % 2, 0:D], ones[0:1, :], brow["bn"][:], start=False, stop=True).then_inc(s_p, 1)

                @block.scalar
                def _(act):
                    act.wait_ge(s_r, 1)
                    for t in range(NT):
                        act.wait_ge(s_p, t + 1)
                        if t >= 2:
                            act.wait_ge(s_z, t - 1)
                        nc.scalar.activation(Y[:, t % 2, :], pb[:, t % 2, 0:D], ACT.Copy, scale=rdeg[:, t:t + 1]).then_inc(s_y, 1)

                @block.vector
                def _(dve):
                    link = Chain(dve, s_ch)
                    link(nc.vector.tensor_scalar(rdeg[:], DEG[:], 1.0, None, ALU.max))
                    nc.vector.reciprocal(rdeg[:], rdeg[:]).then_inc(s_r, 1)
                    for t in range(NT):
                        dve.wait_ge(s_y, t + 1)
                        nc.vector.tensor_tensor(Z[:, t % 2, :], pa[:, t % 2, 0:D], Y[:, t % 2, :], ALU.add).then_inc(s_z, 1)
                        dve.wait_ge(s_z, t + 1)
                        nc.vector.scalar_tensor_tensor(X[:, t, :], Z[:, t % 2, :], 0.0, X[:, t, :], ALU.max,
                                                       ALU.add).then_inc(s_x, 1)

                @block.sync
                def _(sp):
                    for a in range(0, NT - 1, 6):
                        b = min(a + 6, NT - 1)
                        sp.wait_ge(s_x, b)
                        sp.dma_start(out[a * P:b * P, :].rearrange("(t p) d -> p t d", p=P), X[:, a:b, :]).then_inc(s_out, 16)
                    sp.wait_ge(s_x, NT)
                    sp.dma_start(out[(NT - 1) * P:N, :], X[0:NR, NT - 1, :]).then_inc(s_out, 16)
                    sp.wait_ge(s_out, 16 * 5)


_INS = ["x", "src", "dst", "edge_attr_64", "edge_type_100", "L0_gnn_msg_w1", "L0_gnn_msg_b1", "L0_gnn_msg_w2",
        "L0_gnn_msg_b2", "L0_gnn_upd_w1", "L0_gnn_upd_b1", "L0_gnn_upd_w2", "L0_gnn_upd_b2", "L1_gnn_W", "L1_gnn_attn",
        "L1_gnn_rel_emb", "L2_gnn_W", "L2_gnn_b", "L3_gnn_W_self", "L3_gnn_b_self", "L3_gnn_W_neigh", "L3_gnn_b_neigh"]


def kernel(**inputs):
    import numpy as _np
    import concourse.bacc as _bacc
    from concourse import mybir as _mybir
    from concourse.bass_utils import run_bass_kernel_spmd as _run

    nc = _bacc.Bacc("TRN2", target_bir_lowering=False, num_devices=1)
    arrays, args = {}, []
    for name in _INS:
        a = _np.ascontiguousarray(inputs[name])
        arrays[f"in_{name}_dram"] = a
        args.append(nc.dram_tensor(f"in_{name}_dram", a.shape, _mybir.dt.from_np(a.dtype), kind="ExternalInput").ap())
    args.append(nc.dram_tensor("out_0_dram", (N, D), _mybir.dt.float32, kind="ExternalOutput").ap())
    build(nc, *args)
    r = _run(nc, [arrays], core_ids=[0])
    return r.results[0]["out_0_dram"]
```

```python
from contextlib import ExitStack

import concourse.bass as bass
from concourse import mybir

F32 = mybir.dt.float32
F16 = mybir.dt.float16
BF16 = mybir.dt.bfloat16
I32 = mybir.dt.int32
ALU = mybir.AluOpType
ACT = mybir.ActivationFunctionType
AX = mybir.AxisListType
ds = bass.ds

P = 128
D = 128
N = 3125
NT = -(-N // P)
NP = NT * P
NR = N - (NT - 1) * P
ED = 64
E = 103125
EC = -(-E // P)
ER = E - (P - 1) * EC
NREL = 100
BINS = NT * NT
ROW = D + 4
CH = 13
NCH = EC // CH
assert EC % (2 * CH) == 0
G = 4
RING = 4
LOOPS = -(-(EC + BINS + NT * (G - 1)) // (G * RING))
TT = LOOPS * RING * G
TCOL = -(-TT // P)
DUMMY = NT * P * NT
EPS = 1e-5
BANK = 512
CUTS = [(a, min(a + BANK, NP)) for a in range(0, NP, BANK)]
INTERNAL = "Internal"


def back(i, k, n):
    return (i + (k - n) // RING if (k - n) // RING else i), (k - n) % RING


def loads(nc, engine, ap, top):
    return nc.values_load_multi_w_load_instructions(
        ap, engines=[engine], min_val=0, max_val=top,
        skip_runtime_bounds_check_because="the table counts bins: its values are in range by construction")[1]


class Chain:

    def __init__(self, eng, sem):
        self.eng, self.sem, self.count = eng, sem, 0

    def __call__(self, ins):
        ins.then_inc(self.sem, 1)
        self.count += 1
        self.eng.wait_ge(self.sem, self.count)


def build(nc, x, src, dst, ea, et, w1, b1, w2, b2, u1, c1, u2, c2,
          W1, attn, rel, W2, bb2, Ws, bs, Wn, bn, out):
    sortd = nc.dram_tensor("sorted_rows", [TT * P, ROW], F32, kind=INTERNAL).ap()
    ar = nc.dram_tensor("count_matrices", [(NT + 1) * P * NT, 2 * P], F32, kind=INTERNAL).ap()
    rows1 = nc.dram_tensor("row_a", [2, BINS], F32, kind=INTERNAL).ap()
    rowinc = nc.dram_tensor("row_inc", [BINS], F32, kind=INTERNAL).ap()
    nodes_row = nc.dram_tensor("node_rows", [2, NP], F32, kind=INTERNAL).ap()

    with ExitStack() as top:
        def tsb(name, shape, dt=F32):
            return top.enter_context(nc.sbuf_tensor(name, shape, dt))

        def sem(name):
            return top.enter_context(nc.semaphore(name))

        X = tsb("X", [P, NT, D])
        H = tsb("H", [P, NT, D])
        HT = tsb("HT", [P, NP])
        ident = tsb("ident", [P, P])
        iota128 = tsb("iota128", [P, P])
        stats = tsb("stats", [P, NT, 6])
        mv = tsb("mv", [P, NT, 2])
        rstd = tsb("rstd", [P, NT])
        nbias = tsb("nbias", [P, NT])
        eps = tsb("eps", [P, 1])
        ones = tsb("ones", [P, P])
        DEG = tsb("DEG", [P, NT])
        ZR = 8
        zrow = tsb("zrow", [P, ZR, ROW])
        s_zd = sem("rows_cleared")
        wl = {}
        for name in ("w1a", "w2", "u1a", "u1b", "u2", "W1", "W2", "WsT", "WnT"):
            wl[name] = tsb("sb_" + name, [P, P])
        w1b = tsb("sb_w1b", [ED, D])
        brow = {}
        for name in ("b1", "b2", "c2", "bs", "bn", "bb2"):
            brow[name] = tsb("row_" + name, [1, D])
        c1col = tsb("c1col", [P, 1])

        mid = ExitStack()

        def msb(name, shape, dt=F32):
            return mid.enter_context(nc.sbuf_tensor(name, shape, dt))

        table = msb("table", [P, 4, TCOL])
        tilei = msb("tilei", [1, 3, TT], I32)
        keep = msb("keep", [P, TT])
        S = msb("S", [P, NT + 1, D + 1])

        s_ln = {name: sem("ln_" + name) for name in ("stats", "root", "h", "turned", "copied", "chain")}
        NQ = -(-NT // 4)

        def layernorm(r):
            with ExitStack() as ctx:
                tp = ctx.enter_context(nc.psum_tensor("ln_tp%d" % r, [P, 2, BANK], F32))
                block = ctx.enter_context(nc.Block())

                @block.vector
                def _(dve):
                    link = Chain(dve, s_ln["chain"])
                    link.count = 2 * r
                    for t in range(NT):
                        last = nc.vector.bn_stats(stats[:, t, :], X[:, t, :])
                    link(last)
                    for t in range(NT):
                        last = nc.vector.bn_aggr(mv[:, t, :], stats[:, t, :])
                    last.then_inc(s_ln["stats"], 1)
                    dve.wait_ge(s_ln["root"], r + 1)
                    link(nc.vector.reciprocal(rstd[:], rstd[:]))
                    nc.vector.scalar_tensor_tensor(nbias[:], mv[:, :, 0], -1.0, rstd[:],
                                                   ALU.mult, ALU.mult).then_inc(s_ln["stats"], 1)
                    for g in range(NQ):
                        k = min(4, NT - 4 * g)
                        dve.wait_ge(s_ln["turned"], r * NQ + g + 1)
                        nc.vector.tensor_copy(HT[:, 4 * g * P:(4 * g + k) * P], tp[:, g % 2, 0:k * P]).then_inc(s_ln["copied"], 1)

                @block.scalar
                def _(act):
                    act.wait_ge(s_ln["stats"], 2 * r + 1)
                    nc.scalar.activation(rstd[:], mv[:, :, 1], ACT.Sqrt, bias=eps[:, 0:1]).then_inc(s_ln["root"], 1)
                    act.wait_ge(s_ln["stats"], 2 * r + 2)
                    for t in range(NT):
                        nc.scalar.activation(H[:, t, :], X[:, t, :], ACT.Relu, bias=nbias[:, t:t + 1],
                                             scale=rstd[:, t:t + 1]).then_inc(s_ln["h"], 1)

                @block.tensor
                def _(pe):
                    for t in range(NT):
                        pe.wait_ge(s_ln["h"], r * NT + t + 1)
                        if t % 4 == 0 and t >= 8:
                            pe.wait_ge(s_ln["copied"], r * NQ + t // 4 - 1)
                        last = nc.tensor.transpose(tp[:, t // 4 % 2, (t % 4) * P:(t % 4 + 1) * P], H[:, t, :], ident[:])
                        if t % 4 == 3 or t == NT - 1:
                            last.then_inc(s_ln["turned"], 1)

        def evacuate(tag, num, AGT):
            with nc.Block() as block:
                @block.vector
                def _(dve):
                    for c, (a, b) in enumerate(CUTS[0::2]):
                        nc.vector.tensor_copy(AGT[:, a:b], num[:, 2 * c, 0:b - a])

                @block.scalar
                def _(act):
                    for c, (a, b) in enumerate(CUTS[1::2]):
                        nc.scalar.activation(AGT[:, a:b], num[:, 2 * c + 1, 0:b - a], ACT.Copy)

        with ExitStack() as ctx:
            s_z = sem("zero_row")
            wraw = [ctx.enter_context(nc.sbuf_tensor("wraw%d" % k, [P, P], F32)) for k in range(2)]
            tp = ctx.enter_context(nc.psum_tensor("ld_tp", [P, 2, BANK], F32))
            s_ld = sem("loads")
            s_ms = sem("memsets")
            s_x = sem("x_padding")
            s_id = sem("identity")
            s_t = sem("w_transposed")
            block = ctx.enter_context(nc.Block())

            @block.sync
            def _(sp):
                sp.wait_ge(s_x, 1)
                sp.dma_start(X[:, 0:NT - 1, :], x[0:(NT - 1) * P, :].rearrange("(t p) d -> p t d", p=P)).then_inc(s_ld, 16)
                sp.dma_start(X[0:NR, NT - 1, :], x[(NT - 1) * P:N, :]).then_inc(s_ld, 16)
                for to, fr in ((wl["w1a"], w1[0:P, :]), (wl["w2"], w2), (wl["u1a"], u1[0:P, :]),
                               (wl["u1b"], u1[P:2 * P, :]), (wl["u2"], u2), (wl["W1"], W1), (wl["W2"], W2),
                               (wraw[0], Ws), (wraw[1], Wn), (w1b, w1[P:P + ED, :])):
                    sp.dma_start(to[:], fr).then_inc(s_ld, 16)
                for name, fr in (("b1", b1), ("b2", b2), ("c2", c2), ("bs", bs), ("bn", bn), ("bb2", bb2)):
                    sp.dma_start(brow[name][:], fr.rearrange("(a d) -> a d", a=1)).then_inc(s_ld, 16)
                sp.dma_start(c1col[:], c1.rearrange("(d a) -> d a", a=1)).then_inc(s_ld, 16)
                sp.wait_ge(s_ld, 16 * 19)

            @block.gpsimd
            def _(pool):
                nc.gpsimd.memset(zrow[:], 0.0).then_inc(s_z, 1)
                pool.wait_ge(s_z, 1)
                nc.gpsimd.memset(zrow[:, :, D:D + 2], -1.0).then_inc(s_z, 1)
                nc.gpsimd.iota(iota128[:], pattern=[[1, P]], base=0, channel_multiplier=0,
                               allow_small_or_imprecise_dtypes=True)
                nc.gpsimd.memset(ident[:], 0.0).then_inc(s_ms, 1)
                pool.wait_ge(s_ms, 1)
                nc.gpsimd.affine_select(out=ident[:], in_=ident[:], compare_op=ALU.not_equal, fill=1.0, base=0,
                                        pattern=[[-1, P]], channel_multiplier=1).then_inc(s_id, 1)

            @block.vector
            def _(dve):
                nc.vector.memset(X[:], 0.0).then_inc(s_x, 1)
                nc.vector.memset(eps[:], EPS)
                nc.vector.memset(ones[:], 1.0)
                nc.vector.memset(S[:], 0.0)
                for k, name in enumerate(("WsT", "WnT")):
                    dve.wait_ge(s_t, k + 1)
                    nc.vector.tensor_copy(wl[name][:], tp[:, k, 0:P])

            @block.tensor
            def _(pe):
                pe.wait_ge(s_id, 1)
                pe.wait_ge(s_ld, 16 * 19)
                for k in range(2):
                    nc.tensor.transpose(tp[:, k, 0:P], wraw[k][:], ident[:]).then_inc(s_t, 1)

        layernorm(0)

        with ExitStack() as srt:
            def sb(name, shape, dt=F32):
                return srt.enter_context(nc.sbuf_tensor(name, shape, dt))

            raw = sb("raw", [P, 3, EC], I32)
            hi = sb("hi", [P, 2, EC], I32)
            lo = sb("lo", [P, 3, EC])
            tile = sb("tile", [P, 2, EC])
            binf = sb("binf", [P, EC])
            iota25 = sb("iota25", [P, NT])
            iota625 = sb("iota625", [P, BINS], F16)
            tri = sb("tri", [P, P], F16)
            ntri = sb("ntri", [P, P], F16)
            typ = sb("typ", [P, EC])
            relt = sb("relt", [P, NREL])
            iotar = sb("iotar", [P, NREL])
            starts = sb("starts", [1, 2, BINS])
            incb = sb("incb", [P, BINS])

            with ExitStack() as ctx:
                SUB = 62
                ohd = ctx.enter_context(nc.sbuf_tensor("ohd", [P, 2, SUB, NT], F16))
                ohs = ctx.enter_context(nc.sbuf_tensor("ohs", [P, 2, SUB, NT], F16))
                hist = ctx.enter_context(nc.psum_tensor("hist", [NT, 2, BANK], F32))
                triF = ctx.enter_context(nc.sbuf_tensor("triF", [P, P], F32))
                cnt = ctx.enter_context(nc.sbuf_tensor("cnt", [NT, 8, NT], F32))
                cnti = ctx.enter_context(nc.sbuf_tensor("cnti", [NT, 2, NT], I32))
                pre = ctx.enter_context(nc.psum_tensor("pre", [NT, BANK], F32))
                dcol = ctx.enter_context(nc.sbuf_tensor("dcol", [P, 1], I32))
                dcolf = ctx.enter_context(nc.sbuf_tensor("dcolf", [P, 1], F32))
                WC = 2 * CH
                jw = ctx.enter_context(nc.sbuf_tensor("jw", [P, WC, NREL], F32))
                tw = ctx.enter_context(nc.sbuf_tensor("tw", [P, 2, WC], F32))
                kidx = ctx.enter_context(nc.sbuf_tensor("kidx", [P, 3, TCOL], F32))
                junk = ctx.enter_context(nc.sbuf_tensor("junk", [P, BINS], F32))
                junk4 = ctx.enter_context(nc.sbuf_tensor("junk4", [P, 4, BINS], F32))
                assert TCOL % 4 == 0
                edges = ctx.enter_context(nc.sbuf_tensor("edges", [P, NT], F32))
                s_ms = sem("h_memset")
                s_ld = sem("h_load")
                s_ch = sem("h_chain")
                s_oh = sem("h_onehot")
                s_mm = sem("h_counted")
                s_con = sem("h_const")
                s_w = sem("h_weights")
                s_pc = sem("h_pool_chain")
                s_rt = sem("h_row_totals")
                s_pre = sem("h_prefix")
                s_st = sem("h_starts")
                s_bo = sem("h_bounce")
                s_tb = sem("h_tables")
                block = ctx.enter_context(nc.Block())

                @block.sync
                def _(sp):
                    sp.wait_ge(s_ms, 1)
                    for k, a in enumerate((dst, src, et)):
                        sp.dma_start(raw[0:P - 1, k, :], a[0:(P - 1) * EC].rearrange("(p c) -> p c", c=EC)).then_inc(s_ld, 16)
                        sp.dma_start(raw[P - 1:P, k, 0:ER], a[(P - 1) * EC:E].rearrange("(p c) -> p c", p=1)).then_inc(s_ld, 16)
                    sp.dma_start(relt[:], rel.rearrange("r a -> a r").partition_broadcast(P).rearrange("p a r -> p (a r)")).then_inc(s_ld, 16)
                    sp.wait_ge(s_st, 1)
                    sp.dma_start(rows1[0].rearrange("(a b) -> a b", a=NT), cnt[:, 4, :]).then_inc(s_bo, 16)
                    sp.dma_start(rows1[1].rearrange("(a b) -> a b", a=NT), cnt[:, 5, :]).then_inc(s_bo, 16)
                    sp.dma_start(rowinc.rearrange("(a b) -> a b", a=NT), cnt[:, 6, :]).then_inc(s_bo, 16)
                    sp.wait_ge(s_bo, 48)
                    sp.dma_start(starts[0:1, :, :].rearrange("a b c -> a (b c)"), rows1.rearrange("a b -> (a b)").unsqueeze(0)).then_inc(s_bo, 16)
                    sp.dma_start(incb[:], rowinc.partition_broadcast(P)).then_inc(s_bo, 16)
                    sp.wait_ge(s_bo, 80)

                @block.scalar
                def _(act):
                    act.wait_ge(s_ld, 16 * 7)
                    sv = sortd.rearrange("(n p k) w -> n p (k w)", p=P, k=ZR)
                    with act.Fori(0, TT // ZR) as n:
                        act.dma_start(sv[ds(n, 1)].squeeze(0), zrow[:].rearrange("p k w -> p (k w)")).then_inc(s_zd, 16)

                @block.gpsimd
                def _(pool):
                    nc.gpsimd.iota(iota25[:], pattern=[[1, NT]], base=0, channel_multiplier=0,
                                   allow_small_or_imprecise_dtypes=True).then_inc(s_con, 1)
                    nc.gpsimd.iota(iota625[:], pattern=[[1, BINS]], base=0, channel_multiplier=0,
                                   allow_small_or_imprecise_dtypes=True).then_inc(s_con, 1)
                    nc.gpsimd.iota(iotar[:], pattern=[[1, NREL]], base=0, channel_multiplier=0,
                                   allow_small_or_imprecise_dtypes=True).then_inc(s_con, 1)
                    nc.gpsimd.iota(edges[:], pattern=[[NT, NT]], base=NT, channel_multiplier=0,
                                   allow_small_or_imprecise_dtypes=True).then_inc(s_con, 1)
                    for k in range(3):
                        nc.gpsimd.iota(kidx[:, k, :], pattern=[[P, TCOL]], base=k - 1, channel_multiplier=1,
                                       allow_small_or_imprecise_dtypes=True).then_inc(s_con, 1)
                    nc.gpsimd.iota(dcol[:], pattern=[[0, 1]], base=0, channel_multiplier=1).then_inc(s_con, 1)
                    nc.gpsimd.memset(triF[:], 1.0).then_inc(s_pc, 1)
                    pool.wait_ge(s_pc, 1)
                    nc.gpsimd.affine_select(out=triF[:], in_=triF[:], compare_op=ALU.is_gt, fill=0.0, base=0,
                                            pattern=[[1, P]], channel_multiplier=-1).then_inc(s_pc, 1)
                    pool.wait_ge(s_pc, 2)
                    nc.gpsimd.tensor_copy(tri[:], triF[:]).then_inc(s_con, 1)
                    nc.gpsimd.tensor_scalar(ntri[:], triF[:], -1.0, 1.0, ALU.mult, ALU.add).then_inc(s_con, 1)

                @block.vector
                def _(dve):
                    link = Chain(dve, s_ch)
                    link(nc.vector.memset(raw[:, 2, :], 0))
                    nc.vector.memset(raw[:, 0:2, :], NP - 1).then_inc(s_ms, 1)
                    dve.wait_ge(s_ld, 16 * 7)
                    nc.vector.tensor_single_scalar(hi[:], raw[:, 0:2, :], 7, ALU.logical_shift_right)
                    nc.vector.memset(relt[:, 0:1], 0.0)
                    link(nc.vector.tensor_copy(typ[:], raw[:, 2, :]))
                    link(nc.vector.tensor_single_scalar(raw[:, 0:2, :], raw[:, 0:2, :], P - 1, ALU.bitwise_and))
                    nc.vector.tensor_copy(lo[:, 0:2, :], raw[:, 0:2, :])
                    link(nc.vector.tensor_copy(tile[:], hi[:]))
                    link(nc.vector.scalar_tensor_tensor(binf[:], tile[:, 1, :], float(NT), tile[:, 0, :], ALU.mult, ALU.add))
                    dve.wait_ge(s_con, 10)
                    for n in range(EC // SUB):
                        if n >= 2:
                            dve.wait_ge(s_mm, n - 1)
                        c = slice(n * SUB, (n + 1) * SUB)
                        for k, oh in ((0, ohd), (1, ohs)):
                            ins = nc.vector.tensor_tensor(
                                oh[:, n % 2, :, :], iota25[:].unsqueeze(1).to_broadcast([P, SUB, NT]),
                                tile[:, k, c].unsqueeze(2).to_broadcast([P, SUB, NT]), ALU.is_equal)
                        ins.then_inc(s_oh, 1)
                    dve.wait_ge(s_mm, EC // SUB)
                    link(nc.vector.tensor_copy(cnt[:, 0:2, :], hist[:, :, 0:NT]))
                    link(nc.vector.tensor_tensor(cnt[:, 2, :], cnt[:, 0, :], cnt[:, 1, :], ALU.add))
                    link(nc.vector.tensor_scalar(cnt[:, 2, :], cnt[:, 2, :], float(P - 1), float(P), ALU.add, ALU.max))
                    link(nc.vector.tensor_copy(cnti[:, 0, :], cnt[:, 2, :]))
                    link(nc.vector.tensor_single_scalar(cnti[:, 1, :], cnti[:, 0, :], 7, ALU.logical_shift_right))
                    link(nc.vector.tensor_copy(cnt[:, 2, :], cnti[:, 1, :]))
                    link(nc.vector.tensor_tensor_scan(cnt[:, 3, :], ones[0:NT, 0:NT], cnt[:, 2, :], 0.0, ALU.mult, ALU.add))
                    link(nc.vector.tensor_scalar(cnt[:, 7, 2:3], cnt[:, 3, NT - 1:NT], float(G - 1), None, ALU.add))
                    link(nc.vector.tensor_copy(cnti[:, 0, 0:1], cnt[:, 7, 2:3]))
                    link(nc.vector.tensor_single_scalar(cnti[:, 1, 0:1], cnti[:, 0, 0:1], -G, ALU.bitwise_and))
                    nc.vector.tensor_copy(cnt[:, 7, 0:1], cnti[:, 1, 0:1]).then_inc(s_rt, 1)
                    dve.wait_ge(s_pre, 1)
                    link(nc.vector.tensor_copy(cnt[:, 7, 1:2], pre[:, 0:1]))
                    link(nc.vector.tensor_scalar(cnt[:, 6, :], cnt[:, 3, :], cnt[:, 7, 1:2], None, ALU.add))
                    link(nc.vector.tensor_tensor(cnt[:, 3, :], cnt[:, 6, :], cnt[:, 2, :], ALU.subtract))
                    link(nc.vector.tensor_scalar(cnt[:, 4, :], cnt[:, 3, :], float(P), None, ALU.mult))
                    link(nc.vector.tensor_tensor(cnt[:, 6, NT - 1:NT], cnt[:, 7, 0:1], cnt[:, 7, 1:2], ALU.add))
                    nc.vector.tensor_tensor(cnt[:, 5, :], cnt[:, 4, :], cnt[:, 0, :], ALU.add).then_inc(s_st, 1)
                    with dve.Fori(0, EC // WC) as i:
                        nc.vector.tensor_copy(tw[:, 0, :], typ[:, ds(i * WC, WC)]).then_inc(s_w, 1)
                        dve.wait_ge(s_w, i * 3 + 1)
                        for c in range(WC):
                            last = nc.vector.scalar_tensor_tensor(jw[:, c, :], iotar[:], tw[:, 0, c:c + 1], relt[:],
                                                                  ALU.is_equal, ALU.mult, accum_out=tw[:, 1, c:c + 1])
                        last.then_inc(s_w, 1)
                        dve.wait_ge(s_w, i * 3 + 2)
                        nc.vector.tensor_copy(lo[:, 2, ds(i * WC, WC)], tw[:, 1, :]).then_inc(s_w, 1)
                        dve.wait_ge(s_w, i * 3 + 3)
                    dve.wait_ge(s_bo, 80)
                    for k in range(3):
                        for j in range(TCOL):
                            ins = nc.vector.tensor_scalar(junk4[:, j % 4, :], incb[:], kidx[:, k, j:j + 1], None, ALU.is_le,
                                                          ALU.add, accum_out=table[:, k, j:j + 1])
                            if j % 4 == 3:
                                link(ins)
                    link(nc.vector.tensor_tensor(table[:, 0, :], table[:, 0, :], table[:, 1, :], ALU.is_equal))
                    link(nc.vector.tensor_tensor(table[:, 2, :], table[:, 2, :], table[:, 1, :], ALU.is_equal))
                    for j in range(TCOL):
                        ins = nc.vector.tensor_scalar(junk4[:, 0, j * NT:(j + 1) * NT], edges[:], table[:, 1, j:j + 1], None,
                                                      ALU.is_le, ALU.add, accum_out=table[:, 3, j:j + 1])
                    link(ins)
                    link(nc.vector.scalar_tensor_tensor(table[:, 1, :], table[:, 3, :], -float(NT), table[:, 1, :],
                                                        ALU.mult, ALU.add))
                    link(nc.vector.scalar_tensor_tensor(junk[:, 0:TCOL], table[:, 3, :], float(P * NT), table[:, 1, :],
                                                        ALU.mult, ALU.add))
                    link(nc.vector.tensor_single_scalar(dcol[:, 0:1], dcol[:, 0:1], 2 * G - 1, ALU.bitwise_and))
                    link(nc.vector.tensor_scalar(dcolf[:], dcol[:], float(DUMMY), None, ALU.add))
                    link(nc.vector.tensor_scalar(junk[:, TCOL:2 * TCOL], junk[:, 0:TCOL], dcolf[:, 0:1], -1.0,
                                                 ALU.subtract, ALU.mult))
                    link(nc.vector.tensor_tensor(junk[:, TCOL:2 * TCOL], junk[:, TCOL:2 * TCOL], table[:, 2, :], ALU.mult))
                    nc.vector.tensor_tensor(table[:, 2, :], junk[:, 0:TCOL], junk[:, TCOL:2 * TCOL], ALU.add).then_inc(s_tb, 1)

                @block.tensor
                def _(pe):
                    for n in range(EC // SUB):
                        pe.wait_ge(s_oh, n + 1)
                        for c in range(SUB):
                            a = n * SUB + c
                            last = nc.tensor.matmul(hist[:, a % 2, 0:NT], ohs[:, n % 2, c, :], ohd[:, n % 2, c, :],
                                                    start=(a < 2), stop=(a >= EC - 2))
                        last.then_inc(s_mm, 1)
                    pe.wait_ge(s_rt, 1)
                    nc.tensor.matmul(pre[:, 0:1], triF[0:NT, 0:NT], cnt[:, 7, 0:1], start=True, stop=True).then_inc(s_pre, 1)

            with ExitStack() as ctx:
                trow = nc.dram_tensor("tile_rows", [4, TCOL * P], F32, kind=INTERNAL).ap()
                tf = ctx.enter_context(nc.sbuf_tensor("tf", [1, 3, TT], F32))
                tT = ctx.enter_context(nc.sbuf_tensor("tT", [TCOL, 4, P], F32))
                tp = ctx.enter_context(nc.psum_tensor("tb_tp", [TCOL, 4, P], F32))
                s_t = sem("tb_transposed")
                s_c = sem("tb_copied")
                s_b = sem("tb_bounce")
                block = ctx.enter_context(nc.Block())

                @block.tensor
                def _(pe):
                    for k in range(4):
                        last = nc.tensor.transpose(tp[:, k, :], table[:, k, :], ident[:])
                    last.then_inc(s_t, 1)

                @block.vector
                def _(dve):
                    dve.wait_ge(s_t, 1)
                    nc.vector.tensor_copy(tT[:], tp[:]).then_inc(s_c, 1)
                    dve.wait_ge(s_b, 80)
                    nc.vector.tensor_copy(tilei[:], tf[:])

                @block.sync
                def _(sp):
                    sp.wait_ge(s_zd, 16 * (TT // ZR))
                    sp.wait_ge(s_c, 1)
                    sp.dma_start(trow.rearrange("k (j p) -> j k p", p=P), tT[:]).then_inc(s_b, 16)
                    sp.wait_ge(s_b, 16)
                    sp.dma_start(keep[:], trow[0, 0:TT].partition_broadcast(P)).then_inc(s_b, 16)
                    for k, r in ((0, 1), (1, 3), (2, 2)):
                        sp.dma_start(tf[:, k, :], trow[r:r + 1, 0:TT]).then_inc(s_b, 16)
                    sp.wait_ge(s_b, 80)

            with ExitStack() as ctx:
                def sb2(name, shape, dt=F32):
                    return ctx.enter_context(nc.sbuf_tensor(name, shape, dt))

                K = 2 * CH
                BODIES = NCH // 2
                ef = sb2("ef", [P, 2, CH, ED])
                eT = sb2("eT", [ED, 2, P])
                rows = sb2("rows", [P, 2, CH, ROW])
                binc = sb2("binc", [P, 2, CH])
                oh = sb2("oh", [P, CH, BINS], F16)
                posf = sb2("posf", [P, 2, CH])
                posi = sb2("posi", [P, 2, CH], I32)
                junk = sb2("junk2", [P, 2, BINS])
                run = ctx.enter_context(nc.psum_tensor("run", [P, 2, 2 * BANK], F32))
                pe_t = ctx.enter_context(nc.psum_tensor("s_pet", [P, 2, BANK], F32))
                pe_q = ctx.enter_context(nc.psum_tensor("s_peq", [P, 2, BANK], F32))
                s_row = [sem("s_row_a"), sem("s_row_b")]
                s_idx = sem("s_row_indices")
                s_bin = sem("s_bins_copied")
                s_oh = sem("s_onehot")
                s_run = sem("s_running")
                s_pos = sem("s_position")
                s_upd = sem("s_run_updated")
                s_int = sem("s_position_int")
                s_te = sem("s_features_turned")
                s_ce = sem("s_features_copied")
                s_q = sem("s_projected")
                s_cq = sem("s_projected_copied")
                s_sc = [sem("s_scattered_a"), sem("s_scattered_b")]
                s_pad = sem("s_rows_padded")
                s_go = sem("s_pool_passed")
                s_ago = sem("s_act_passed")
                block = ctx.enter_context(nc.Block())

                def half(k):
                    return k // CH, k % CH

                def prev(i, k):
                    return (i, k - 1) if k else (i - 1, K - 1)

                @block.sync
                def _(sp):
                    sp.wait_ge(s_pad, 2)

                    def load(i, h, first):
                        if not first:
                            sp.wait_ge(s_te, (i - 1) * K + (h + 1) * CH)
                        c0 = (i * 2 + h) * CH
                        sp.dma_start(ef[0:P - 1, h, :, :],
                                     ea[0:(P - 1) * EC, :].rearrange("(p c) d -> p c d", c=EC)[:, ds(c0, CH), :]).then_inc(s_row[h], 16)

                    def load_last(i, h, n):
                        c0 = (P - 1) * EC + (i * 2 + h) * CH
                        sp.dma_start(ef[P - 1:P, h, 0:n, :], ea[ds(c0, n), :].unsqueeze(0)).then_inc(s_row[h], 16)

                    whole = ER // CH // 2
                    for h in range(2):
                        load(0, h, True)
                        load_last(0, h, CH)
                    with sp.Fori(1, whole) as i:
                        for h in range(2):
                            load(i, h, False)
                            load_last(i, h, CH)
                    for i in range(whole, BODIES):
                        for h in range(2):
                            load(i, h, False)
                            n = min(CH, ER - (i * 2 + h) * CH)
                            if n > 0:
                                load_last(i, h, n)
                            else:
                                load_last(0, h, 1)

                @block.scalar
                def _(act):
                    act.wait_ge(s_pad, 2)

                    def projected(i, k):
                        h, c = half(k)
                        act.wait_ge(s_q, i * K + k + 1)
                        nc.scalar.activation(rows[:, h, c, 0:D], pe_q[:, k % 2, 0:D], ACT.Copy).then_inc(s_cq, 1)

                    def step(i, first):
                        for k in range(K):
                            h, c = half(k)
                            act.wait_ge(s_te, i * K + k + 1)
                            nc.scalar.activation(eT[:, k % 2, :], pe_t[0:ED, k % 2, 0:P], ACT.Copy).then_inc(s_ce, 1)
                            if not (first and k == 0):
                                projected(*prev(i, k))
                            if c == 0:
                                if not first:
                                    act.wait_ge(s_sc[h], i * (16 * CH))
                                act.sem_inc(s_ago, 1)
                                nc.scalar.activation(rows[:, h, :, D:D + 3].rearrange("p c k -> p k c"),
                                                     lo[:, :, ds((i * 2 + h) * CH, CH)], ACT.Copy).then_inc(s_idx, 1)
                            act.wait_ge(s_pos, i * K + k + 1)
                            nc.scalar.activation(posi[:, h, c:c + 1], posf[:, h, c:c + 1], ACT.Copy).then_inc(s_int, 1)
                    step(0, True)
                    with act.Fori(1, BODIES) as i:
                        step(i, False)
                    projected(BODIES - 1, K - 1)

                @block.vector
                def _(dve):
                    nc.vector.memset(rows[:], 0.0).then_inc(s_pad, 1)
                    nc.vector.memset(ef[:], 0.0).then_inc(s_pad, 1)

                    def step(i, first):
                        for h in range(2):
                            c0 = (i * 2 + h) * CH
                            if not first:
                                dve.wait_ge(s_int, (i - 1) * K + (h + 1) * CH)
                            nc.vector.tensor_copy(binc[:, h, :], binf[:, ds(c0, CH)]).then_inc(s_bin, 1)
                            dve.wait_ge(s_bin, i * 2 + h + 1)

                            def onehot(c):
                                if not (first and h == 0):
                                    dve.wait_ge(s_upd, i * K + h * CH + c - CH + 1)
                                nc.vector.tensor_scalar(oh[:, c, :], iota625[:], binc[:, h, c:c + 1], None,
                                                        ALU.is_equal).then_inc(s_oh, 1)

                            onehot(0)
                            for c in range(CH):
                                k = h * CH + c
                                if c + 1 < CH:
                                    onehot(c + 1)
                                dve.wait_ge(s_run, i * K + k + 1)
                                nc.vector.tensor_tensor_reduce(
                                    junk[:, k % 2, :], run[:, k % 2, 0:BINS], oh[:, c, :], 1.0, 0.0, ALU.mult, ALU.add,
                                    posf[:, h, c:c + 1]).then_inc(s_pos, 1)
                    step(0, True)
                    with dve.Fori(1, BODIES) as i:
                        step(i, False)

                @block.tensor
                def _(pe):
                    parts = ((0, BANK), (BANK, BINS))
                    for k in range(2):
                        for a, b in parts:
                            nc.tensor.matmul(run[:, k, a:b], ones[0:1, :], starts[:, k, a:b], start=True, stop=False,
                                             skip_group_check=True)

                    def update(i, k):
                        pe.wait_ge(s_pos, i * K + k + 1)
                        for a, b in parts:
                            last = nc.tensor.matmul(run[:, k % 2, a:b], ntri[:], oh[:, k % CH, a:b], start=False,
                                                    stop=False, skip_group_check=True)
                        last.then_inc(s_upd, 1)

                    def project(i, k, first):
                        n = i * K + k
                        pe.wait_ge(s_ce, n + 1)
                        if not (first and k < 2):
                            pe.wait_ge(s_cq, n - 1)
                        nc.tensor.matmul(pe_q[:, k % 2, 0:D], eT[:, k % 2, :], w1b[:], start=True, stop=True).then_inc(s_q, 1)

                    def step(i, first):
                        for k in range(K):
                            h, c = half(k)
                            if c == 0:
                                pe.wait_ge(s_row[h], i * 32 + 32)
                            pe.wait_ge(s_oh, i * K + k + 1)
                            for a, b in parts:
                                last = nc.tensor.matmul(run[:, k % 2, a:b], tri[:], oh[:, c, a:b], start=False,
                                                        stop=False, skip_group_check=True)
                            last.then_inc(s_run, 1)
                            nc.tensor.matmul(pe_t[0:ED, k % 2, 0:P], ef[:, h, c, :], ident[:], is_transpose=True,
                                             start=True, stop=True).then_inc(s_te, 1)
                            if not (first and k < 1):
                                project(*prev(i, k), first)
                                update(*prev(i, k))
                    step(0, True)
                    with pe.Fori(1, BODIES) as i:
                        step(i, False)
                    project(BODIES - 1, K - 1, False)

                @block.gpsimd
                def _(pool):
                    def step(i):
                        for k in range(K):
                            h, c = half(k)
                            if c == 0:
                                pool.wait_ge(s_idx, i * 2 + h + 1)
                            pool.wait_ge(s_cq, i * K + k + 1)
                            pool.wait_ge(s_int, i * K + k + 1)
                            pool.sem_inc(s_go, 1)
                            pool.indirect_dma_start(
                                sortd, bass.IndirectOffsetOnAxis(ap=posi[:, h, c:c + 1], axis=0),
                                rows[:, h, c, :], None).then_inc(s_sc[h], 16)
                    step(0)
                    with pool.Fori(1, BODIES) as i:
                        step(i)
                    for h in range(2):
                        pool.wait_ge(s_sc[h], 16 * CH * BODIES)

        with ExitStack() as ctx:
            def sb(name, shape, dt=F32):
                return ctx.enter_context(nc.sbuf_tensor(name, shape, dt))

            def pb(name, shape, dt=F32):
                return ctx.enter_context(nc.psum_tensor(name, shape, dt))

            PN = sb("PN", [P, NT + 1, 3, D], BF16)
            pr = sb("pr", [P, 2, 2, D])
            iota16 = sb("iota16", [P, P], BF16)
            ident16 = sb("ident16", [P, P], BF16)
            rt = sb("rt", [P, RING, G, ROW])
            ohd = sb("ohd_e", [P, RING, G, P], BF16)
            ohw = sb("ohw_e", [P, RING, G, P])
            ohs = sb("ohs_e", [P, RING, G, P])
            ohs16 = sb("ohs16_e", [P, RING, G, P], BF16)
            dT = sb("dT", [P, 2, G, P], BF16)
            pre = sb("pre_e", [P, 2, G, P])
            excess = sb("excess", [P, 2, G, P])
            hid = sb("hid", [P, 2, G, D + 1])
            acc = sb("acc", [P, 2, G, 2 * P])
            pdt = pb("pdt", [P, 2, 2 * G, P], BF16)
            px = pb("px", [P, 2, G, P])
            pm = pb("pm", [P, 2, 2, 2 * P])
            ps = pb("ps", [P, 2, BANK])
            s_pn = sem("e_pn")
            s_pc = sem("e_pn_copied")
            s_pr = sem("e_pn_parts")
            s_k = sem("e_constants")
            s_rt = [sem("e_rows%d" % r) for r in range(RING)]
            s_od = sem("e_dst_onehots")
            s_os = sem("e_src_onehots")
            s_o3 = sem("e_last_src_onehot")
            s_o16 = sem("e_src_onehots16")
            s_td = sem("e_dst_turned")
            s_cd = sem("e_dst_copied")
            s_x = sem("e_hidden")
            s_pre = sem("e_pre")
            s_y = sem("e_excess")
            s_g = sem("e_leaky")
            s_ow = sem("e_weighted_onehots")
            s_m = sem("e_pair_products")
            s_acc = sem("e_accumulated")
            s_sp = sem("e_group_sums")
            s_sa = sem("e_sums_added")
            s_w = [[sem("e_written%d_%d" % (p, j)) for j in range(G)] for p in range(2)]
            s_go = sem("e_pool_passed")
            block = ctx.enter_context(nc.Block())
            sv = sortd.rearrange("(n j p) w -> n p j w", p=P, j=G)
            GROUPS = LOOPS * RING


            @block.sync
            def _(sp):
                def load(n, r):
                    sp.dma_start(rt[:, r, :, :], sv[ds(n, 1)].squeeze(0)).then_inc(s_rt[r], 16)

                def step(i, k, more):
                    n = i * RING + k
                    rows = loads(nc, mybir.EngineType.SP, tilei[0:1, 2, ds(n * G, G)], DUMMY + 2 * G - 1)
                    for j in range(G):
                        if more and j == 2:
                            sp.wait_ge(s_pre, n + 2)
                            sp.wait_ge(s_ow, n + 2)
                            sp.wait_ge(s_os, n + 2)
                            sp.wait_ge(s_o3, n + 2)
                            load(n + 1 + RING, (k + 1) % RING)
                        sp.wait_ge(s_acc, n * G + j + 1)
                        sp.dma_start(ar[ds(rows[j], P, NT), :], acc[:, k % 2, j, :]).then_inc(s_w[k % 2][j], 16)

                for r in range(RING):
                    load(r, r)
                sp.wait_ge(s_pre, 1)
                sp.wait_ge(s_ow, 1)
                sp.wait_ge(s_os, 1)
                sp.wait_ge(s_o3, 1)
                load(RING, 0)
                with sp.Fori(0, LOOPS - 2) as i:
                    for k in range(RING):
                        step(i, k, True)
                for k in range(RING):
                    step(LOOPS - 2, k, k < RING - 1)
                for k in range(RING):
                    step(LOOPS - 1, k, False)
                for p in range(2):
                    for j in range(G):
                        sp.wait_ge(s_w[p][j], 16 * LOOPS * RING // 2)

            @block.gpsimd
            def _(pool):
                def onehots(i, k, first):
                    n = i * RING + k
                    pool.wait_ge(s_rt[k], i * 16 + 16)
                    if not first:
                        pool.wait_ge(s_sp, n - RING + 1)
                        pool.wait_ge(s_o16, n - RING + 1)
                    pool.sem_inc(s_go, 1)
                    for j in range(G - 1):
                        last = nc.gpsimd.tensor_scalar(ohs[:, k, j, :], iota128[:], rt[:, k, j, D + 1:D + 2], None, ALU.is_equal)
                    last.then_inc(s_os, 1)

                def leaky(i, k, first):
                    n = i * RING + k
                    pool.wait_ge(s_y, n + 1)
                    if not (first and k < 2):
                        pool.wait_ge(s_sp, n - 1)
                    pool.sem_inc(s_go, 1)
                    nc.gpsimd.tensor_tensor(hid[:, k % 2, :, 0:D], pre[:, k % 2, :, :], excess[:, k % 2, :, :],
                                            ALU.add).then_inc(s_g, 1)

                onehots(0, 0, True)
                for k in range(RING):
                    onehots(*back(0, k, -1), k + 1 < RING)
                    if k:
                        leaky(0, k - 1, True)
                with pool.Fori(1, LOOPS - 1) as i:
                    for k in range(RING):
                        onehots(*back(i, k, -1), False)
                        leaky(*back(i, k, 1), False)
                for k in range(RING):
                    if k + 1 < RING:
                        onehots(LOOPS - 1, k + 1, False)
                    leaky(*back(LOOPS - 1, k, 1), False)
                leaky(LOOPS - 1, RING - 1, False)

            @block.scalar
            def _(act):
                def negative(i, k, first):
                    n = i * RING + k
                    act.wait_ge(s_pre, n + 1)
                    if not (first and k < 2):
                        act.wait_ge(s_g, n - 1)
                    nc.scalar.activation(excess[:, k % 2, :, :], pre[:, k % 2, :, :], ACT.Relu, scale=-0.8).then_inc(s_y, 1)

                def step(i, k, first):
                    n = i * RING + k
                    if not (first and k < 2):
                        act.wait_ge(s_x, n - 1)
                    act.wait_ge(s_td, n + 1)
                    nc.scalar.activation(dT[:, k % 2, :, :], pdt[:, k % 2, 0:G, :], ACT.Copy).then_inc(s_cd, 1)
                    if not (first and k < 1):
                        negative(*back(i, k, 1), first)
                    if not first:
                        act.wait_ge(s_m, 2 * (n - RING) + 2)
                    act.wait_ge(s_os, n + 1)
                    act.wait_ge(s_o3, n + 1)
                    nc.scalar.activation(ohs16[:, k, :, :], ohs[:, k, :, :], ACT.Copy).then_inc(s_o16, 1)
                    for j in range(G):
                        last = nc.scalar.activation(ohw[:, k, j, :], ohd[:, k, j, :], ACT.Copy, scale=rt[:, k, j, D + 2:D + 3])
                    last.then_inc(s_ow, 1)

                for k in range(RING):
                    step(0, k, True)
                with act.Fori(1, LOOPS) as i:
                    for k in range(RING):
                        step(i, k, False)
                negative(LOOPS - 1, RING - 1, False)

            @block.tensor
            def _(pe):
                for t in range(NT):
                    if t >= 2:
                        pe.wait_ge(s_pc, t - 1)
                    nc.tensor.matmul(px[:, t % 2, 0, :], HT[:, t * P:(t + 1) * P], wl["w1a"][:], start=True, stop=False)
                    nc.tensor.matmul(px[:, t % 2, 0, :], ones[0:1, :], brow["b1"][:], start=False, stop=True).then_inc(s_pn, 1)
                pe.wait_ge(s_k, 1)

                def turn(i, k, first):
                    n = i * RING + k
                    pe.wait_ge(s_od, n + 1)
                    if not (first and k < 2):
                        pe.wait_ge(s_cd, n - 1)
                    for j in range(G):
                        last = nc.tensor.transpose(pdt[:, k % 2, j, :], ohd[:, k, j, :], ident16[:])
                    last.then_inc(s_td, 1)

                def tiles(hid_of, pair_of, first):
                    if hid_of:
                        ih, kh = hid_of
                        nh = ih * RING + kh
                        dt = loads(nc, mybir.EngineType.PE, tilei[0:1, 0, ds(nh * G, G)], NT)
                        pe.wait_ge(s_cd, nh + 1)
                        if not (first and kh < 2):
                            pe.wait_ge(s_pre, nh - 1)
                    if pair_of:
                        ip, kp = pair_of
                        m = ip * RING + kp
                        pe.wait_ge(s_ow, m + 1)
                    for j in range(G):
                        if pair_of:
                            q = j // 2
                            if j % 2 == 0 and not (first and kp < 1):
                                pe.wait_ge(s_acc, (m - 1) * G + 2 * q + 2)
                            nc.tensor.matmul(pm[:, q, j % 2, 0:P], ohs16[:, kp, j, :], ohd[:, kp, j, :], start=True, stop=True)
                            last = nc.tensor.matmul(pm[:, q, j % 2, P:2 * P], ohs[:, kp, j, :], ohw[:, kp, j, :],
                                                    start=True, stop=True)
                            if j % 2:
                                last.then_inc(s_m, 1)
                        if hid_of:
                            for part in range(3):
                                last = nc.tensor.matmul(px[:, kh % 2, j, :], dT[:, kh % 2, j, :],
                                                        PN[:, ds(dt[j], 1), part, :].squeeze(1), start=(part == 0), stop=(part == 2))
                            if j == G - 1:
                                last.then_inc(s_x, 1)

                def group_sums(i, k, first):
                    n = i * RING + k
                    pe.wait_ge(s_g, n + 1)
                    if not (first and k < 2):
                        pe.wait_ge(s_sa, n - 1)
                    for j in range(G):
                        last = nc.tensor.matmul(ps[:, k % 2, 0:D + 1], ohs[:, k, j, :], hid[:, k % 2, j, :],
                                                start=(j == 0), stop=(j == G - 1))
                    last.then_inc(s_sp, 1)

                def step(i, k, first):
                    one, two = not (first and k < 1), not (first and k < 2)
                    turn(i, k, first)
                    if one:
                        tiles(back(i, k, 1), back(i, k, 2) if two else None, first)
                    if two:
                        group_sums(*back(i, k, 2), first)

                for k in range(RING):
                    step(0, k, True)
                with pe.Fori(1, LOOPS) as i:
                    for k in range(RING):
                        step(i, k, False)
                tiles((LOOPS - 1, RING - 1), (LOOPS - 1, RING - 2), False)
                group_sums(LOOPS - 1, RING - 2, False)
                tiles(None, (LOOPS - 1, RING - 1), False)
                group_sums(LOOPS - 1, RING - 1, False)

            @block.vector
            def _(dve):
                nc.vector.tensor_copy(iota16[:], iota128[:])
                nc.vector.tensor_copy(ident16[:], ident[:])
                nc.vector.memset(acc[:], 0.0)
                nc.vector.memset(hid[:], 1.0)
                link = Chain(dve, s_pr)
                for t in range(NT):
                    dve.wait_ge(s_pn, t + 1)
                    v = px[:, t % 2, 0, :]
                    link(nc.vector.tensor_copy(PN[:, t, 0, :], v))
                    link(nc.vector.tensor_tensor(pr[:, t % 2, 0, :], v, PN[:, t, 0, :], ALU.subtract))
                    nc.vector.tensor_copy(PN[:, t, 1, :], pr[:, t % 2, 0, :]).then_inc(s_pc, 1)
                    dve.wait_ge(s_pc, t + 1)
                    nc.vector.tensor_tensor(PN[:, t, 2, :], pr[:, t % 2, 0, :], PN[:, t, 1, :], ALU.subtract)
                link(nc.vector.memset(PN[:, NT, :, :], 0.0))
                dve.drain().then_inc(s_k, 1)
                dve.wait_ge(s_k, 1)

                def onehots(i, k, first, js):
                    n = i * RING + k
                    if js[0] == 0:
                        dve.wait_ge(s_rt[k], i * 16 + 16)
                        if not first:
                            dve.wait_ge(s_m, 2 * (n - RING) + 2)
                    for j in js:
                        last = nc.vector.tensor_scalar(ohd[:, k, j, :], iota16[:], rt[:, k, j, D:D + 1], None, ALU.is_equal)
                    if js[-1] == G - 1:
                        last.then_inc(s_od, 1)

                def add(i, k, first):
                    n = i * RING + k
                    dve.wait_ge(s_x, n + 1)
                    if not (first and k < 2):
                        dve.wait_ge(s_g, n - 1)
                    nc.vector.tensor_tensor(pre[:, k % 2, :, :], px[:, k % 2, :, :], rt[:, k, :, 0:D], ALU.add).then_inc(s_pre, 1)

                def collect(i, k, first, j):
                    n = i * RING + k
                    if j % 2 == 0:
                        dve.wait_ge(s_m, 2 * n + j // 2 + 1)
                    if not (first and k < 2):
                        dve.wait_ge(s_w[k % 2][j], (i * 2 + k // 2) * 16)
                    if not (first and k < 1 and j < 1):
                        dve.wait_ge(s_acc, n * G + j)
                    at = n * G + j
                    before = acc[:, k % 2, j - 1, :] if j else acc[:, (k - 1) % 2, G - 1, :]
                    nc.vector.scalar_tensor_tensor(acc[:, k % 2, j, :], before,
                                                   keep[:, at:at + 1] if isinstance(at, int) else keep[:, ds(at, 1)],
                                                   pm[:, j // 2, j % 2, :], ALU.mult, ALU.add).then_inc(s_acc, 1)

                def place(i, k):
                    return loads(nc, mybir.EngineType.DVE, tilei[0:1, 1, ds((i * RING + k) * G, 1)], NT)[0]

                def sums(i, k, first, st):
                    n = i * RING + k
                    dve.wait_ge(s_sp, n + 1)
                    if not (first and k < 1):
                        dve.wait_ge(s_sa, n)
                    Sv = S[:, ds(st, 1), :].squeeze(1)
                    nc.vector.tensor_tensor(Sv, Sv, ps[:, k % 2, 0:D + 1], ALU.add).then_inc(s_sa, 1)

                def source_onehot(i, k, first):
                    n = i * RING + k
                    dve.wait_ge(s_rt[k], i * 16 + 16)
                    if not first:
                        dve.wait_ge(s_sp, n - RING + 1)
                    nc.vector.tensor_scalar(ohs[:, k, G - 1, :], iota128[:], rt[:, k, G - 1, D + 1:D + 2], None,
                                            ALU.is_equal).then_inc(s_o3, 1)

                def step(i, k, first, final):
                    one, two, three = (not (first and k < n) for n in (1, 2, 3))
                    if two:
                        collect(*back(i, k, 2), first, 0)
                    if not (final and k == RING - 1):
                        source_onehot(*back(i, k, -1), first and k + 1 < RING)
                    if two:
                        collect(*back(i, k, 2), first, 1)
                    if one:
                        add(*back(i, k, 1), first)
                    if three:
                        st = place(*back(i, k, 3))
                    if not (final and k >= RING - 2):
                        onehots(*back(i, k, -2), first and k + 2 < RING, (0, 1))
                    if two:
                        collect(*back(i, k, 2), first, 2)
                    if three:
                        sums(*back(i, k, 3), first, st)
                    if two:
                        collect(*back(i, k, 2), first, 3)
                    if not (final and k >= RING - 2):
                        onehots(*back(i, k, -2), first and k + 2 < RING, (2, 3))

                onehots(0, 0, True, (0, 1, 2, 3))
                onehots(0, 1, True, (0, 1, 2, 3))
                source_onehot(0, 0, True)
                for k in range(RING):
                    step(0, k, True, False)
                with dve.Fori(1, LOOPS - 1) as i:
                    for k in range(RING):
                        step(i, k, False, False)
                for k in range(RING):
                    step(LOOPS - 1, k, False, True)
                add(LOOPS - 1, RING - 1, False)
                sums(LOOPS - 1, RING - 3, False, place(LOOPS - 1, RING - 3))
                for k in (RING - 2, RING - 1):
                    for j in range(G):
                        collect(LOOPS - 1, k, False, j)
                    sums(LOOPS - 1, k, False, place(LOOPS - 1, k))

        with ExitStack() as ctx:
            ST = ctx.enter_context(nc.sbuf_tensor("ST", [P, NP], F32))
            OD = ctx.enter_context(nc.sbuf_tensor("OD", [1, NP], F32))
            AG = ctx.enter_context(nc.sbuf_tensor("AG", [P, NP], F32))
            Y2 = ctx.enter_context(nc.sbuf_tensor("Y2", [P, 2, BANK], F32))
            c02 = ctx.enter_context(nc.sbuf_tensor("c02", [P, 1], F32))
            tp = ctx.enter_context(nc.psum_tensor("u_tp", [P, 2, BANK], F32))
            tr = ctx.enter_context(nc.psum_tensor("u_tr", [1, 2, BANK], F32))
            mm = ctx.enter_context(nc.psum_tensor("u_mm", [P, 2, BANK], F32))
            po = ctx.enter_context(nc.psum_tensor("u_po", [P, 2, BANK], F32))
            s_t = sem("u_transposed")
            s_tc = sem("u_transposed_copied")
            s_a = sem("u_aggregate")
            s_ac = sem("u_aggregate_copied")
            s_h = sem("u_hidden")
            s_y = sem("u_hidden_02")
            s_hc = sem("u_hidden_done")
            s_o = sem("u_out")
            s_x = sem("u_x")
            s_c = sem("u_bias_02")
            block = ctx.enter_context(nc.Block())
            NC = len(CUTS)

            @block.tensor
            def _(pe):
                def turn(c):
                    a, b = CUTS[c]
                    if c >= 2:
                        pe.wait_ge(s_tc, c - 1)
                    for t in range(a // P, b // P):
                        o = t * P - a
                        nc.tensor.transpose(tp[:, c % 2, o:o + P], S[:, t, 0:D], ident[:])
                        last = nc.tensor.transpose(tr[:, c % 2, o:o + P], S[:, t, D:D + 1], ident[:])
                    last.then_inc(s_t, 1)

                def aggregate(c):
                    a, b = CUTS[c]
                    pe.wait_ge(s_tc, c + 1)
                    if c >= 1:
                        pe.wait_ge(s_hc, c)
                    nc.tensor.matmul(mm[:, 0, 0:b - a], wl["w2"][:], ST[:, a:b], start=True, stop=False)
                    nc.tensor.matmul(mm[:, 0, 0:b - a], brow["b2"][:], OD[:, a:b], start=False, stop=True).then_inc(s_a, 1)

                def hidden(c):
                    a, b = CUTS[c]
                    nc.tensor.matmul(mm[:, 1, 0:b - a], wl["u1a"][:], HT[:, a:b], start=True, stop=False)
                    pe.wait_ge(s_ac, c + 1)
                    nc.tensor.matmul(mm[:, 1, 0:b - a], wl["u1b"][:], AG[:, a:b], start=False, stop=True).then_inc(s_h, 1)

                def out_tiles(c):
                    a, b = CUTS[c]
                    pe.wait_ge(s_hc, c + 1)
                    for t in range(a // P, b // P):
                        if t >= 2:
                            pe.wait_ge(s_x, t - 1)
                        nc.tensor.matmul(po[:, t % 2, 0:D], ST[:, t * P:(t + 1) * P], wl["u2"][:], start=True, stop=False)
                        nc.tensor.matmul(po[:, t % 2, 0:D], ones[0:1, :], brow["c2"][:], start=False, stop=True).then_inc(s_o, 1)

                turn(0)
                for c in range(NC):
                    if c + 1 < NC:
                        turn(c + 1)
                    aggregate(c)
                    hidden(c)
                    out_tiles(c)

            @block.scalar
            def _(act):
                nc.scalar.activation(c02[:], c1col[:], ACT.Copy, scale=0.2).then_inc(s_c, 1)
                act.wait_ge(s_c, 1)
                for c, (a, b) in enumerate(CUTS):
                    act.wait_ge(s_a, c + 1)
                    nc.scalar.activation(AG[:, a:b], mm[:, 0, 0:b - a], ACT.Copy).then_inc(s_ac, 1)
                    act.wait_ge(s_h, c + 1)
                    nc.scalar.activation(Y2[:, c % 2, 0:b - a], mm[:, 1, 0:b - a], ACT.Identity, scale=0.2,
                                         bias=c02[:, 0:1]).then_inc(s_y, 1)

            @block.vector
            def _(dve):
                def copy(c):
                    a, b = CUTS[c]
                    dve.wait_ge(s_t, c + 1)
                    nc.vector.tensor_copy(ST[:, a:b], tp[:, c % 2, 0:b - a])
                    nc.vector.tensor_copy(OD[:, a:b], tr[:, c % 2, 0:b - a]).then_inc(s_tc, 1)

                copy(0)
                for c, (a, b) in enumerate(CUTS):
                    if c + 1 < NC:
                        copy(c + 1)
                    dve.wait_ge(s_y, c + 1)
                    nc.vector.scalar_tensor_tensor(ST[:, a:b], mm[:, 1, 0:b - a], c1col[:, 0:1], Y2[:, c % 2, 0:b - a],
                                                   ALU.add, ALU.max).then_inc(s_hc, 1)
                    for t in range(a // P, b // P):
                        dve.wait_ge(s_o, t + 1)
                        nc.vector.tensor_tensor(X[:, t, :], X[:, t, :], po[:, t % 2, 0:D], ALU.add).then_inc(s_x, 1)

        mid.close()
        layernorm(1)

        arv = ar.rearrange("(s p q) c -> s p q c", p=P, q=NT)
        HALF = [(0, 12), (12, NT)]
        assert HALF[0][1] * P % BANK == 0
        PIECES = [[(a, b) for a, b in CUTS if lo_ * P <= a < hi_ * P] for lo_, hi_ in HALF]

        with ExitStack() as lay:
            ss = lay.enter_context(nc.sbuf_tensor("ss", [P, 4, NT], F32))
            sd = lay.enter_context(nc.sbuf_tensor("sd", [P, NT], F32))
            mn = lay.enter_context(nc.sbuf_tensor("mn", [P, 2], F32))
            MX = lay.enter_context(nc.sbuf_tensor("MX", [P, NP], F32))
            DG = lay.enter_context(nc.sbuf_tensor("DG", [P, NP], F32))
            with ExitStack() as ctx:
                WT = ctx.enter_context(nc.sbuf_tensor("WT", [P, P], F32))
                at = ctx.enter_context(nc.sbuf_tensor("at", [P, 2], F32))
                wa = ctx.enter_context(nc.sbuf_tensor("wa", [P, 2], F32))
                m1 = ctx.enter_context(nc.sbuf_tensor("m1", [P, 1], F32))
                m2 = ctx.enter_context(nc.sbuf_tensor("m2", [1, 1], F32))
                tp = ctx.enter_context(nc.psum_tensor("s_tp", [P, BANK], F32))
                pw = ctx.enter_context(nc.psum_tensor("s_pw", [P, BANK], F32))
                pss = ctx.enter_context(nc.psum_tensor("s_pss", [P, BANK // 2, 2], F32))
                pt = ctx.enter_context(nc.psum_tensor("s_pt", [1, BANK], F32))
                pb = ctx.enter_context(nc.psum_tensor("s_pb", [P, BANK], F32))
                s_ld = sem("a_attn")
                s_pe = sem("a_pe")
                s_dv = sem("a_dve")
                s_ch = sem("a_chain")
                block = ctx.enter_context(nc.Block())

                @block.sync
                def _(sp):
                    with nc.allow_non_contiguous_dma(reason="the attention vector as two columns"):
                        sp.dma_start(at[:], attn.rearrange("(a d) -> d a", a=2)).then_inc(s_ld, 16)
                    sp.wait_ge(s_ld, 16)

                @block.tensor
                def _(pe):
                    nc.tensor.transpose(tp[:, 0:P], wl["W1"][:], ident[:]).then_inc(s_pe, 1)
                    pe.wait_ge(s_ld, 16)
                    pe.wait_ge(s_dv, 1)
                    nc.tensor.matmul(pw[:, 0:2], WT[:], at[:], start=True, stop=True).then_inc(s_pe, 1)
                    pe.wait_ge(s_dv, 2)
                    for t in range(NT):
                        last = nc.tensor.matmul(pss[:, t, :], HT[:, t * P:(t + 1) * P], wa[:], start=True, stop=True)
                    last.then_inc(s_pe, 1)
                    pe.wait_ge(s_dv, 3)
                    nc.tensor.transpose(pt[:, 0:P], m1[:], ident[:]).then_inc(s_pe, 1)
                    pe.wait_ge(s_dv, 4)
                    nc.tensor.matmul(pb[:, 0:1], ones[0:1, :], m2[:], start=True, stop=True).then_inc(s_pe, 1)

                @block.vector
                def _(dve):
                    link = Chain(dve, s_ch)
                    nc.vector.memset(MX[:], 0.0)
                    dve.wait_ge(s_pe, 1)
                    nc.vector.tensor_copy(WT[:], tp[:, 0:P]).then_inc(s_dv, 1)
                    dve.wait_ge(s_pe, 2)
                    nc.vector.tensor_copy(wa[:], pw[:, 0:2]).then_inc(s_dv, 1)
                    dve.wait_ge(s_pe, 3)
                    nc.vector.tensor_copy(sd[:], pss[:, 0:NT, 1])
                    link(nc.vector.tensor_copy(ss[:, 0, :], pss[:, 0:NT, 0]))
                    nc.vector.tensor_scalar(ss[:, 1, :], ss[:, 0, :], 0.01, None, ALU.mult)
                    nc.vector.tensor_scalar(ss[:, 3, :], ss[:, 0, :], 0.99, None, ALU.mult)
                    nc.vector.tensor_reduce(m1[:], ss[:, 0, :], AX.X, ALU.min).then_inc(s_dv, 1)
                    dve.wait_ge(s_pe, 4)
                    nc.vector.tensor_reduce(m2[:], pt[:, 0:P], AX.X, ALU.min).then_inc(s_dv, 1)
                    dve.wait_ge(s_pe, 5)
                    link(nc.vector.tensor_scalar(mn[:, 0:1], pb[:, 0:1], -1.0, None, ALU.add))
                    nc.vector.tensor_scalar(ss[:, 2, :], ss[:, 0, :], mn[:, 0:1], None, ALU.subtract)

            with ExitStack() as ctx:
                R = 5
                assert NT % R == 0
                ab = ctx.enter_context(nc.sbuf_tensor("ab", [P, R, NT, P], F32))
                un = ctx.enter_context(nc.sbuf_tensor("un", [P, NT, P], F32))
                pg = ctx.enter_context(nc.psum_tensor("m_pg", [1, len(CUTS), BANK], F32))
                MXv = MX[:].rearrange("p (q d) -> p q d", q=NT)
                BIG = 1e30
                s_ld = [sem("m_load%d" % r) for r in range(R)]
                s_un = sem("m_where_no_edge")
                s_mx = sem("m_max")
                s_dg = sem("m_degree")
                s_ago = sem("m_act_passed")
                block = ctx.enter_context(nc.Block())

                @block.sync
                def _(sp):
                    def load(s, r):
                        sp.dma_start(ab[:, r, :, :], arv[ds(s, 1), :, :, 0:P].squeeze(0)).then_inc(s_ld[r], 16)
                    for r in range(R):
                        load(r, r)
                    with sp.Fori(1, NT // R) as i:
                        for r in range(R):
                            sp.wait_ge(s_un, ((i - 1) * R + r) * 2 + 2)
                            sp.wait_ge(s_dg, ((i - 1) * R + r) * 2 + 2)
                            load(i * R + r, r)

                @block.scalar
                def _(act):
                    def step(i, first):
                        for r in range(R):
                            s = i * R + r
                            act.wait_ge(s_ld[r], i * 16 + 16)
                            for h, (a, b) in enumerate(HALF):
                                if not (first and r == 0):
                                    act.wait_ge(s_mx, s * 2 + h - 1)
                                act.sem_inc(s_ago, 1)
                                nc.scalar.activation(un[:, a:b, :], ab[:, r, a:b, :], ACT.Relu, bias=ss[:, 2, ds(s, 1)],
                                                     scale=-BIG).then_inc(s_un, 1)
                    step(0, True)
                    with act.Fori(1, NT // R) as i:
                        step(i, False)

                @block.vector
                def _(dve):
                    def step(s, first):
                        for h, (a, b) in enumerate(HALF):
                            dve.wait_ge(s_un, s * 2 + h + 1)
                            if not first:
                                dve.wait_ge(s_mx, s * 2 + h - 1)
                            nc.vector.scalar_tensor_tensor(MXv[:, a:b, :], un[:, a:b, :], ss[:, 2, ds(s, 1)], MXv[:, a:b, :],
                                                           ALU.subtract, ALU.min).then_inc(s_mx, 1)
                    step(0, True)
                    with dve.Fori(1, NT) as s:
                        step(s, False)
                    dve.wait_ge(s_dg, 2 * NT)
                    for c, (a, b) in enumerate(CUTS):
                        nc.vector.tensor_copy(DG[0:1, a:b], pg[:, c, 0:b - a])

                @block.tensor
                def _(pe):
                    def step(i, first, final):
                        for r in range(R):
                            pe.wait_ge(s_ld[r], i * 16 + 16)
                            for c, (a, b) in enumerate(CUTS):
                                last = nc.tensor.matmul(pg[:, c, 0:b - a], ones[:, 0:1],
                                                        ab[:, r, :, :].rearrange("p q d -> p (q d)")[:, a:b],
                                                        start=first and r == 0, stop=final and r == R - 1,
                                                        skip_group_check=True)
                            last.then_inc(s_dg, 2)
                    step(0, True, False)
                    with pe.Fori(1, NT // R - 1) as i:
                        step(i, False, False)
                    step(NT // R - 1, False, True)

            RB = lay.enter_context(nc.sbuf_tensor("RB", [P, 2, NP], F32))
            with ExitStack() as ctx:
                mc = ctx.enter_context(nc.sbuf_tensor("mc", [P, 3, NT], F32))
                dm = ctx.enter_context(nc.sbuf_tensor("dm", [P, 2 * NT], F32))
                dT = ctx.enter_context(nc.sbuf_tensor("dmT", [2 * NT, P], F32))
                tp = ctx.enter_context(nc.psum_tensor("x_tp", [P, 2, BANK], F32))
                pd = ctx.enter_context(nc.psum_tensor("x_pd", [P, BANK], F32))
                pr = ctx.enter_context(nc.psum_tensor("x_pr", [2 * NT, BANK], F32))
                s_t = sem("x_turned")
                s_r = sem("x_reduced")
                s_d = sem("x_degrees")
                s_m = sem("x_rows")
                s_mt = sem("x_rows_turned")
                s_mc = sem("x_rows_copied")
                s_b = sem("x_bounce")
                s_ch = sem("x_chain")
                block = ctx.enter_context(nc.Block())

                @block.tensor
                def _(pe):
                    for t in range(NT):
                        last = nc.tensor.matmul(pd[:, t:t + 1], DG[0:1, t * P:(t + 1) * P], ones[0:1, 0:1], start=True, stop=True)
                    last.then_inc(s_d, 1)
                    for c, (a, b) in enumerate(CUTS):
                        if c >= 2:
                            pe.wait_ge(s_r, c - 1)
                        for t in range(a // P, b // P):
                            last = nc.tensor.transpose(tp[:, c % 2, t * P - a:(t + 1) * P - a], MX[:, t * P:(t + 1) * P], ident[:])
                        last.then_inc(s_t, 1)
                    pe.wait_ge(s_m, 1)
                    nc.tensor.transpose(pr[:, 0:P], dm[:], ident[:]).then_inc(s_mt, 1)

                @block.vector
                def _(dve):
                    link = Chain(dve, s_ch)
                    dve.wait_ge(s_d, 1)
                    nc.vector.tensor_copy(DEG[:], pd[:, 0:NT])
                    for c, (a, b) in enumerate(CUTS):
                        dve.wait_ge(s_t, c + 1)
                        last = nc.vector.tensor_reduce(mc[:, 0, a // P:b // P],
                                                       tp[:, c % 2, 0:b - a].rearrange("p (t d) -> p t d", d=P), AX.X, ALU.min)
                        last.then_inc(s_r, 1)
                    dve.wait_ge(s_r, len(CUTS))
                    link(nc.vector.tensor_scalar(mc[:, 0, :], mc[:, 0, :], mn[:, 0:1], None, ALU.subtract))
                    link(nc.vector.scalar_tensor_tensor(mc[:, 1, :], mc[:, 0, :], -1.0, sd[:], ALU.mult, ALU.add))
                    link(nc.vector.scalar_tensor_tensor(mc[:, 2, :], mc[:, 1, :], 0.01, mc[:, 1, :], ALU.mult, ALU.max))
                    nc.vector.tensor_tensor(dm[:, 0:NT], sd[:], mc[:, 2, :], ALU.subtract)
                    nc.vector.scalar_tensor_tensor(dm[:, NT:2 * NT], sd[:], 0.01, mc[:, 2, :], ALU.mult,
                                                   ALU.subtract).then_inc(s_m, 1)
                    dve.wait_ge(s_mt, 1)
                    nc.vector.tensor_copy(dT[:], pr[:, 0:P]).then_inc(s_mc, 1)

                @block.sync
                def _(sp):
                    sp.wait_ge(s_mc, 1)
                    sp.dma_start(nodes_row.rearrange("a (t p) -> (a t) p", p=P), dT[:]).then_inc(s_b, 16)
                    sp.wait_ge(s_b, 16)
                    sp.dma_start(RB[:].rearrange("p a n -> p (a n)"),
                                 nodes_row.rearrange("a n -> (a n)").partition_broadcast(P)).then_inc(s_b, 16)
                    sp.wait_ge(s_b, 32)

            with ExitStack() as ctx:
                arb = ctx.enter_context(nc.sbuf_tensor("arb", [P, NT, 2, P], F32))
                ex = ctx.enter_context(nc.sbuf_tensor("ex", [P, 2, 13, P], F32))
                rx = ctx.enter_context(nc.sbuf_tensor("rx", [P, NT, P], F32))
                hw = ctx.enter_context(nc.sbuf_tensor("hw", [P, D], F32))
                tmp2 = ctx.enter_context(nc.sbuf_tensor("tmp2", [P, NT, P], F32))
                num = ctx.enter_context(nc.psum_tensor("num", [P, len(CUTS), BANK], F32))
                RBv = RB[:].rearrange("p a (q d) -> p a q d", q=NT)
                MXv = MX[:].rearrange("p (q d) -> p q d", q=NT)
                s_ld = [sem("w_load_a"), sem("w_load_b")]
                s_t = sem("w_exponents")
                s_e = sem("w_exp")
                s_ax = sem("w_edge_weights")
                s_rx = sem("w_relation_weights")
                s_dn = sem("w_denominators")
                s_mm = sem("w_products")
                s_w = sem("w_stationary")
                s_z = sem("w_zero")
                s_ago = sem("w_act_passed")
                blk = ExitStack()
                block = blk.enter_context(nc.Block())

                @block.sync
                def _(sp):
                    def load(s, h):
                        a, b = HALF[h]
                        sp.dma_start(arb[:, a:b, :, :].rearrange("p q a d -> p (q a d)"),
                                     arv[ds(s, 1), :, a:b, :].squeeze(0).rearrange("p q c -> p (q c)")).then_inc(s_ld[h], 16)
                    load(0, 0)
                    load(0, 1)
                    with sp.Fori(1, NT) as s:
                        for h in range(2):
                            sp.wait_ge(s_ax, s * 2 + h - 1)
                            sp.wait_ge(s_rx, s * 2 + h - 1)
                            load(s, h)

                @block.scalar
                def _(act):
                    def exp(s, h):
                        a, b = HALF[h]
                        act.wait_ge(s_t, s * 2 + h + 1)
                        act.sem_inc(s_ago, 1)
                        nc.scalar.activation(ex[:, h, 0:b - a, :], ex[:, h, 0:b - a, :], ACT.Exp,
                                             bias=ss[:, 1, ds(s, 1)]).then_inc(s_e, 1)

                    def step(s, first):
                        exp(s, 0)
                        if not first:
                            act.wait_ge(s_mm, s * 2)
                        act.sem_inc(s_ago, 1)
                        nc.scalar.activation(hw[:], H[:, ds(s, 1), :].squeeze(1), ACT.Copy).then_inc(s_w, 1)
                        exp(s, 1)
                    step(0, True)
                    with act.Fori(1, NT) as s:
                        step(s, False)

                @block.vector
                def _(dve):
                    nc.vector.memset(MX[:], 0.0).then_inc(s_z, 1)

                    def exponent(s, h, first):
                        a, b = HALF[h]
                        if not first:
                            dve.wait_ge(s_rx, s * 2 + h - 1)
                        nc.vector.scalar_tensor_tensor(ex[:, h, 0:b - a, :], RBv[:, 0, a:b, :], ss[:, 3, ds(s, 1)],
                                                       RBv[:, 1, a:b, :], ALU.add, ALU.max).then_inc(s_t, 1)

                    def step(s, first, final):
                        for h, (a, b) in enumerate(HALF):
                            if h == 0:
                                exponent(s, 1, first)
                            elif not final:
                                exponent(s + 1, 0, False)
                            e = ex[:, h, 0:b - a, :]
                            dve.wait_ge(s_e, s * 2 + h + 1)
                            dve.wait_ge(s_ld[h], s * 16 + 16)
                            if not first:
                                dve.wait_ge(s_dn, s * 2 + h - 1)
                                dve.wait_ge(s_mm, s * 2 + h - 1)
                            nc.vector.scalar_tensor_tensor(tmp2[:, a:b, :], e, 2.0, arb[:, a:b, 0, :], ALU.min,
                                                           ALU.mult).then_inc(s_ax, 1)
                            nc.vector.scalar_tensor_tensor(rx[:, a:b, :], e, 2.0, arb[:, a:b, 1, :], ALU.min,
                                                           ALU.mult).then_inc(s_rx, 1)
                    exponent(0, 0, True)
                    step(0, True, False)
                    with dve.Fori(1, NT - 1) as s:
                        step(s, False, False)
                    step(NT - 1, False, True)

                @block.gpsimd
                def _(pool):
                    pool.wait_ge(s_z, 1)

                    def step(s, first):
                        for h, (a, b) in enumerate(HALF):
                            pool.wait_ge(s_ax, s * 2 + h + 1)
                            if not first:
                                pool.wait_ge(s_dn, s * 2 + h - 1)
                            nc.gpsimd.tensor_tensor(MXv[:, a:b, :], MXv[:, a:b, :], tmp2[:, a:b, :], ALU.add).then_inc(s_dn, 1)
                    step(0, True)
                    with pool.Fori(1, NT) as s:
                        step(s, False)

                @block.tensor
                def _(pe):
                    def step(s, first, final):
                        pe.wait_ge(s_w, s + 1)
                        for h in range(2):
                            pe.wait_ge(s_rx, s * 2 + h + 1)
                            for a, b in PIECES[h]:
                                last = nc.tensor.matmul(num[:, a // BANK, 0:b - a], hw[:],
                                                        rx[:].rearrange("p q d -> p (q d)")[:, a:b],
                                                        start=first, stop=final, skip_group_check=True)
                            last.then_inc(s_mm, 1)
                    step(0, True, False)
                    with pe.Fori(1, NT - 1) as s:
                        step(s, False, False)
                    step(NT - 1, False, True)

                blk.close()
                evacuate("w", num, DG)

            with ExitStack() as ctx:
                pden = ctx.enter_context(nc.psum_tensor("q_den", [P, BANK], F32))
                po = ctx.enter_context(nc.psum_tensor("q_po", [P, 2, BANK], F32))
                rden = ctx.enter_context(nc.sbuf_tensor("rden", [P, NT], F32))
                s_d = sem("q_denominators")
                s_ch = sem("q_chain")
                s_o = sem("q_out")
                s_x = sem("q_x")
                block = ctx.enter_context(nc.Block())

                @block.tensor
                def _(pe):
                    for t in range(NT):
                        last = nc.tensor.matmul(pden[:, t:t + 1], MX[:, t * P:(t + 1) * P], ones[:, 0:1], start=True, stop=True)
                    last.then_inc(s_d, 1)
                    for t in range(NT):
                        if t >= 2:
                            pe.wait_ge(s_x, t - 1)
                        nc.tensor.matmul(po[:, t % 2, 0:D], DG[:, t * P:(t + 1) * P], wl["W1"][:], start=True, stop=True).then_inc(s_o, 1)

                @block.vector
                def _(dve):
                    link = Chain(dve, s_ch)
                    dve.wait_ge(s_d, 1)
                    link(nc.vector.tensor_scalar(rden[:], pden[:, 0:NT], 1e-30, None, ALU.max))
                    link(nc.vector.reciprocal(rden[:], rden[:]))
                    for t in range(NT):
                        dve.wait_ge(s_o, t + 1)
                        nc.vector.scalar_tensor_tensor(X[:, t, :], po[:, t % 2, 0:D], rden[:, t:t + 1], X[:, t, :],
                                                       ALU.mult, ALU.add).then_inc(s_x, 1)

        layernorm(2)

        R = 5
        s_gld = [sem("g_load%d" % r) for r in range(R)]
        s_gw = sem("g_stationary")
        s_gmm = sem("g_products")
        s_gon = sem("g_begun")

        def gather_product(tag, turn, scale, AGT):
            with ExitStack() as ctx:
                done = turn * NT
                loaded = turn * 16 * (NT // R)
                ab = ctx.enter_context(nc.sbuf_tensor("ab" + tag, [P, R, NT, P], F32))
                hw = ctx.enter_context(nc.sbuf_tensor("hw" + tag, [P, R, D], F32))
                num = ctx.enter_context(nc.psum_tensor("num" + tag, [P, len(CUTS), BANK], F32))
                assert NT % R == 0

                with nc.Block() as block:
                    @block.sync
                    def _(sp):
                        def load(s, r):
                            sp.dma_start(ab[:, r, :, :], arv[ds(s, 1), :, :, 0:P].squeeze(0)).then_inc(s_gld[r], 16)
                        for r in range(R):
                            load(r, r)
                        with sp.Fori(1, NT // R) as i:
                            for r in range(R):
                                sp.wait_ge(s_gmm, done + (i - 1) * R + r + 1)
                                load(i * R + r, r)

                    @block.scalar
                    def _(act):
                        def step(i, first):
                            for r in range(R):
                                if not first:
                                    act.wait_ge(s_gmm, done + (i - 1) * R + r + 1)
                                act.sem_inc(s_gon, 1)
                                src = H[:, ds(i * R + r, 1), :].squeeze(1)
                                nc.scalar.activation(hw[:, r, :], src, ACT.Copy,
                                                     scale=1.0 if scale is None else scale[:, ds(i * R + r, 1)]).then_inc(s_gw, 1)
                        step(0, True)
                        with act.Fori(1, NT // R) as i:
                            step(i, False)

                    @block.tensor
                    def _(pe):
                        def step(i, first, final):
                            for r in range(R):
                                pe.wait_ge(s_gw, done + i * R + r + 1)
                                pe.wait_ge(s_gld[r], loaded + i * 16 + 16)
                                for c, (a, b) in enumerate(CUTS):
                                    last = nc.tensor.matmul(num[:, c, 0:b - a], hw[:, r, :],
                                                            ab[:, r, :, :].rearrange("p q d -> p (q d)")[:, a:b],
                                                            start=first and r == 0, stop=final and r == R - 1,
                                                            skip_group_check=True)
                                last.then_inc(s_gmm, 1)
                        step(0, True, False)
                        with pe.Fori(1, NT // R - 1) as i:
                            step(i, False, False)
                        step(NT // R - 1, False, True)
                evacuate(tag, num, AGT)

        with ExitStack() as lay:
            AGT = lay.enter_context(nc.sbuf_tensor("AGT", [P, NP], F32))
            dinv = lay.enter_context(nc.sbuf_tensor("dinv", [P, 3, NT], F32))
            bbc = lay.enter_context(nc.sbuf_tensor("bbc", [P, D], F32))
            with ExitStack() as ctx:
                s_ch = sem("d_chain")
                s_a = sem("d_root")
                s_l = sem("d_bias")
                block = ctx.enter_context(nc.Block())

                @block.vector
                def _(dve):
                    link = Chain(dve, s_ch)
                    nc.vector.tensor_tensor(brow["bs"][:], brow["bs"][:], brow["bn"][:], ALU.add)
                    link(nc.vector.tensor_scalar(dinv[:, 2, :], DEG[:], 1.0, None, ALU.add))
                    link(nc.vector.reciprocal(dinv[:, 1, :], dinv[:, 2, :]))
                    dve.wait_ge(s_a, 1)
                    nc.vector.reciprocal(dinv[:, 0, :], dinv[:, 2, :])

                @block.scalar
                def _(act):
                    act.wait_ge(s_ch, 2)
                    nc.scalar.activation(dinv[:, 2, :], dinv[:, 2, :], ACT.Sqrt).then_inc(s_a, 1)

                @block.sync
                def _(sp):
                    sp.dma_start(bbc[:], bb2.partition_broadcast(P)).then_inc(s_l, 16)
                    sp.wait_ge(s_l, 16)

            gather_product("2", 0, dinv[:, 0, :], AGT)
            with ExitStack() as ctx:
                GT = 5
                NG = NT // GT
                assert NT % GT == 0
                Z = ctx.enter_context(nc.sbuf_tensor("Z", [P, NT, D], F32))
                Y = ctx.enter_context(nc.sbuf_tensor("Y", [P, 4, D], F32))
                Q = ctx.enter_context(nc.sbuf_tensor("Q", [P, NT, D], F32))
                V = ctx.enter_context(nc.sbuf_tensor("V", [P, NT, D], F32))
                pa = ctx.enter_context(nc.psum_tensor("pa2", [P, 4, BANK], F32))
                pb = ctx.enter_context(nc.psum_tensor("pb2", [P, 4, BANK], F32))
                s_p = sem("c_products")
                s_y = sem("c_self")
                s_z = sem("c_sum")
                s_e = sem("c_exp")
                s_zm = sem("c_clamped")
                s_q = sem("c_q")
                s_zq = sem("c_z_times_q")
                s_m = sem("c_mish")
                s_ch = sem("c_chain")
                block = ctx.enter_context(nc.Block())

                def of(buf, g):
                    return buf[:, g * GT:(g + 1) * GT, :]


                @block.tensor
                def _(pe):
                    for t in range(NT):
                        if t >= 4:
                            pe.wait_ge(s_z, t - 3)
                        nc.tensor.matmul(pb[:, t % 4, 0:D], HT[:, t * P:(t + 1) * P], wl["W2"][:], start=True, stop=True)
                        nc.tensor.matmul(pa[:, t % 4, 0:D], AGT[:, t * P:(t + 1) * P], wl["W2"][:], start=True,
                                         stop=True).then_inc(s_p, 1)

                @block.scalar
                def _(act):
                    for g in range(NG + 1):
                        if g < NG:
                            for t in range(g * GT, (g + 1) * GT):
                                act.wait_ge(s_p, t + 1)
                                if t >= 4:
                                    act.wait_ge(s_z, t - 3)
                                nc.scalar.activation(Y[:, t % 4, :], pb[:, t % 4, 0:D], ACT.Copy,
                                                     scale=dinv[:, 1, t:t + 1]).then_inc(s_y, 1)
                        if g >= 1:
                            act.wait_ge(s_zm, g)
                            nc.scalar.activation(of(Q, g - 1), of(Q, g - 1), ACT.Exp).then_inc(s_e, 1)

                @block.vector
                def _(dve):
                    link = Chain(dve, s_ch)

                    def value(g):
                        for t in range(g * GT, (g + 1) * GT):
                            dve.wait_ge(s_y, t + 1)
                            nc.vector.scalar_tensor_tensor(Z[:, t, :], pa[:, t % 4, 0:D], dinv[:, 0, t:t + 1], Y[:, t % 4, :],
                                                           ALU.mult, ALU.add).then_inc(s_z, 1)
                        dve.wait_ge(s_z, (g + 1) * GT)
                        link(nc.vector.tensor_tensor(of(Z, g), of(Z, g), bbc[:].unsqueeze(1).to_broadcast([P, GT, D]), ALU.add))
                        nc.vector.tensor_scalar(of(Q, g), of(Z, g), 20.0, None, ALU.min).then_inc(s_zm, 1)

                    def ratio(g):
                        dve.wait_ge(s_e, g + 1)
                        nc.vector.scalar_tensor_tensor(of(Q, g), of(Q, g), 2.0, of(Q, g), ALU.add, ALU.mult).then_inc(s_q, 1)
                        dve.wait_ge(s_q, g + 1)
                        link(nc.vector.tensor_scalar(of(V, g), of(Q, g), 2.0, None, ALU.add))
                        link(nc.vector.reciprocal(of(V, g), of(V, g)))

                    def mish(g):
                        dve.wait_ge(s_zq, g + 1)
                        nc.vector.tensor_tensor(of(Z, g), of(Z, g), of(V, g), ALU.mult).then_inc(s_m, 1)

                    for g in range(NG + 2):
                        if g < NG:
                            value(g)
                        if 1 <= g <= NG:
                            ratio(g - 1)
                        if g >= 2:
                            mish(g - 2)

                @block.gpsimd
                def _(pool):
                    for g in range(NG + 1):
                        if g < NG:
                            pool.wait_ge(s_q, g + 1)
                            nc.gpsimd.tensor_tensor(of(Z, g), of(Z, g), of(Q, g), ALU.mult).then_inc(s_zq, 1)
                        if g >= 1:
                            pool.wait_ge(s_m, g)
                            nc.gpsimd.tensor_tensor(of(X, g - 1), of(X, g - 1), of(Z, g - 1), ALU.add)

            layernorm(3)
            gather_product("3", 1, None, AGT)
            with ExitStack() as ctx:
                Y = ctx.enter_context(nc.sbuf_tensor("Y3", [P, 2, D], F32))
                Z = ctx.enter_context(nc.sbuf_tensor("Z3", [P, 2, D], F32))
                rdeg = ctx.enter_context(nc.sbuf_tensor("rdeg", [P, NT], F32))
                pa = ctx.enter_context(nc.psum_tensor("pa3", [P, 2, BANK], F32))
                pb = ctx.enter_context(nc.psum_tensor("pb3", [P, 2, BANK], F32))
                s_ch = sem("f_chain")
                s_r = sem("f_degree")
                s_p = sem("f_products")
                s_y = sem("f_neighbours")
                s_z = sem("f_sum")
                s_x = sem("f_x")
                s_out = sem("f_out")
                block = ctx.enter_context(nc.Block())

                @block.tensor
                def _(pe):
                    for t in range(NT):
                        if t >= 2:
                            pe.wait_ge(s_z, t - 1)
                        nc.tensor.matmul(pb[:, t % 2, 0:D], AGT[:, t * P:(t + 1) * P], wl["WnT"][:], start=True, stop=True)
                        nc.tensor.matmul(pa[:, t % 2, 0:D], HT[:, t * P:(t + 1) * P], wl["WsT"][:], start=True, stop=False)
                        nc.tensor.matmul(pa[:, t % 2, 0:D], ones[0:1, :], brow["bs"][:], start=False, stop=True).then_inc(s_p, 1)

                @block.scalar
                def _(act):
                    act.wait_ge(s_r, 1)
                    for t in range(NT):
                        act.wait_ge(s_p, t + 1)
                        if t >= 2:
                            act.wait_ge(s_z, t - 1)
                        nc.scalar.activation(Y[:, t % 2, :], pb[:, t % 2, 0:D], ACT.Copy, scale=rdeg[:, t:t + 1]).then_inc(s_y, 1)

                @block.vector
                def _(dve):
                    link = Chain(dve, s_ch)
                    link(nc.vector.tensor_scalar(rdeg[:], DEG[:], 1.0, None, ALU.max))
                    nc.vector.reciprocal(rdeg[:], rdeg[:]).then_inc(s_r, 1)
                    for t in range(NT):
                        dve.wait_ge(s_y, t + 1)
                        nc.vector.tensor_tensor(Z[:, t % 2, :], pa[:, t % 2, 0:D], Y[:, t % 2, :], ALU.add).then_inc(s_z, 1)
                        dve.wait_ge(s_z, t + 1)
                        nc.vector.scalar_tensor_tensor(X[:, t, :], Z[:, t % 2, :], 0.0, X[:, t, :], ALU.max,
                                                       ALU.add).then_inc(s_x, 1)

                @block.sync
                def _(sp):
                    for a in range(0, NT - 1, 6):
                        b = min(a + 6, NT - 1)
                        sp.wait_ge(s_x, b)
                        sp.dma_start(out[a * P:b * P, :].rearrange("(t p) d -> p t d", p=P), X[:, a:b, :]).then_inc(s_out, 16)
                    sp.wait_ge(s_x, NT)
                    sp.dma_start(out[(NT - 1) * P:N, :], X[0:NR, NT - 1, :]).then_inc(s_out, 16)
                    sp.wait_ge(s_out, 16 * 5)


_INS = ["x", "src", "dst", "edge_attr_64", "edge_type_100", "L0_gnn_msg_w1", "L0_gnn_msg_b1", "L0_gnn_msg_w2",
        "L0_gnn_msg_b2", "L0_gnn_upd_w1", "L0_gnn_upd_b1", "L0_gnn_upd_w2", "L0_gnn_upd_b2", "L1_gnn_W", "L1_gnn_attn",
        "L1_gnn_rel_emb", "L2_gnn_W", "L2_gnn_b", "L3_gnn_W_self", "L3_gnn_b_self", "L3_gnn_W_neigh", "L3_gnn_b_neigh"]


def kernel(**inputs):
    import numpy as _np
    import concourse.bacc as _bacc
    from concourse import mybir as _mybir
    from concourse.bass_utils import run_bass_kernel_spmd as _run

    nc = _bacc.Bacc("TRN2", target_bir_lowering=False, num_devices=1)
    arrays, args = {}, []
    for name in _INS:
        a = _np.ascontiguousarray(inputs[name])
        arrays[f"in_{name}_dram"] = a
        args.append(nc.dram_tensor(f"in_{name}_dram", a.shape, _mybir.dt.from_np(a.dtype), kind="ExternalInput").ap())
    args.append(nc.dram_tensor("out_0_dram", (N, D), _mybir.dt.float32, kind="ExternalOutput").ap())
    build(nc, *args)
    r = _run(nc, [arrays], core_ids=[0])
    return r.results[0]["out_0_dram"]
```
